# Optimizing a Trainium2 kernel written in Bass

```python
import numpy as np
import jax
import jax.numpy as jnp

def _softmax(x, axis=-1):
    return jax.nn.softmax(x, axis=axis)

def _gelu(x):
    return jax.nn.gelu(x, approximate=True)

def _silu(x):
    return jax.nn.silu(x)

def _sigmoid(x):
    return jax.nn.sigmoid(x)

def _layernorm(x, axis=-1, eps=1e-05):
    m = jnp.mean(x, axis=axis, keepdims=True)
    v = jnp.var(x, axis=axis, keepdims=True)
    return (x - m) / jnp.sqrt(v + eps)

def _scatter_add(tgt, idx, src, axis=0):
    return tgt.at[idx].add(src)

def _segment_sum(src, seg, n):
    return jax.ops.segment_sum(src, seg, n)
kernel_name = 'mk_vit_tower_d1_tok_img1024_r4_b8dba6'

def setup_inputs(seed: int=0):
    np.random.seed(seed)
    _w = jnp.asarray

    def _rec_inputs():
        import jax
        import jax.numpy as jnp
        _rk = jax.random.key(seed)
        x = -0.00016672 + 0.999947 * jax.random.normal(jax.random.fold_in(_rk, 1), (32, 3, 112, 112), jnp.float32)
        return x
    x = _rec_inputs()

    def _L0_tok_setup():
        import jax, jax.numpy as jnp
        import numpy as np
        PATCH = 16
        D_MODEL = 256

        def patchify(imgs, p):
            n, c, H, W = imgs.shape
            h, w = (H // p, W // p)
            x = imgs.reshape(n, c, h, p, w, p)
            x = jnp.einsum('nchpwq->nhwpqc', x)
            return x.reshape(n, h * w, p * p * c)
        key = jax.random.key(seed)
        k1, k2, k3 = jax.random.split(key, 3)
        val = jax.random.normal(k1, (64, 3, 96, 96), dtype=jnp.float32)
        in_dim = PATCH * PATCH * 3
        bound = 1.0 / np.sqrt(in_dim)
        W = jax.random.uniform(k2, (D_MODEL, in_dim), dtype=jnp.float32, minval=-bound, maxval=bound)
        b = jax.random.uniform(k3, (D_MODEL,), dtype=jnp.float32, minval=-bound, maxval=bound)
        return {'val': val, 'W': W, 'b': b}
    _L0_tok_all = _L0_tok_setup()
    _L0_tok_in = {k: v for k, v in _L0_tok_all.items() if k in ('W', 'b')}
    del _L0_tok_all

    def _L0_attn_setup():
        import jax, jax.numpy as jnp
        import numpy as np
        D_MODEL = 256
        D_HEAD = 64
        N_HEADS = 16
        STATE = 64
        D_INNER = D_HEAD * N_HEADS
        B, T = (4, 512)
        LN_EPS = 1e-05

        def _linear_params(key, fan_out, fan_in):
            k1, k2 = jax.random.split(key)
            s = 1.0 / np.sqrt(fan_in)
            W = jax.random.uniform(k1, (fan_out, fan_in), jnp.float32, -s, s)
            b = jax.random.uniform(k2, (fan_out,), jnp.float32, -s, s)
            return (W, b)

        def _layer_norm(x, gamma, beta):
            mu = jnp.mean(x, axis=-1, keepdims=True)
            var = jnp.mean(jnp.square(x - mu), axis=-1, keepdims=True)
            return (x - mu) * jax.lax.rsqrt(var + LN_EPS) * gamma + beta
        key = jax.random.key(seed)
        ks = jax.random.split(key, 8)
        WQ, bQ = _linear_params(ks[0], D_INNER, D_MODEL)
        WK, bK = _linear_params(ks[1], D_INNER, D_MODEL)
        WV, bV = _linear_params(ks[2], D_INNER, D_MODEL)
        WO, bO = _linear_params(ks[3], D_MODEL, D_INNER)
        Wg, bg = _linear_params(ks[4], D_INNER, D_MODEL)
        alpha_logit = jax.random.normal(ks[5], (N_HEADS, STATE), jnp.float32) * 0.1
        ln_gamma = jnp.ones((D_MODEL,), jnp.float32)
        ln_beta = jnp.zeros((D_MODEL,), jnp.float32)
        x = jax.random.normal(ks[6], (B, T, D_MODEL), jnp.float32)
        return {'x': x, 'WQ': WQ, 'bQ': bQ, 'WK': WK, 'bK': bK, 'WV': WV, 'bV': bV, 'WO': WO, 'bO': bO, 'Wg': Wg, 'bg': bg, 'alpha_logit': alpha_logit, 'ln_gamma': ln_gamma, 'ln_beta': ln_beta}
    _L0_attn_all = _L0_attn_setup()
    _L0_attn_in = {k: v for k, v in _L0_attn_all.items() if k in ('WQ', 'bQ', 'WK', 'bK', 'WV', 'bV', 'WO', 'bO', 'Wg', 'bg', 'alpha_logit', 'ln_gamma', 'ln_beta')}
    del _L0_attn_all

    def _L0_ffn_setup():
        import jax, jax.numpy as jnp
        import numpy as np
        E = 32
        H = 256
        I = 128
        G = 8
        TKG = 4
        TOPK = 8
        NSH = 2
        SCALE = 2.5
        key = jax.random.key(seed)
        ks = jax.random.split(key, 10)
        s = 0.02
        return {'hidden_states': jax.random.normal(ks[0], (2, 256, H), jnp.float32), 'gate_w': jax.random.normal(ks[1], (E, H), jnp.float32) * s, 'gate_bias': jax.random.normal(ks[2], (E,), jnp.float32) * s, 'w_gate': jax.random.normal(ks[3], (E, I, H), jnp.float32) * s, 'w_up': jax.random.normal(ks[4], (E, I, H), jnp.float32) * s, 'w_down': jax.random.normal(ks[5], (E, H, I), jnp.float32) * s, 'sh_gate': jax.random.normal(ks[6], (I * NSH, H), jnp.float32) * s, 'sh_up': jax.random.normal(ks[7], (I * NSH, H), jnp.float32) * s, 'sh_down': jax.random.normal(ks[8], (H, I * NSH), jnp.float32) * s}
    _L0_ffn_all = _L0_ffn_setup()
    _L0_ffn_in = {k: v for k, v in _L0_ffn_all.items() if k in ('gate_w', 'gate_bias', 'w_gate', 'w_up', 'w_down', 'sh_gate', 'sh_up', 'sh_down')}
    del _L0_ffn_all
    return {'x': x, 'L0_tok_W': _L0_tok_in['W'], 'L0_tok_b': _L0_tok_in['b'], 'L0_attn_WQ': _L0_attn_in['WQ'], 'L0_attn_bQ': _L0_attn_in['bQ'], 'L0_attn_WK': _L0_attn_in['WK'], 'L0_attn_bK': _L0_attn_in['bK'], 'L0_attn_WV': _L0_attn_in['WV'], 'L0_attn_bV': _L0_attn_in['bV'], 'L0_attn_WO': _L0_attn_in['WO'], 'L0_attn_bO': _L0_attn_in['bO'], 'L0_attn_Wg': _L0_attn_in['Wg'], 'L0_attn_bg': _L0_attn_in['bg'], 'L0_attn_alpha_logit': _L0_attn_in['alpha_logit'], 'L0_attn_ln_gamma': _L0_attn_in['ln_gamma'], 'L0_attn_ln_beta': _L0_attn_in['ln_beta'], 'L0_ffn_gate_w': _L0_ffn_in['gate_w'], 'L0_ffn_gate_bias': _L0_ffn_in['gate_bias'], 'L0_ffn_w_gate': _L0_ffn_in['w_gate'], 'L0_ffn_w_up': _L0_ffn_in['w_up'], 'L0_ffn_w_down': _L0_ffn_in['w_down'], 'L0_ffn_sh_gate': _L0_ffn_in['sh_gate'], 'L0_ffn_sh_up': _L0_ffn_in['sh_up'], 'L0_ffn_sh_down': _L0_ffn_in['sh_down']}

def reference(x, L0_tok_W, L0_tok_b, L0_attn_WQ, L0_attn_bQ, L0_attn_WK, L0_attn_bK, L0_attn_WV, L0_attn_bV, L0_attn_WO, L0_attn_bO, L0_attn_Wg, L0_attn_bg, L0_attn_alpha_logit, L0_attn_ln_gamma, L0_attn_ln_beta, L0_ffn_gate_w, L0_ffn_gate_bias, L0_ffn_w_gate, L0_ffn_w_up, L0_ffn_w_down, L0_ffn_sh_gate, L0_ffn_sh_up, L0_ffn_sh_down):
    import jax
    import jax.numpy as jnp

    def _L0_tok_ref(val, W, b):
        import jax, jax.numpy as jnp
        import numpy as np
        PATCH = 16
        D_MODEL = 256

        def patchify(imgs, p):
            n, c, H, W = imgs.shape
            h, w = (H // p, W // p)
            x = imgs.reshape(n, c, h, p, w, p)
            x = jnp.einsum('nchpwq->nhwpqc', x)
            return x.reshape(n, h * w, p * p * c)
        patches = patchify(val, PATCH)
        return jnp.einsum('nld,md->nlm', patches, W) + b

    def _L0_attn_ref(x, WQ, bQ, WK, bK, WV, bV, WO, bO, Wg, bg, alpha_logit, ln_gamma, ln_beta):
        import jax, jax.numpy as jnp
        import numpy as np
        D_MODEL = 256
        D_HEAD = 64
        N_HEADS = 16
        STATE = 64
        D_INNER = D_HEAD * N_HEADS
        B, T = (4, 512)
        LN_EPS = 1e-05

        def _linear_params(key, fan_out, fan_in):
            k1, k2 = jax.random.split(key)
            s = 1.0 / np.sqrt(fan_in)
            W = jax.random.uniform(k1, (fan_out, fan_in), jnp.float32, -s, s)
            b = jax.random.uniform(k2, (fan_out,), jnp.float32, -s, s)
            return (W, b)

        def _layer_norm(x, gamma, beta):
            mu = jnp.mean(x, axis=-1, keepdims=True)
            var = jnp.mean(jnp.square(x - mu), axis=-1, keepdims=True)
            return (x - mu) * jax.lax.rsqrt(var + LN_EPS) * gamma + beta
        batch, seq_len, _ = x.shape
        residual = x
        xn = _layer_norm(x, ln_gamma, ln_beta)
        Q = (xn @ WQ.T + bQ).reshape(batch, seq_len, N_HEADS, D_HEAD)
        K = (xn @ WK.T + bK).reshape(batch, seq_len, N_HEADS, D_HEAD)
        V = (xn @ WV.T + bV).reshape(batch, seq_len, N_HEADS, D_HEAD)
        gate = jax.nn.silu(xn @ Wg.T + bg).reshape(batch, seq_len, N_HEADS, D_HEAD)
        alpha = jax.nn.sigmoid(alpha_logit)
        Qs = Q[..., :STATE]
        Ks = K[..., :STATE]

        def step(h, qkv):
            q, k, v = qkv
            h = alpha[None, :, :, None] * h + k[:, :, :, None] * v[:, :, None, :]
            o = jnp.einsum('bhi,bhij->bhj', q, h)
            return (h, o)
        h0 = jnp.zeros((batch, N_HEADS, STATE, D_HEAD), x.dtype)
        qkv_t = (jnp.moveaxis(Qs, 1, 0), jnp.moveaxis(Ks, 1, 0), jnp.moveaxis(V, 1, 0))
        _, o = jax.lax.scan(step, h0, qkv_t)
        o = jnp.moveaxis(o, 0, 1)
        o = o * gate
        y = o.reshape(batch, seq_len, D_INNER) @ WO.T + bO
        return residual + y

    def _L0_ffn_ref(hidden_states, gate_w, gate_bias, w_gate, w_up, w_down, sh_gate, sh_up, sh_down):
        import jax, jax.numpy as jnp
        import numpy as np
        E = 32
        H = 256
        I = 128
        G = 8
        TKG = 4
        TOPK = 8
        NSH = 2
        SCALE = 2.5
        B, S, Hd = hidden_states.shape
        h = hidden_states.reshape(-1, Hd)
        logits = h.astype(jnp.float32) @ gate_w.T
        scores = jax.nn.sigmoid(logits)
        sc = scores + gate_bias
        grp = sc.reshape(-1, G, E // G)
        group_scores = jax.lax.top_k(grp, 2)[0].sum(-1)
        gidx = jax.lax.top_k(group_scores, TKG)[1]
        gmask = jnp.sum(jax.nn.one_hot(gidx, G, dtype=sc.dtype), axis=1)
        smask = jnp.repeat(gmask, E // G, axis=1)
        masked = jnp.where(smask > 0, sc, jnp.zeros_like(sc))
        tki = jax.lax.top_k(masked, TOPK)[1]
        tkw = jnp.take_along_axis(scores, tki, axis=1)
        tkw = tkw / (tkw.sum(-1, keepdims=True) + 1e-20)
        tkw = tkw * SCALE
        combine = (jax.nn.one_hot(tki, E, dtype=tkw.dtype) * tkw[..., None]).sum(1)
        g = jax.nn.silu(jnp.einsum('th,eih->tei', h, w_gate))
        u = jnp.einsum('th,eih->tei', h, w_up)
        routed = jnp.einsum('tei,ehi->th', g * u * combine[:, :, None], w_down)
        sg = jax.nn.silu(h @ sh_gate.T)
        shared = sg * (h @ sh_up.T) @ sh_down.T
        return (routed + shared).reshape(B, S, Hd)
    h = _L0_tok_ref(x, L0_tok_W, L0_tok_b)
    h = h + _L0_attn_ref(_layernorm(h, axis=-1), L0_attn_WQ, L0_attn_bQ, L0_attn_WK, L0_attn_bK, L0_attn_WV, L0_attn_bV, L0_attn_WO, L0_attn_bO, L0_attn_Wg, L0_attn_bg, L0_attn_alpha_logit, L0_attn_ln_gamma, L0_attn_ln_beta)
    h = h + _L0_ffn_ref(_layernorm(h, axis=-1), L0_ffn_gate_w, L0_ffn_gate_bias, L0_ffn_w_gate, L0_ffn_w_up, L0_ffn_w_down, L0_ffn_sh_gate, L0_ffn_sh_up, L0_ffn_sh_down)
    return h

_drawn_inputs = setup_inputs


def setup_inputs(seed=0):
    import zlib

    import numpy as np

    out = dict(_drawn_inputs(seed))
    spreads = {'L0_attn_ln_gamma': (1.0, 0.2), 'L0_attn_ln_beta': (0.0, 0.1)}
    factors = {'L0_attn_bQ': 3.953,
     'L0_attn_bK': 3.855,
     'L0_attn_bV': 3.819,
     'L0_attn_bO': 5.008,
     'L0_attn_bg': 3.92,
     'L0_attn_alpha_logit': 6.259,
     'L0_ffn_gate_w': 8.0,
     'L0_ffn_gate_bias': 8.0,
     'L0_ffn_w_gate': 8.0,
     'L0_ffn_w_up': 8.0,
     'L0_ffn_w_down': 8.0,
     'L0_ffn_sh_gate': 5.502,
     'L0_ffn_sh_up': 5.461,
     'L0_ffn_sh_down': 5.469}
    for name, (base, spread) in spreads.items():
        noise = np.random.default_rng([zlib.crc32(name.encode()), seed]).standard_normal(out[name].shape)
        drawn = base * np.exp(spread * noise) if base else spread * noise
        out[name] = jnp.asarray(drawn.astype(out[name].dtype))
    for name, factor in factors.items():
        out[name] = (out[name] * factor).astype(out[name].dtype)
    return out
```

```python
from contextlib import ExitStack

import concourse.bass as bass
from concourse import mybir

ALU = mybir.AluOpType
ACT = mybir.ActivationFunctionType
AX = mybir.AxisListType
F32 = mybir.dt.float32
F32R = mybir.dt.float32r

P = 128
IMAGES, SEQ, D = 32, 49, 256
PATCH_D = 768
HEADS, D_HEAD = 16, 64
D_INNER = HEADS * D_HEAD
EXPERTS, SHARED, TOP_GROUPS, ROUTE_SCALE = 32, 2, 4, 2.5
ROUTE_GROUPS = 8
EPS = 1e-5

TOKENS = IMAGES * SEQ
GT = 2 * SEQ
GROUPS = 4
BT = GROUPS * GT
BLOCKS = TOKENS // BT
KD = D // P
KP = PATCH_D // P
CH = D_INNER // P
STARTS = (0, 9, 17, 25, 33, 41)
LENS = (9, 8, 8, 8, 8, 8)
HALF = 4
MIN_DECAY = 1e-8
QOFF = [2 * s for s in STARTS]
ENDS = [2 * (s + n) for s, n in zip(STARTS, LENS)]
KOFF = [sum(ENDS[:j]) for j in range(len(ENDS))]
KCOLS = sum(ENDS)
POWERS = SEQ + HALF
STEPS = 2 * BLOCKS
PAIRS = (EXPERTS + SHARED) // 2
MATS = 4
PAIR_COLS = 2 * 3 * D
CHUNK_COLS = MATS * KD * P

PB, PLOGIT, PTOKB, PBO, PGAMMA, PBETA, PCOLS = 0, 32, 40, 42, 44, 46, 48


def build(nc, patches, w_tok, w_qkvg, w_o, w_ffn, params, w_route, b_route, ident_d, causal_d,
          before_d, comb_rows, out):
    with ExitStack() as ctx:
        def sb(name, cols, dt=F32, rows=P):
            return ctx.enter_context(nc.sbuf_tensor(name, [rows, cols], dt))

        def sem(name):
            return ctx.enter_context(nc.semaphore(name))

        bank = [ctx.enter_context(nc.psum_tensor(f"bank{i}", [P, 512], F32)) for i in range(8)]

        xn = [sb("xn_hi", KD * TOKENS, F32R), sb("xn_lo", KD * TOKENS, F32R)]
        mov = sb("moving_parts", 2 * CH * BT, F32R)
        wbuf = [sb("weights_even", 2 * PAIR_COLS, F32R), sb("weights_odd", 2 * PAIR_COLS, F32R)]
        w_edge = sb("weights_tok_out", 2 * CH * D, F32R)
        og = sb("gated_heads", CH * TOKENS)
        token_store = sb("token_store", BLOCKS * GROUPS * D)
        raw = sb("weights_raw", 2 * PAIR_COLS)
        par = sb("channel_params", PCOLS)
        ident = sb("identity", P)
        causal = sb("causal", GT)
        before = sb("before", ROUTE_GROUPS * ROUTE_GROUPS)
        route_w = sb("route_w", KD * EXPERTS)
        route_b = sb("route_b", EXPERTS)
        decay = sb("decay", 2 * CH)
        tab_q = sb("powers_q", CH * GT)
        tab_k = sb("powers_k", CH * KCOLS)
        work = sb("work", 2 * BT + GROUPS * KCOLS + 2 * BT + BT + GROUPS * P + BT + 264)
        small = sb("small", 96)
        rt = sb("router", 1024 + 256)
        ones = sb("ones", BT)

        def cut(t, at, n):
            return t[:, at:at + n], at + n

        at = 0
        q_dec, at = cut(work, at, 2 * BT)
        k_dec, at = cut(work, at, GROUPS * KCOLS)
        probs, at = cut(work, at, 2 * BT)
        v_ch, at = cut(work, at, BT)
        v_tok, at = cut(work, at, GROUPS * P)
        gate, at = cut(work, at, BT)
        q_dec = q_dec.rearrange("p (h t) -> p h t", h=2)
        v_tok = v_tok.rearrange("p (g c) -> p g c", g=GROUPS)
        k_dec = [k_dec[:, GROUPS * KOFF[j]:GROUPS * (KOFF[j] + ENDS[j])].rearrange("p (g s) -> p g s", g=GROUPS)
                 for j in range(len(ENDS))]
        at = 0
        y_ch, at = cut(work, at, KD * BT)
        h2_tok, at = cut(work, at, GROUPS * D)
        x3_tok, at = cut(work, at, GROUPS * D)
        x3_ch, at = cut(work, at, KD * BT)
        cmp1, at = cut(work, at, GROUPS * ROUTE_GROUPS ** 2)
        cmp2, at = cut(work, at, GROUPS * ROUTE_GROUPS ** 2)
        cmp1, cmp2 = cmp1[0:GT, :], cmp2[0:GT, :]
        comb_sb = work[0:EXPERTS, at:at + BT]
        at = CH * TOKENS // 2
        patch_raw, at = cut(og, at, KP * BT)
        h_ch, at = cut(og, at, KD * BT)
        x2_tok, at = cut(og, at, GROUPS * D)
        z_tok, at = cut(og, at, GROUPS * D)
        xn_ch, at = cut(og, at, KD * BT)
        tok_raw = og[:, 0:KP * D]
        pw = og[:, 2048:2048 + CH * POWERS].rearrange("p (c e) -> p c e", c=CH)
        rw = og[:, 3072:3072 + CH * POWERS].rearrange("p (c e) -> p c e", c=CH)
        at = 0
        silu_g, weighted, hidden, comb = [], [], [], []
        for e in range(2):
            t, at = cut(og, at, BT)
            silu_g.append(t)
            t, at = cut(og, at, BT)
            weighted.append(t)
            t, at = cut(og, at, BT)
            hidden.append(t)
        for k in range(2):
            t, at = cut(og, at, 2 * BT)
            comb.append(t)

        def og_at(c, b):
            return og[:, bass.ds(c * TOKENS + b * BT, BT)]

        def xn_at(part, k, b):
            return xn[part][:, k * TOKENS + b * BT:k * TOKENS + (b + 1) * BT]

        def res(b):
            return token_store[0:GT, b * GROUPS * D:(b + 1) * GROUPS * D]

        def acc(b, m):
            return token_store[:, b * GROUPS * D + m * BT:b * GROUPS * D + (m + 1) * BT]

        def mov_at(part, c):
            return mov[:, (part * CH + c) * BT:(part * CH + c + 1) * BT]

        def rview(at, n):
            return rt[0:GT, at:at + n]

        GE, GG = GROUPS * EXPERTS, GROUPS * ROUTE_GROUPS
        r_score, r_choice = rview(0, GE), rview(GE, GE)
        r_a, r_b, r_c = rview(2 * GE, GE), rview(3 * GE, GE), rview(4 * GE, GE)
        comb_tok = rview(5 * GE, GE)
        r_max, r_min = rview(6 * GE, 2 * GG), rview(6 * GE + 2 * GG, 2 * GG)
        r_gs, r_sel, r_t0, r_t1 = (rview(7 * GE + i * GG, GG) for i in range(4))
        r_top = rview(8 * GE, GG)
        r_sum = rview(8 * GE + GG, GROUPS)
        r_inv = rview(8 * GE + GG + GROUPS, GROUPS)

        stat = small[0:GT, 0:GROUPS * 6].rearrange("p (g n) -> p g n", g=GROUPS)
        mv = small[0:GT, 24:24 + GROUPS * 2].rearrange("p (g n) -> p g n", g=GROUPS)
        ve = small[0:GT, 32:32 + GROUPS]
        sd = small[0:GT, 36:36 + GROUPS]
        rstd = small[0:GT, 40:40 + GROUPS]
        r2 = small[0:GT, 44:44 + GROUPS]
        ve2 = small[0:GT, 48:48 + GROUPS]
        sd2 = small[0:GT, 52:52 + GROUPS]
        rstd_n = small[0:GT, 56:56 + GROUPS]
        bias_now = [small[:, 64:66], small[:, 66:68]]
        zsc = small[0:GT, 60:60 + GROUPS]

        s_params_in = sem("params_in")
        s_consts_in = sem("consts_in")
        s_patch_in = sem("patch_in")
        s_tokw_in = sem("tokw_in")
        s_chunk_in = sem("chunk_in")
        s_chunk_in1 = sem("chunk_in1")
        s_wo_in = sem("wo_in")
        s_pair_in = sem("pair_in")
        s_pair_in1 = sem("pair_in1")
        s_comb_in = sem("comb_in")
        s_comb_in1 = sem("comb_in1")
        s_ones_in = sem("ones_in")
        s_stored = sem("stored")
        s_out_done = sem("out_done")
        s_patch_hi = sem("patch_hi")
        s_patch_lo = sem("patch_lo")
        s_tokw_hi = sem("tokw_hi")
        s_tokw_lo = sem("tokw_lo")
        s_h_proj = sem("h_proj")
        s_h_copied = sem("h_copied")
        s_h_turned = sem("h_turned")
        s_stats = sem("stats")
        s_agg = sem("agg")
        s_veps = sem("veps")
        s_std = sem("std")
        s_rstd = sem("rstd")
        s_v2 = sem("v2")
        s_std2 = sem("std2")
        s_zscale = sem("zscale")
        s_x2_done = sem("x2_done")
        s_res_done = sem("res_done")
        s_z_done = sem("z_done")
        s_z_turned = sem("z_turned")
        s_xn_done = sem("xn_done")
        s_xn_split = sem("xn_split")
        s_decay_e = sem("decay_e")
        s_pw_step = sem("pw_step")
        s_tables = sem("tables")
        s_zeroed = sem("zeroed")
        s_chunk_split = sem("chunk_split")
        s_wo_split = sem("wo_split")
        s_k_proj = sem("k_proj")
        s_q_proj = sem("q_proj")
        s_v_proj = sem("v_proj")
        s_g_proj = sem("g_proj")
        s_k_scaled = sem("k_scaled")
        s_q_scaled = sem("q_scaled")
        s_scores = sem("scores")
        s_masked = sem("masked")
        s_bias_ready = sem("bias_ready")
        s_v_copied = sem("v_copied")
        s_v_turned = sem("v_turned")
        s_v_ready = sem("v_ready")
        s_gated = sem("gated")
        s_pv = sem("pv")
        s_og_done = sem("og_done")
        s_og_hi = sem("og_hi")
        s_og_lo = sem("og_lo")
        s_og_used = sem("og_used")
        s_y_copied = sem("y_copied")
        s_y_turned = sem("y_turned")
        s_h2_done = sem("h2_done")
        s_stats2 = sem("stats2")
        s_agg2 = sem("agg2")
        s_veps2 = sem("veps2")
        s_std3 = sem("std3")
        s_rstd2 = sem("rstd2")
        s_x3_done = sem("x3_done")
        s_h2_turned = sem("h2_turned")
        s_x3_turned = sem("x3_turned")
        s_acc_set = sem("acc_set")
        s_x3_copied = sem("x3_copied")
        s_x3_split = sem("x3_split")
        s_logits = sem("logits")
        s_exp_done = sem("exp_done")
        s_r_step = sem("r_step")
        s_comb_done = sem("comb_done")
        s_comb_turned = sem("comb_turned")
        s_comb_kept = sem("comb_kept")
        s_pair0_split = sem("pair0_split")
        s_silu_done = sem("silu_done")
        s_weighted_done = sem("weighted_done")
        s_hidden_done = sem("hidden_done")
        s_hid_hi = sem("hid_hi")
        s_hid_lo = sem("hid_lo")
        s_g_ready = sem("g_ready")
        s_u_ready = sem("u_ready")
        s_y_ready = sem("y_ready")
        s_added = sem("added")
        s_wsplit_hi = sem("wsplit_hi")
        s_wsplit_lo = sem("wsplit_lo")

        block = ctx.enter_context(nc.Block())

        def weight_parts(w, cols):
            return w[:, 0:cols], w[:, cols:2 * cols]

        tok_hi, tok_lo = weight_parts(w_edge, KP * D)
        wo_hi, wo_lo = weight_parts(w_edge, CH * D)

        @block.sync
        def _(sp):
            sp.dma_start(tok_raw, w_tok).then_inc(s_tokw_in, 16)
            for b in range(BLOCKS):
                if b >= 1:
                    sp.wait_ge(s_patch_hi, b)
                    sp.wait_ge(s_patch_lo, b)
                sp.dma_start(patch_raw, patches[:, b, :]).then_inc(s_patch_in, 16)
                if b == 0:
                    sp.dma_start(par[:, :], params).then_inc(s_params_in, 16)
                    sp.dma_start(ident[:, :], ident_d).then_inc(s_consts_in, 16)
                    sp.dma_start(causal[0:GT, :], causal_d).then_inc(s_consts_in, 16)
                    sp.dma_start(before[0:GT, :], before_d).then_inc(s_consts_in, 16)
                    sp.dma_start(route_w[:, :], w_route).then_inc(s_consts_in, 16)
                    sp.dma_start(route_b[0:GT, :], b_route.broadcast_to([GT, EXPERTS])).then_inc(s_consts_in, 16)
                    for c in range(2):
                        sp.dma_start(raw[:, c * CHUNK_COLS:(c + 1) * CHUNK_COLS],
                                     w_qkvg[c]).then_inc((s_chunk_in, s_chunk_in1)[c], 16)
                    sp.dma_start(raw[:, 2 * CHUNK_COLS:3 * CHUNK_COLS], w_o[0]).then_inc(s_wo_in, 16)
            with sp.Fori(0, CH // 2 - 1) as q:
                for w in range(2):
                    sp.wait_ge(s_chunk_split, 4 * q + 2 * (w + 1))
                    sp.dma_start(raw[:, w * CHUNK_COLS:(w + 1) * CHUNK_COLS],
                                 w_qkvg[bass.ds(2 * q + 2 + w, 1)].rearrange("a p n -> p (a n)")
                                 ).then_inc((s_chunk_in, s_chunk_in1)[w], 16)
            sp.wait_ge(s_wo_split, 2)
            sp.dma_start(raw[:, 2 * CHUNK_COLS:3 * CHUNK_COLS], w_o[1]).then_inc(s_wo_in, 16)
            sp.wait_ge(s_wo_split, 4)
            sp.wait_ge(s_chunk_split, 2 * CH)
            for p in range(2):
                sp.dma_start(raw[:, p * PAIR_COLS:(p + 1) * PAIR_COLS], w_ffn[p]).then_inc(
                    (s_pair_in, s_pair_in1)[p], 16)
            sp.wait_ge(s_zeroed, 2)
            for b in range(BLOCKS):
                sp.dma_start(comb_rows[EXPERTS:EXPERTS + SHARED, b * BT:(b + 1) * BT],
                             ones[0:SHARED, :]).then_inc(s_ones_in, 16)
            for b in range(BLOCKS):
                sp.wait_ge(s_comb_kept, b + 1)
                sp.dma_start(comb_rows[0:EXPERTS, b * BT:(b + 1) * BT], comb_sb).then_inc(s_stored, 16)
            sp.wait_ge(s_ones_in, 16 * BLOCKS)
            sp.wait_ge(s_stored, 16 * BLOCKS)

            def load_comb(pair, b):
                for e in range(2):
                    sp.dma_start(comb[b % 2][:, e * BT:(e + 1) * BT],
                                 comb_rows[bass.ds(2 * pair + e, 1), b * BT:(b + 1) * BT].broadcast_to([P, BT])
                                 ).then_inc((s_comb_in, s_comb_in1)[b % 2], 16)

            load_comb(0, 0)
            load_comb(0, 1)

            def pair_loads(p, w, load_next, more):
                if load_next:
                    if isinstance(p, int) and p == 0:
                        sp.wait_ge(s_pair0_split, 2)
                    else:
                        sp.wait_ge(s_wsplit_hi, 3 * p)
                        sp.wait_ge(s_wsplit_lo, 3 * p)
                    sp.dma_start(raw[:, w * PAIR_COLS:(w + 1) * PAIR_COLS],
                                 w_ffn[bass.ds(p + 2, 1)].rearrange("a p n -> p (a n)")).then_inc(
                        (s_pair_in, s_pair_in1)[w], 16)
                for b in range(BLOCKS):
                    if b < 2 or more:
                        sp.wait_ge(s_weighted_done, 2 * (BLOCKS * p + b + 1))
                        load_comb(p + (b + 2) // BLOCKS, (b + 2) % BLOCKS)

            pair_loads(0, 0, True, True)
            pair_loads(1, 1, True, True)
            with sp.Fori(1, PAIRS // 2 - 1) as q:
                pair_loads(2 * q, 0, True, True)
                pair_loads(2 * q + 1, 1, True, True)
            pair_loads(PAIRS - 3, 0, True, True)
            pair_loads(PAIRS - 2, 1, False, True)
            pair_loads(PAIRS - 1, 0, False, False)
            for b in range(BLOCKS):
                sp.wait_ge(s_added, BLOCKS * (PAIRS - 1) + b + 1)
                sp.dma_start(out[:, b, :], token_store[:, b * GROUPS * D:b * GROUPS * D + KD * BT]
                             ).then_inc(s_out_done, 16)
            sp.wait_ge(s_out_done, 16 * BLOCKS)

        @block.tensor
        def _(pe):
            def three_pass(dst, terms):
                for k, (wh, wl, xh, xl, first, last) in enumerate(terms):
                    pe.matmul(dst, wl, xh, start=first, stop=False)
                    pe.matmul(dst, wh, xh, start=False, stop=False)
                    mm = pe.matmul(dst, wh, xl, start=False, stop=last)
                return mm

            def patch_project(b):
                pe.wait_ge(s_patch_hi, b + 1)
                pe.wait_ge(s_patch_lo, b + 1)
                if b >= 1:
                    pe.wait_ge(s_h_copied, 2 * b)
                for m in range(KD):
                    mm = three_pass(bank[m][:, 0:BT], [
                        (tok_hi[:, k * D + m * P:k * D + (m + 1) * P], tok_lo[:, k * D + m * P:k * D + (m + 1) * P],
                         mov_at(0, k), mov_at(1, k), k == 0, k == KP - 1) for k in range(KP)])
                    mm.then_inc(s_h_proj, 1)

            def turn_tokens(src, done):
                for g in range(GROUPS):
                    for m in range(KD):
                        mm = pe.transpose(bank[2 + g // 2][0:GT, (g % 2) * D + m * P:(g % 2) * D + (m + 1) * P],
                                          src[:, m * BT + g * GT:m * BT + (g + 1) * GT], ident[:, :])
                mm.then_inc(done, 1)

            def turn_channels(src, first_bank, done):
                for m in range(KD):
                    for g in range(GROUPS):
                        mm = pe.transpose(bank[first_bank + m][:, g * GT:(g + 1) * GT],
                                          src[0:GT, g * D + m * P:g * D + (m + 1) * P], ident[0:GT, 0:GT])
                mm.then_inc(done, 1)

            pe.wait_ge(s_tokw_hi, 1)
            pe.wait_ge(s_tokw_lo, 1)
            patch_project(0)
            pe.wait_ge(s_consts_in, 16 * 5)
            for b in range(BLOCKS):
                pe.wait_ge(s_h_copied, 2 * (b + 1))
                if b >= 1:
                    pe.wait_ge(s_res_done, b)
                turn_tokens(h_ch, s_h_turned)
                if b < BLOCKS - 1:
                    patch_project(b + 1)
                pe.wait_ge(s_z_done, b + 1)
                if b >= 1:
                    pe.wait_ge(s_xn_done, b)
                turn_channels(z_tok, 4, s_z_turned)

            def project(c, b, it, w, first=False):
                pe.wait_ge(s_chunk_split, 2 * (c + 1))
                pe.wait_ge(s_xn_split, 2 * (b + 1))
                hi, lo = weight_parts(wbuf[w], CHUNK_COLS)
                ready = (s_k_proj, s_q_proj, s_v_proj, s_g_proj)
                for m, free in enumerate((s_k_scaled, s_q_scaled, s_v_copied, s_gated)):
                    if not first:
                        pe.wait_ge(free, it)
                    cols = [slice((m * KD + k) * P, (m * KD + k + 1) * P) for k in range(KD)]
                    three_pass(bank[m][:, 0:BT], [
                        (hi[:, cols[k]], lo[:, cols[k]], xn_at(0, k, b), xn_at(1, k, b), k == 0, k == KD - 1)
                        for k in range(KD)]).then_inc(ready[m], 1)

            def turn_values(it, first=False):
                pe.wait_ge(s_v_copied, it + 1)
                if not first:
                    pe.wait_ge(s_v_ready, it)
                for g in range(GROUPS):
                    mm = pe.transpose(bank[4][0:GT, g * P:(g + 1) * P], v_ch[:, g * GT:(g + 1) * GT], ident[:, :])
                mm.then_inc(s_v_turned, 1)

            def score(it):
                pe.wait_ge(s_k_scaled, it + 1)
                pe.wait_ge(s_q_scaled, it + 1)
                pe.wait_ge(s_masked, 2 * it + 2)
                for g in range(GROUPS):
                    dst = bank[6 + g // 2][:, (g % 2) * 2 * GT:(g % 2 + 1) * 2 * GT].rearrange(
                        "p (h t) -> p h t", h=2)
                    for j in range(len(ENDS)):
                        mm = pe.matmul(dst[0:ENDS[j], :, QOFF[j]:QOFF[j] + 2 * LENS[j]], k_dec[j][:, g, :],
                                       q_dec[:, :, g * GT + QOFF[j]:g * GT + QOFF[j] + 2 * LENS[j]],
                                       start=True, stop=True)
                    if g % 2:
                        mm.then_inc(s_scores, 1)

            def mix_values(it):
                pe.wait_ge(s_v_ready, it + 1)
                pe.wait_ge(s_og_done, it + 1)
                for g in range(GROUPS):
                    if g % 2 == 0:
                        pe.wait_ge(s_masked, 2 * it + g // 2 + 3)
                    for h in range(2):
                        mm = pe.matmul(bank[5][h * D_HEAD:(h + 1) * D_HEAD, g * GT:(g + 1) * GT],
                                       v_tok[0:GT, g, h * D_HEAD:(h + 1) * D_HEAD],
                                       probs[0:GT, (2 * g + h) * GT:(2 * g + h + 1) * GT], start=True, stop=True)
                mm.then_inc(s_pv, 1)

            def turn(q, last=False):
                for u in range(STEPS):
                    it = STEPS * q + u
                    score(it)
                    end = last and u == STEPS - 1
                    n = u + 1
                    if not end:
                        project(2 * q + n // BLOCKS, n % BLOCKS, it + 1, (n // BLOCKS) % 2)
                    mix_values(it)
                    if not end:
                        turn_values(it + 1)

            pe.wait_ge(s_h_copied, 2 * BLOCKS)
            pe.wait_ge(s_res_done, BLOCKS)
            project(0, 0, 0, 0, first=True)
            pe.wait_ge(s_xn_done, BLOCKS)
            turn_values(0, first=True)
            pe.wait_ge(s_zeroed, 2)
            with pe.Fori(0, CH // 2 - 1) as q:
                turn(q)
            turn(CH // 2 - 1, last=True)

            def out_project(b):
                if b == 0:
                    pe.wait_ge(s_wo_split, 4)
                    pe.wait_ge(s_k_scaled, STEPS * CH // 2)
                    pe.wait_ge(s_q_scaled, STEPS * CH // 2)
                else:
                    pe.wait_ge(s_y_copied, 2 * b)
                for k in range(CH):
                    pe.wait_ge(s_og_hi, CH * b + k + 1)
                    pe.wait_ge(s_og_lo, CH * b + k + 1)
                    for m in range(KD):
                        cols = slice(k * D + m * P, k * D + (m + 1) * P)
                        mm = three_pass(bank[m][:, 0:BT], [
                            (wo_hi[:, cols], wo_lo[:, cols], mov_at(0, k), mov_at(1, k), k == 0, k == CH - 1)])
                    mm.then_inc(s_og_used, 1)

            def turn_y(b):
                pe.wait_ge(s_y_copied, 2 * (b + 1))
                if b == 0:
                    pe.wait_ge(s_v_copied, STEPS * CH // 2)
                    pe.wait_ge(s_gated, STEPS * CH // 2)
                else:
                    pe.wait_ge(s_h2_done, 2 * b)
                turn_tokens(y_ch, s_y_turned)

            def turn_h2(b):
                pe.wait_ge(s_h2_done, 2 * (b + 1))
                if b == 0:
                    pe.wait_ge(s_v_ready, STEPS * CH // 2)
                    pe.wait_ge(s_og_done, STEPS * CH // 2 + 1)
                    pe.wait_ge(s_masked, STEPS * CH + 2)
                else:
                    pe.wait_ge(s_exp_done, b)
                    pe.wait_ge(s_comb_kept, b)
                turn_channels(h2_tok, 4, s_h2_turned)
                pe.wait_ge(s_x3_done, b + 1)
                if b >= 1:
                    pe.wait_ge(s_x3_copied, 2 * b)
                turn_channels(x3_tok, 6, s_x3_turned)

            def route(b):
                pe.wait_ge(s_x3_copied, 2 * (b + 1))
                pe.wait_ge(s_acc_set, 2 * (b + 1))
                for g in range(GROUPS):
                    for m in range(KD):
                        mm = pe.matmul(bank[4][0:GT, g * EXPERTS:(g + 1) * EXPERTS],
                                       x3_ch[:, m * BT + g * GT:m * BT + (g + 1) * GT],
                                       route_w[:, m * EXPERTS:(m + 1) * EXPERTS], start=m == 0, stop=m == KD - 1)
                mm.then_inc(s_logits, 1)

            def turn_comb(b):
                pe.wait_ge(s_comb_done, b + 1)
                for g in range(GROUPS):
                    mm = pe.transpose(bank[5][0:EXPERTS, g * GT:(g + 1) * GT],
                                      comb_tok[0:GT, g * EXPERTS:(g + 1) * EXPERTS], ident[0:GT, 0:GT])
                mm.then_inc(s_comb_turned, 1)

            out_project(0)
            turn_y(0)
            for b in range(BLOCKS):
                if b < BLOCKS - 1:
                    out_project(b + 1)
                if b >= 1:
                    turn_comb(b - 1)
                turn_h2(b)
                route(b)
                if b < BLOCKS - 1:
                    turn_y(b + 1)

            def expert_up(p, b, n, w, first=False):
                if first:
                    pe.wait_ge(s_pair0_split, 2)
                else:
                    pe.wait_ge(s_wsplit_hi, 3 * p)
                    pe.wait_ge(s_wsplit_lo, 3 * p)
                pe.wait_ge(s_x3_split, 2 * (b + 1))
                hi, lo = weight_parts(wbuf[w], PAIR_COLS)
                for e in range(2):
                    for gu, (ready, free) in enumerate(((s_g_ready, s_silu_done), (s_u_ready, s_hidden_done))):
                        if not first:
                            pe.wait_ge(free, 2 * n - 1 + e)
                        cols = [slice(e * 3 * D + k * D + gu * P, e * 3 * D + k * D + gu * P + P) for k in range(KD)]
                        three_pass(bank[2 * e + gu][:, 0:BT], [
                            (hi[:, cols[k]], lo[:, cols[k]], xn_at(0, k, b), xn_at(1, k, b), k == 0, k == KD - 1)
                            for k in range(KD)]).then_inc(ready, 1)

            def expert_down(b, n, w, first=False):
                hi, lo = weight_parts(wbuf[w], PAIR_COLS)
                if not first:
                    pe.wait_ge(s_added, n - 1)
                for e in range(2):
                    pe.wait_ge(s_hid_hi, 2 * n + e + 1)
                    pe.wait_ge(s_hid_lo, 2 * n + e + 1)
                    x_hi, x_lo = mov_at(b % 2, 2 * e), mov_at(b % 2, 2 * e + 1)
                    for m in range(KD):
                        cols = slice(e * 3 * D + KD * D + m * P, e * 3 * D + KD * D + (m + 1) * P)
                        mm = three_pass(bank[4 + 2 * (b % 2) + m][:, 0:BT],
                                        [(hi[:, cols], lo[:, cols], x_hi, x_lo, e == 0, e == 1)])
                mm.then_inc(s_y_ready, 1)

            def pair_steps(p, w, first=False, last=False):
                for b in range(BLOCKS):
                    n = BLOCKS * p + b
                    if b < BLOCKS - 1:
                        expert_up(p, b + 1, n + 1, w)
                    elif not last:
                        expert_up(p + 1, 0, n + 1, 1 - w)
                    expert_down(b, n, w, first=first and b == 0)

            expert_up(0, 0, 0, 0, first=True)
            turn_comb(BLOCKS - 1)
            pe.wait_ge(s_comb_kept, BLOCKS)
            pe.wait_ge(s_exp_done, BLOCKS)
            pair_steps(0, 0, first=True)
            pair_steps(1, 1)
            with pe.Fori(1, PAIRS // 2) as q:
                pair_steps(2 * q, 0)
                pair_steps(2 * q + 1, 1)
            pair_steps(PAIRS - 1, 0, last=True)

        @block.vector
        def _(dve):
            dve.memset(bank[6][:, :], 0.0).then_inc(s_masked, 1)
            dve.memset(bank[7][:, :], 0.0).then_inc(s_masked, 1)
            dve.memset(gate, 0.0).then_inc(s_og_done, 1)
            dve.memset(q_dec[:, :, :], 0.0).then_inc(s_zeroed, 1)
            dve.memset(ones[:, :], 1.0).then_inc(s_zeroed, 1)

            def split_patches(b):
                dve.wait_ge(s_patch_hi, b + 1)
                dve.tensor_tensor(mov[:, CH * BT:CH * BT + KP * BT], patch_raw, mov[:, 0:KP * BT].bitcast(F32),
                                  ALU.subtract).then_inc(s_patch_lo, 1)

            dve.wait_ge(s_tokw_hi, 1)
            dve.tensor_tensor(tok_lo, tok_raw, tok_hi.bitcast(F32), ALU.subtract).then_inc(s_tokw_lo, 1)
            split_patches(0)

            dve.wait_ge(s_decay_e, 1)
            n = [0]

            def power(ins):
                n[0] += 1
                ins.then_inc(s_pw_step, 1)

            def powers_done():
                dve.wait_ge(s_pw_step, n[0])

            e_neg, alpha = decay[:, 0:CH], decay[:, CH:2 * CH]
            power(dve.tensor_scalar(e_neg, e_neg, 1.0, None, ALU.add))
            powers_done()
            power(dve.reciprocal(alpha, e_neg))
            powers_done()
            power(dve.tensor_scalar(pw[:, :, HALF + 1], alpha, MIN_DECAY, None, ALU.max))
            power(dve.tensor_scalar(rw[:, :, SEQ - 2], alpha, MIN_DECAY, None, ALU.max))
            power(dve.memset(pw[:, :, HALF:HALF + 1], 1.0))
            power(dve.memset(rw[:, :, SEQ - 1:SEQ], 1.0))
            k = 1
            while k < SEQ - 1:
                m = min(k, SEQ - 1 - k)
                powers_done()
                power(dve.tensor_tensor(pw[:, :, HALF + k + 1:HALF + k + 1 + m], pw[:, :, HALF + 1:HALF + 1 + m],
                                        pw[:, :, HALF + k:HALF + k + 1].broadcast_to([P, CH, m]), ALU.mult))
                e = SEQ - 1
                power(dve.tensor_tensor(rw[:, :, e - k - m:e - k], rw[:, :, e - m:e],
                                        rw[:, :, e - k:e - k + 1].broadcast_to([P, CH, m]), ALU.mult))
                k *= 2
            powers_done()
            power(dve.reciprocal(pw[:, :, 0:HALF], rw[:, :, SEQ - 1 - HALF:SEQ - 1]))
            power(dve.reciprocal(rw[:, :, SEQ:SEQ + HALF], pw[:, :, HALF + 1:2 * HALF + 1]))
            powers_done()
            tq = tab_q[:, :].rearrange("p (c t) -> p c t", c=CH)
            tk = tab_k[:, :].rearrange("p (c t) -> p c t", c=CH)
            for j, (s0, ln) in enumerate(zip(STARTS, LENS)):
                for i in range(2):
                    dve.tensor_copy(tq[:, :, QOFF[j] + i * ln:QOFF[j] + (i + 1) * ln], pw[:, :, 0:ln])
                for s1, l1, o1 in list(zip(STARTS, LENS, QOFF))[:j + 1]:
                    r = SEQ - 1 - HALF - s0 + s1
                    for i in range(2):
                        last = dve.tensor_copy(tk[:, :, KOFF[j] + o1 + i * l1:KOFF[j] + o1 + (i + 1) * l1],
                                               rw[:, :, r:r + l1])
            last.then_inc(s_tables, 1)

            def two_banks(first, g):
                return bank[first + g // 2][0:GT, (g % 2) * D:(g % 2 + 1) * D]

            for b in range(BLOCKS):
                dve.wait_ge(s_h_turned, b + 1)
                for g in range(GROUPS):
                    ins = dve.bn_stats(stat[:, g, :], two_banks(2, g))
                ins.then_inc(s_stats, 1)
                dve.wait_ge(s_stats, b + 1)
                for g in range(GROUPS):
                    ins = dve.bn_aggr(mv[:, g, :], stat[:, g, :])
                ins.then_inc(s_agg, 1)
                dve.wait_ge(s_agg, b + 1)
                dve.tensor_scalar(ve, mv[:, :, 1], EPS, None, ALU.add).then_inc(s_veps, 1)
                dve.wait_ge(s_std, b + 1)
                dve.reciprocal(rstd, sd).then_inc(s_rstd, 1)
                dve.wait_ge(s_rstd, 3 * b + 1)
                for g in range(GROUPS):
                    ins = dve.tensor_scalar(x2_tok[0:GT, g * D:(g + 1) * D], two_banks(2, g), mv[:, g, 0:1],
                                            rstd[:, g:g + 1], ALU.subtract, ALU.mult)
                ins.then_inc(s_x2_done, 1)
                dve.tensor_tensor(r2, rstd, rstd, ALU.mult).then_inc(s_rstd, 1)
                dve.wait_ge(s_rstd, 3 * b + 2)
                dve.tensor_tensor(r2, r2, mv[:, :, 1], ALU.mult).then_inc(s_rstd, 1)
                dve.wait_ge(s_rstd, 3 * b + 3)
                dve.tensor_scalar(ve2, r2, EPS, None, ALU.add).then_inc(s_v2, 1)
                if b + 1 < BLOCKS:
                    split_patches(b + 1)
                dve.wait_ge(s_x2_done, b + 1)
                for g in range(GROUPS):
                    ins = dve.tensor_tensor(res(b)[:, g * D:(g + 1) * D], two_banks(2, g),
                                            x2_tok[0:GT, g * D:(g + 1) * D], ALU.add)
                ins.then_inc(s_res_done, 1)
                dve.wait_ge(s_std2, b + 1)
                dve.reciprocal(zsc, sd2).then_inc(s_zscale, 1)
                dve.wait_ge(s_zscale, b + 1)
                if b >= 1:
                    dve.wait_ge(s_z_turned, b)
                for g in range(GROUPS):
                    ins = dve.tensor_scalar(z_tok[0:GT, g * D:(g + 1) * D], x2_tok[0:GT, g * D:(g + 1) * D],
                                            zsc[:, g:g + 1], None, ALU.mult)
                ins.then_inc(s_z_done, 1)

            biases = par[:, PB + 2 * CH:PB + 4 * CH].rearrange("p (m c) -> p m c", m=2)

            def fetch_biases(c, w):
                dve.tensor_scalar(bias_now[w].rearrange("p (m o) -> p m o", o=1), biases[:, :, bass.ds(c, 1)],
                                  1.0, None, ALU.mult).then_inc(s_bias_ready, 1)

            def scale_keys(c, it):
                dve.wait_ge(s_k_proj, it + 1)
                src = bank[0][:, 0:BT].rearrange("p (g t) -> p g t", g=GROUPS)
                for j in range(len(ENDS)):
                    table = tab_k[:, bass.ds(c * KCOLS + KOFF[j], ENDS[j])]
                    ins = dve.scalar_tensor_tensor(
                        out=k_dec[j], in0=src[:, :, 0:ENDS[j]], scalar=par[:, bass.ds(PB + c, 1)],
                        in1=table.rearrange("p (o t) -> p o t", o=1).broadcast_to([P, GROUPS, ENDS[j]]),
                        op0=ALU.add, op1=ALU.mult)
                ins.then_inc(s_k_scaled, 1)

            def scale_queries(c, it):
                dve.wait_ge(s_q_proj, it + 1)
                for h in range(2):
                    rows = slice(h * D_HEAD, (h + 1) * D_HEAD)
                    ins = dve.scalar_tensor_tensor(
                        out=q_dec[rows, h, :].rearrange("p (g t) -> p g t", g=GROUPS),
                        in0=bank[1][rows, 0:BT].rearrange("p (g t) -> p g t", g=GROUPS),
                        scalar=par[rows, bass.ds(PB + CH + c, 1)],
                        in1=tab_q[rows, bass.ds(c * GT, GT)].rearrange("p (o t) -> p o t", o=1).broadcast_to(
                            [D_HEAD, GROUPS, GT]), op0=ALU.add, op1=ALU.mult)
                ins.then_inc(s_q_scaled, 1)

            def mask_scores(it):
                for k in range(2):
                    dve.wait_ge(s_scores, 2 * it + k + 1)
                    dve.tensor_tensor(
                        probs[0:GT, k * BT:(k + 1) * BT].rearrange("p (n t) -> p n t", n=4),
                        bank[6 + k][0:GT, 0:BT].rearrange("p (n t) -> p n t", n=4),
                        causal[0:GT, :].rearrange("p (o t) -> p o t", o=1).broadcast_to([GT, 4, GT]),
                        ALU.mult).then_inc(s_masked, 1)

            def gate_heads(c, b, it):
                dve.wait_ge(s_pv, it + 1)
                dve.wait_ge(s_gated, it + 1)
                dve.tensor_tensor(og_at(c, b), bank[5][:, 0:BT], gate, ALU.mult).then_inc(s_og_done, 1)

            def turn(q, last=False):
                for u in range(STEPS):
                    it = STEPS * q + u
                    mask_scores(it)
                    if not (last and u == STEPS - 1):
                        c = 2 * q + (u + 1) // BLOCKS
                        scale_keys(c, it + 1)
                        scale_queries(c, it + 1)
                    gate_heads(2 * q + u // BLOCKS, u % BLOCKS, it)
                    w = u // BLOCKS
                    if u % BLOCKS == 0 and not (last and w == 1):
                        fetch_biases(2 * q + w + 1, 1 - w)

            dve.wait_ge(s_tables, 1)
            fetch_biases(0, 0)
            scale_keys(0, 0)
            scale_queries(0, 0)
            with dve.Fori(0, CH // 2 - 1) as q:
                turn(q)
            turn(CH // 2 - 1, last=True)

            def split_heads(b):
                for k in range(CH):
                    dve.wait_ge(s_og_hi, CH * b + k + 1)
                    dve.tensor_tensor(mov_at(1, k), og[:, k * TOKENS + b * BT:k * TOKENS + (b + 1) * BT],
                                      mov_at(0, k).bitcast(F32), ALU.subtract).then_inc(s_og_lo, 1)

            rs = [0]

            def r_op(ins, steps=24):
                rs[0] += 1
                ins.then_inc(s_r_step, 1)
                dve.wait_ge(s_r_step, rs[0])

            def router(b):
                score3 = r_score.rearrange("p (g e) -> p g e", g=GROUPS)
                choice3 = r_choice.rearrange("p (g e) -> p g e", g=GROUPS)
                dve.wait_ge(s_exp_done, b + 1)
                r_op(dve.tensor_scalar(r_a, r_a, 1.0, None, ALU.add))
                r_op(dve.reciprocal(r_score, r_a))
                r_op(dve.tensor_tensor(choice3, score3, route_b[0:GT, :].rearrange("p (o e) -> p o e", o=1)
                                       .broadcast_to([GT, GROUPS, EXPERTS]), ALU.add))
                quad = r_choice.rearrange("p (n a) -> p n a", a=4)
                mx = r_max.rearrange("p (n a) -> p n a", a=2)
                mn = r_min.rearrange("p (n a) -> p n a", a=2)
                r_op(dve.tensor_tensor(mx, quad[:, :, 0:4:2], quad[:, :, 1:4:2], ALU.max))
                r_op(dve.tensor_tensor(mn, quad[:, :, 0:4:2], quad[:, :, 1:4:2], ALU.min))
                r_op(dve.tensor_tensor(r_gs, mx[:, :, 0], mx[:, :, 1], ALU.max))
                r_op(dve.tensor_tensor(r_t0, mx[:, :, 0], mx[:, :, 1], ALU.min))
                r_op(dve.tensor_tensor(r_t1, mn[:, :, 0], mn[:, :, 1], ALU.max))
                r_op(dve.tensor_tensor(r_t0, r_t0, r_t1, ALU.max))
                r_op(dve.tensor_tensor(r_gs, r_gs, r_t0, ALU.add))
                mine = r_gs.rearrange("p (n o) -> p n o", o=1).broadcast_to([GT, GG, ROUTE_GROUPS])
                c1, c2 = (c.rearrange("p (n j) -> p n j", j=ROUTE_GROUPS) for c in (cmp1, cmp2))
                for g in range(GROUPS):
                    n0 = g * ROUTE_GROUPS
                    theirs = r_gs[:, n0:n0 + ROUTE_GROUPS].rearrange("p (o j) -> p o j", o=1).broadcast_to(
                        [GT, ROUTE_GROUPS, ROUTE_GROUPS])
                    dve.tensor_tensor(c1[:, n0:n0 + ROUTE_GROUPS, :], theirs, mine[:, n0:n0 + ROUTE_GROUPS, :],
                                      ALU.is_gt)
                    ins = dve.tensor_tensor(c2[:, n0:n0 + ROUTE_GROUPS, :], theirs,
                                            mine[:, n0:n0 + ROUTE_GROUPS, :], ALU.is_equal)
                r_op(ins)
                r_op(dve.tensor_tensor(cmp2.rearrange("p (g n) -> p g n", g=GROUPS),
                                       cmp2.rearrange("p (g n) -> p g n", g=GROUPS),
                                       before[0:GT, :].rearrange("p (o n) -> p o n", o=1).broadcast_to(
                                           [GT, GROUPS, ROUTE_GROUPS * ROUTE_GROUPS]), ALU.mult))
                r_op(dve.tensor_tensor(cmp1, cmp1, cmp2, ALU.add))
                r_op(dve.tensor_reduce(r_sel, c1, AX.X, ALU.add))
                r_op(dve.tensor_scalar(r_sel, r_sel, TOP_GROUPS - 0.5, None, ALU.is_lt))
                r_op(dve.tensor_tensor(quad, quad, r_sel.rearrange("p (n o) -> p n o", o=1).broadcast_to(
                    [GT, GG, 4]), ALU.mult))
                r_op(dve.tensor_scalar(r_b, r_choice, 0.0, None, ALU.add))
                for g in range(GROUPS):
                    ins = dve.max(r_top[:, g * 8:(g + 1) * 8], r_b[:, g * EXPERTS:(g + 1) * EXPERTS])
                r_op(ins)
                for g in range(GROUPS):
                    ins = dve.match_replace(r_c[:, g * EXPERTS:(g + 1) * EXPERTS], r_top[:, g * 8:(g + 1) * 8],
                                            r_b[:, g * EXPERTS:(g + 1) * EXPERTS], -3e38)
                r_op(ins)
                r_op(dve.tensor_tensor(r_c, r_c, r_b, ALU.not_equal))
                r_op(dve.tensor_tensor(r_a, r_c, r_score, ALU.mult))
                r_op(dve.tensor_reduce(r_sum, r_a.rearrange("p (g e) -> p g e", g=GROUPS), AX.X, ALU.add))
                r_op(dve.tensor_scalar(r_sum, r_sum, 1e-20, None, ALU.add))
                r_op(dve.reciprocal(r_inv, r_sum))
                if b >= 1:
                    dve.wait_ge(s_comb_turned, b)
                for g in range(GROUPS):
                    ins = dve.tensor_scalar(comb_tok[:, g * EXPERTS:(g + 1) * EXPERTS],
                                            r_a[:, g * EXPERTS:(g + 1) * EXPERTS], r_inv[:, g:g + 1], ROUTE_SCALE,
                                            ALU.mult, ALU.mult)
                ins.then_inc(s_comb_done, 1)

            split_heads(0)
            for b in range(BLOCKS):
                dve.wait_ge(s_y_turned, b + 1)
                for k in range(2):
                    ins = dve.tensor_tensor(h2_tok[0:GT, k * 2 * D:(k + 1) * 2 * D], bank[2 + k][0:GT, :],
                                            res(b)[:, k * 2 * D:(k + 1) * 2 * D], ALU.add)
                    ins.then_inc(s_h2_done, 1)
                dve.wait_ge(s_h2_done, 2 * (b + 1))
                for g in range(GROUPS):
                    ins = dve.bn_stats(stat[:, g, :], h2_tok[0:GT, g * D:(g + 1) * D])
                ins.then_inc(s_stats2, 1)
                dve.wait_ge(s_stats2, b + 1)
                for g in range(GROUPS):
                    ins = dve.bn_aggr(mv[:, g, :], stat[:, g, :])
                ins.then_inc(s_agg2, 1)
                dve.wait_ge(s_agg2, b + 1)
                dve.tensor_scalar(ve, mv[:, :, 1], EPS, None, ALU.add).then_inc(s_veps2, 1)
                dve.wait_ge(s_std3, b + 1)
                dve.reciprocal(rstd_n, sd).then_inc(s_rstd2, 1)
                dve.wait_ge(s_rstd2, b + 1)
                for g in range(GROUPS):
                    ins = dve.tensor_scalar(x3_tok[0:GT, g * D:(g + 1) * D], h2_tok[0:GT, g * D:(g + 1) * D],
                                            mv[:, g, 0:1], rstd_n[:, g:g + 1], ALU.subtract, ALU.mult)
                ins.then_inc(s_x3_done, 1)
                if b + 1 < BLOCKS:
                    split_heads(b + 1)
                router(b)

            def expert(p, b, n, w, first=False):
                for e in range(2):
                    dve.wait_ge(s_u_ready, 2 * n + e + 1)
                    dve.wait_ge(s_weighted_done, 2 * n + e + 1)
                    if not first:
                        dve.wait_ge(s_hid_lo, 2 * n - 1 + e)
                    dve.tensor_tensor(hidden[e], bank[2 * e + 1][:, 0:BT], weighted[e], ALU.mult).then_inc(
                        s_hidden_done, 1)
                for e in range(2):
                    dve.wait_ge(s_hid_hi, 2 * n + e + 1)
                    dve.tensor_tensor(mov_at(b % 2, 2 * e + 1), hidden[e], mov_at(b % 2, 2 * e).bitcast(F32),
                                      ALU.subtract).then_inc(s_hid_lo, 1)
                if b < 3 and w is not None:
                    cols = slice(b * 2 * D, (b + 1) * 2 * D)
                    hi, lo = weight_parts(wbuf[1 - w], PAIR_COLS)
                    dve.wait_ge(s_wsplit_hi, 3 * p + b + 1)
                    dve.tensor_tensor(lo[:, cols], raw[:, (1 - w) * PAIR_COLS:(2 - w) * PAIR_COLS][:, cols],
                                      hi[:, cols].bitcast(F32), ALU.subtract).then_inc(s_wsplit_lo, 1)
                if not first:
                    add_down((b - 1) % BLOCKS, n - 1, b >= 1 and isinstance(p, int) and p == 0)

            def add_down(b, n, fresh=False):
                dve.wait_ge(s_y_ready, n + 1)
                if not fresh:
                    dve.wait_ge(s_added, n - BLOCKS + 1)
                for m in range(KD):
                    ins = dve.tensor_tensor(acc(b, m), bank[4 + 2 * (b % 2) + m][:, 0:BT], acc(b, m), ALU.add)
                ins.then_inc(s_added, 1)

            def pair(p, w, first=False, last=False):
                for b in range(BLOCKS):
                    expert(p, b, BLOCKS * p + b, None if last else w, first=first and b == 0)

            dve.wait_ge(s_acc_set, 2 * BLOCKS)
            pair(0, 0, first=True)
            pair(1, 1)
            with dve.Fori(1, PAIRS // 2) as q:
                pair(2 * q, 0)
                pair(2 * q + 1, 1)
            pair(PAIRS - 1, 0, last=True)
            add_down(BLOCKS - 1, BLOCKS * PAIRS - 1)

        @block.scalar
        def _(act):
            def split_patches(b):
                act.wait_ge(s_patch_in, 16 * (b + 1))
                if b >= 1:
                    act.wait_ge(s_h_proj, 2 * b)
                act.activation(mov[:, 0:KP * BT], patch_raw, ACT.Copy).then_inc(s_patch_hi, 1)

            act.wait_ge(s_tokw_in, 16)
            act.activation(tok_hi, tok_raw, ACT.Copy).then_inc(s_tokw_hi, 1)
            split_patches(0)
            act.wait_ge(s_params_in, 16)
            act.activation(decay[:, 0:CH], par[:, PLOGIT:PLOGIT + CH], ACT.Exp, scale=-1.0).then_inc(s_decay_e, 1)
            for b in range(BLOCKS):
                for m in range(KD):
                    act.wait_ge(s_h_proj, 2 * b + m + 1)
                    act.activation(h_ch[:, m * BT:(m + 1) * BT], bank[m][:, 0:BT], ACT.Identity,
                                   bias=par[:, PTOKB + m:PTOKB + m + 1]).then_inc(s_h_copied, 1)
                if b + 1 < BLOCKS:
                    split_patches(b + 1)
                act.wait_ge(s_veps, b + 1)
                act.activation(sd, ve, ACT.Sqrt).then_inc(s_std, 1)
                act.wait_ge(s_v2, b + 1)
                act.activation(sd2, ve2, ACT.Sqrt).then_inc(s_std2, 1)
                act.wait_ge(s_z_turned, b + 1)
                if b >= 1:
                    act.wait_ge(s_xn_split, 2 * b)
                for m in range(KD):
                    ins = act.activation(xn_ch[:, m * BT:(m + 1) * BT], bank[4 + m][:, 0:BT], ACT.Identity,
                                         bias=par[:, PBETA + m:PBETA + m + 1], scale=par[:, PGAMMA + m:PGAMMA + m + 1])
                ins.then_inc(s_xn_done, 1)

            def step(c, it, w):
                act.wait_ge(s_v_proj, it + 1)
                act.wait_ge(s_bias_ready, c + 1)
                act.activation(v_ch, bank[2][:, 0:BT], ACT.Identity,
                               bias=bias_now[w][:, 0:1]).then_inc(s_v_copied, 1)
                act.wait_ge(s_v_turned, it + 1)
                act.activation(v_tok[0:GT, :, :].rearrange("p g c -> p (g c)"), bank[4][0:GT, :],
                               ACT.Copy).then_inc(s_v_ready, 1)
                act.wait_ge(s_g_proj, it + 1)
                act.wait_ge(s_og_done, it + 1)
                act.activation(gate, bank[3][:, 0:BT], ACT.Silu,
                               bias=bias_now[w][:, 1:2]).then_inc(s_gated, 1)

            with act.Fori(0, CH // 2) as q:
                for u in range(STEPS):
                    step(2 * q + u // BLOCKS, STEPS * q + u, u // BLOCKS)

            def split_heads(b):
                for k in range(CH):
                    if b == 0:
                        act.wait_ge(s_og_done, BLOCKS * k + 2)
                    else:
                        act.wait_ge(s_og_used, CH * (b - 1) + k + 1)
                        act.wait_ge(s_og_done, STEPS * CH // 2 + 1)
                    act.activation(mov_at(0, k), og[:, k * TOKENS + b * BT:k * TOKENS + (b + 1) * BT],
                                   ACT.Copy).then_inc(s_og_hi, 1)

            def keep_comb(b):
                act.wait_ge(s_comb_turned, b + 1)
                if b >= 1:
                    act.wait_ge(s_stored, 16 * b)
                act.activation(comb_sb, bank[5][0:EXPERTS, 0:BT], ACT.Copy).then_inc(s_comb_kept, 1)

            split_heads(0)
            for b in range(BLOCKS):
                act.wait_ge(s_og_used, CH * (b + 1))
                if b >= 1:
                    act.wait_ge(s_y_turned, b)
                for m in range(KD):
                    act.activation(y_ch[:, m * BT:(m + 1) * BT], bank[m][:, 0:BT], ACT.Identity,
                                   bias=par[:, PBO + m:PBO + m + 1]).then_inc(s_y_copied, 1)
                act.wait_ge(s_veps2, b + 1)
                act.activation(sd, ve, ACT.Sqrt).then_inc(s_std3, 1)
                if b + 1 < BLOCKS:
                    split_heads(b + 1)
                if b >= 1:
                    keep_comb(b - 1)
                act.wait_ge(s_h2_turned, b + 1)
                for m in range(KD):
                    act.activation(acc(b, m), bank[4 + m][:, 0:BT], ACT.Copy).then_inc(s_acc_set, 1)
                act.wait_ge(s_x3_turned, b + 1)
                if b >= 1:
                    act.wait_ge(s_x3_split, 2 * b)
                for m in range(KD):
                    act.activation(x3_ch[:, m * BT:(m + 1) * BT], bank[6 + m][:, 0:BT], ACT.Copy).then_inc(
                        s_x3_copied, 1)
                act.wait_ge(s_logits, b + 1)
                if b >= 1:
                    act.wait_ge(s_comb_done, b)
                act.activation(r_a, bank[4][0:GT, 0:GE], ACT.Exp, scale=-1.0).then_inc(s_exp_done, 1)
            keep_comb(BLOCKS - 1)

            def expert(p, b, n, w, first=False):
                for e in range(2):
                    act.wait_ge(s_g_ready, 2 * n + e + 1)
                    if not first:
                        act.wait_ge(s_weighted_done, 2 * n - 1 + e)
                    act.activation(silu_g[e], bank[2 * e][:, 0:BT], ACT.Silu).then_inc(s_silu_done, 1)
                for e in range(2):
                    act.wait_ge(s_hidden_done, 2 * n + e + 1)
                    act.activation(mov_at(b % 2, 2 * e), hidden[e], ACT.Copy).then_inc(s_hid_hi, 1)
                if b < 3 and w is not None:
                    if b == 0:
                        if w == 0:
                            act.wait_ge(s_pair_in1, 8 * p + 16)
                        else:
                            act.wait_ge(s_pair_in, 8 * p + 24)
                        if not first:
                            act.wait_ge(s_y_ready, n)
                    cols = slice(b * 2 * D, (b + 1) * 2 * D)
                    hi, lo = weight_parts(wbuf[1 - w], PAIR_COLS)
                    act.activation(hi[:, cols], raw[:, (1 - w) * PAIR_COLS:(2 - w) * PAIR_COLS][:, cols],
                                   ACT.Copy).then_inc(s_wsplit_hi, 1)

            def pair(p, w, first=False, last=False):
                for b in range(BLOCKS):
                    expert(p, b, BLOCKS * p + b, None if last else w, first=first and b == 0)

            pair(0, 0, first=True)
            pair(1, 1)
            with act.Fori(1, PAIRS // 2) as q:
                pair(2 * q, 0)
                pair(2 * q + 1, 1)
            pair(PAIRS - 1, 0, last=True)

        @block.gpsimd
        def _(pool):
            def split_chunk(w, cols):
                hi, lo = weight_parts(wbuf[w], cols)
                src = raw[:, w * cols:(w + 1) * cols]
                return hi, lo, src

            def split_weights(hi, lo, src, done, count):
                pool.tensor_copy(hi, src).then_inc(done, 1)
                pool.wait_ge(done, count + 1)
                pool.tensor_tensor(lo, src, hi.bitcast(F32), ALU.subtract).then_inc(done, 1)

            pool.wait_ge(s_chunk_in, 16)
            split_weights(*split_chunk(0, CHUNK_COLS), s_chunk_split, 0)

            xparts = [t[:, :].rearrange("p (k t) -> p k t", k=KD) for t in xn]

            def split_input(b, src, copied, done):
                src = src.rearrange("p (k t) -> p k t", k=KD)
                pool.wait_ge(*copied)
                pool.tensor_copy(xparts[0][:, :, b * BT:(b + 1) * BT], src).then_inc(done, 1)
                pool.wait_ge(done, 2 * b + 1)
                pool.tensor_tensor(xparts[1][:, :, b * BT:(b + 1) * BT], src,
                                   xparts[0][:, :, b * BT:(b + 1) * BT].bitcast(F32),
                                   ALU.subtract).then_inc(done, 1)

            for b in range(BLOCKS):
                split_input(b, xn_ch, (s_xn_done, b + 1), s_xn_split)
            pool.wait_ge(s_chunk_in1, 16)
            split_weights(*split_chunk(1, CHUNK_COLS), s_chunk_split, 2)

            for c in range(2, CH):
                pool.wait_ge((s_chunk_in, s_chunk_in1)[c % 2], 16 * (c // 2 + 1))
                pool.wait_ge(s_g_proj, BLOCKS * (c - 1))
                split_weights(*split_chunk(c % 2, CHUNK_COLS), s_chunk_split, 2 * c)
            half = CH * D // 2
            for i in range(2):
                pool.wait_ge(s_wo_in, 16 * (i + 1))
                split_weights(wo_hi[:, i * half:(i + 1) * half], wo_lo[:, i * half:(i + 1) * half],
                              raw[:, 2 * CHUNK_COLS:3 * CHUNK_COLS], s_wo_split, 2 * i)
            pool.wait_ge(s_pair_in, 16)
            pool.wait_ge(s_g_proj, STEPS * CH // 2)
            split_weights(*split_chunk(0, PAIR_COLS), s_pair0_split, 0)

            for b in range(BLOCKS):
                split_input(b, x3_ch, (s_x3_copied, 2 * (b + 1)), s_x3_split)

            def expert(b, n, arrivals):
                pool.wait_ge((s_comb_in, s_comb_in1)[b % 2], arrivals)
                for e in range(2):
                    pool.wait_ge(s_silu_done, 2 * n + e + 1)
                    if not (isinstance(n, int) and n == 0):
                        pool.wait_ge(s_hidden_done, 2 * n - 1 + e)
                    pool.tensor_tensor(weighted[e], silu_g[e], comb[b % 2][:, e * BT:(e + 1) * BT],
                                       ALU.mult).then_inc(s_weighted_done, 1)

            def pair(p):
                for b in range(BLOCKS):
                    expert(b, BLOCKS * p + b, 64 * p + 32 * (b // 2 + 1))

            pair(0)
            with pool.Fori(1, PAIRS) as p:
                pair(p)


def _token_order():
    import numpy as np
    order = []
    for g in range(IMAGES // 2):
        for s0, ln in zip(STARTS, LENS):
            for i in range(2):
                order += [(2 * g + i) * SEQ + s0 + t for t in range(ln)]
    return np.array(order)


def kernel(**inputs):
    import numpy as np
    import concourse.bacc as _bacc
    from concourse import mybir as _mybir
    from concourse.bass_utils import run_bass_kernel_spmd as _run

    a = {k: np.asarray(v) for k, v in inputs.items()}
    f = np.ascontiguousarray
    order = _token_order()

    def chunked(w):
        return w.reshape(-1, P, w.shape[-1]).transpose(1, 0, 2)

    x = a["x"].reshape(IMAGES, 3, 7, 16, 7, 16).transpose(0, 2, 4, 3, 5, 1).reshape(TOKENS, PATCH_D)
    patches = x[order].T.reshape(KP, P, BLOCKS, BT).transpose(1, 2, 0, 3).reshape(P, BLOCKS, KP * BT)
    w_tok = chunked(a["L0_tok_W"].T).reshape(P, KP * D)
    mats = np.stack([a[f"L0_attn_{n}"] for n in ("WK", "WQ", "WV", "Wg")])
    w_qkvg = mats.reshape(MATS, CH, P, KD, P).transpose(1, 4, 0, 3, 2).reshape(CH, P, CHUNK_COLS)
    w_o = chunked(a["L0_attn_WO"].T).reshape(P, 2, CH * D // 2).transpose(1, 0, 2)
    I = 128
    gates = np.concatenate([a["L0_ffn_w_gate"], a["L0_ffn_sh_gate"].reshape(SHARED, I, D)])
    ups = np.concatenate([a["L0_ffn_w_up"], a["L0_ffn_sh_up"].reshape(SHARED, I, D)])
    downs = np.concatenate([a["L0_ffn_w_down"], a["L0_ffn_sh_down"].reshape(D, SHARED, I).transpose(1, 0, 2)])
    E = EXPERTS + SHARED
    gu = np.stack([gates, ups], 1).reshape(E, 2, I, KD, P).transpose(0, 4, 3, 1, 2).reshape(E, P, KD * D)
    w_ffn = np.concatenate([gu, downs.transpose(0, 2, 1)], 2)
    w_ffn = w_ffn.reshape(PAIRS, 2, P, 3 * D).transpose(0, 2, 1, 3).reshape(PAIRS, P, PAIR_COLS)

    def column(v):
        return v.reshape(-1, P).T

    params = np.concatenate([column(a[f"L0_attn_{n}"]) for n in ("bK", "bQ", "bV", "bg")]
                            + [column(a["L0_attn_alpha_logit"].reshape(-1)), column(a["L0_tok_b"]),
                               column(a["L0_attn_bO"]), column(a["L0_attn_ln_gamma"]),
                               column(a["L0_attn_ln_beta"])], 1)
    image = np.concatenate([[i] * ln for ln in LENS for i in range(2)])
    time = np.concatenate([np.arange(s0, s0 + ln) for s0, ln in zip(STARTS, LENS) for i in range(2)])
    causal = ((image[:, None] == image[None]) & (time[:, None] <= time[None])).astype(np.float32)
    before = np.tile((np.arange(8)[None] < np.arange(8)[:, None]).astype(np.float32).reshape(1, 64), (GT, 1))
    arrays = {
        "patches": patches, "w_tok": w_tok, "w_qkvg": w_qkvg, "w_o": w_o, "w_ffn": w_ffn, "params": params,
        "w_route": chunked(a["L0_ffn_gate_w"].T).reshape(P, KD * EXPERTS),
        "b_route": a["L0_ffn_gate_bias"].reshape(1, EXPERTS),
        "identity": np.eye(P, dtype=np.float32), "causal_order": causal, "group_order": before,
    }
    nc = _bacc.Bacc("TRN2", target_bir_lowering=False, num_devices=1)
    args, arrays = [], {k: f(v) for k, v in arrays.items()}
    for name, v in arrays.items():
        args.append(nc.dram_tensor("in_" + name, v.shape, _mybir.dt.from_np(v.dtype), kind="ExternalInput").ap())
    args.append(nc.dram_tensor("comb_dram", (E, TOKENS), F32, kind="Internal").ap())
    args.append(nc.dram_tensor("out_ch", (P, BLOCKS, KD * BT), F32, kind="ExternalOutput").ap())
    build(nc, *args)
    r = _run(nc, [{"in_" + k: v for k, v in arrays.items()}], core_ids=[0])
    got = r.results[0]["out_ch"].reshape(P, BLOCKS, KD, BT).transpose(1, 3, 2, 0).reshape(TOKENS, D)
    y = np.empty_like(got)
    y[order] = got
    return y.reshape(IMAGES, SEQ, D)
```

```python
from contextlib import ExitStack

import concourse.bass as bass
from concourse import mybir

ALU = mybir.AluOpType
ACT = mybir.ActivationFunctionType
AX = mybir.AxisListType
F32 = mybir.dt.float32
F32R = mybir.dt.float32r

P = 128
IMAGES, SEQ, D = 32, 49, 256
PATCH_D = 768
HEADS, D_HEAD = 16, 64
D_INNER = HEADS * D_HEAD
EXPERTS, SHARED, TOP_GROUPS, ROUTE_SCALE = 32, 2, 4, 2.5
ROUTE_GROUPS = 8
EPS = 1e-5

TOKENS = IMAGES * SEQ
GT = 2 * SEQ
GROUPS = 4
BT = GROUPS * GT
BLOCKS = TOKENS // BT
KD = D // P
KP = PATCH_D // P
CH = D_INNER // P
STARTS = (0, 9, 17, 25, 33, 41)
LENS = (9, 8, 8, 8, 8, 8)
HALF = 4
MIN_DECAY = 1e-8
QOFF = [2 * s for s in STARTS]
ENDS = [2 * (s + n) for s, n in zip(STARTS, LENS)]
KOFF = [sum(ENDS[:j]) for j in range(len(ENDS))]
KCOLS = sum(ENDS)
POWERS = SEQ + HALF
STEPS = 2 * BLOCKS
PAIRS = (EXPERTS + SHARED) // 2
MATS = 4
PAIR_COLS = 2 * 3 * D
CHUNK_COLS = MATS * KD * P

PB, PLOGIT, PTOKB, PBO, PGAMMA, PBETA, PCOLS = 0, 32, 40, 42, 44, 46, 48


def build(nc, patches, w_tok, w_qkvg, w_o, w_ffn, params, w_route, b_route, ident_d, causal_d,
          before_d, comb_rows, out):
    with ExitStack() as ctx:
        def sb(name, cols, dt=F32, rows=P):
            return ctx.enter_context(nc.sbuf_tensor(name, [rows, cols], dt))

        def sem(name):
            return ctx.enter_context(nc.semaphore(name))

        bank = [ctx.enter_context(nc.psum_tensor(f"bank{i}", [P, 512], F32)) for i in range(8)]

        xn = [sb("xn_hi", KD * TOKENS, F32R), sb("xn_lo", KD * TOKENS, F32R)]
        mov = sb("moving_parts", 2 * CH * BT, F32R)
        wbuf = [sb("weights_even", 2 * PAIR_COLS, F32R), sb("weights_odd", 2 * PAIR_COLS, F32R)]
        w_edge = sb("weights_tok_out", 2 * CH * D, F32R)
        og = sb("gated_heads", CH * TOKENS)
        token_store = sb("token_store", BLOCKS * GROUPS * D)
        raw = sb("weights_raw", 2 * PAIR_COLS)
        par = sb("channel_params", PCOLS)
        ident = sb("identity", P)
        causal = sb("causal", GT)
        before = sb("before", ROUTE_GROUPS * ROUTE_GROUPS)
        route_w = sb("route_w", KD * EXPERTS)
        route_b = sb("route_b", EXPERTS)
        decay = sb("decay", 2 * CH)
        tab_q = sb("powers_q", CH * GT)
        tab_k = sb("powers_k", CH * KCOLS)
        work = sb("work", 2 * BT + GROUPS * KCOLS + 2 * BT + BT + GROUPS * P + BT + 656)
        small = sb("small", 96)
        rt = sb("router", 11 * GROUPS * EXPERTS + 2 * GROUPS * ROUTE_GROUPS)

        def cut(t, at, n):
            return t[:, at:at + n], at + n

        at = 0
        q_dec, at = cut(work, at, 2 * BT)
        k_dec, at = cut(work, at, GROUPS * KCOLS)
        probs, at = cut(work, at, 2 * BT)
        v_ch, at = cut(work, at, BT)
        v_tok, at = cut(work, at, GROUPS * P)
        gate, at = cut(work, at, BT)
        q_dec = q_dec.rearrange("p (h t) -> p h t", h=2)
        v_tok = v_tok.rearrange("p (g c) -> p g c", g=GROUPS)
        k_dec = [k_dec[:, GROUPS * KOFF[j]:GROUPS * (KOFF[j] + ENDS[j])].rearrange("p (g s) -> p g s", g=GROUPS)
                 for j in range(len(ENDS))]
        at = 0
        y_ch, at = cut(work, at, KD * BT)
        h2_tok, at = cut(work, at, GROUPS * D)
        x3_tok, at = cut(work, at, GROUPS * D)
        x3_ch, at = cut(work, at, KD * BT)
        cmp1, at = cut(work, at, GROUPS * ROUTE_GROUPS ** 2)
        cmp2, at = cut(work, at, GROUPS * ROUTE_GROUPS ** 2)
        cmp1, cmp2 = cmp1[0:GT, :], cmp2[0:GT, :]
        comb_sb = [None, None]
        for k in range(2):
            comb_sb[k], at = cut(work, at, BT)
            comb_sb[k] = comb_sb[k][0:EXPERTS, :]
        at = CH * TOKENS // 2
        patch_raw = [None, None]
        patch_raw[0], at = cut(og, at, KP * BT)
        patch_raw[1] = og[:, 3584:3584 + KP * BT]
        h_ch, at = cut(og, at, KD * BT)
        x2_tok, at = cut(og, at, GROUPS * D)
        z_tok, at = cut(og, at, GROUPS * D)
        xn_ch, at = cut(og, at, KD * BT)
        tok_raw = og[:, 0:KP * D]
        pw = og[:, 2048:2048 + CH * POWERS].rearrange("p (c e) -> p c e", c=CH)
        rw = og[:, 3072:3072 + CH * POWERS].rearrange("p (c e) -> p c e", c=CH)
        at = 0
        silu_g, weighted, hidden, comb = [], [], [], []
        for e in range(2):
            t, at = cut(og, at, BT)
            silu_g.append(t)
            t, at = cut(og, at, BT)
            weighted.append(t)
            t, at = cut(og, at, BT)
            hidden.append(t)
        for k in range(2):
            t, at = cut(og, at, 2 * BT)
            comb.append(t)

        def og_at(c, b):
            return og[:, bass.ds(c * TOKENS + b * BT, BT)]

        def xn_at(part, k, b):
            return xn[part][:, k * TOKENS + b * BT:k * TOKENS + (b + 1) * BT]

        def res(b):
            return token_store[0:GT, b * GROUPS * D:(b + 1) * GROUPS * D]

        def acc(b, m):
            return token_store[:, b * GROUPS * D + m * BT:b * GROUPS * D + (m + 1) * BT]

        def mov_at(part, c):
            return mov[:, (part * CH + c) * BT:(part * CH + c + 1) * BT]

        def rview(at, n):
            return rt[0:GT, at:at + n]

        GE, GG = GROUPS * EXPERTS, GROUPS * ROUTE_GROUPS
        r_score, r_choice = rview(0, GE), rview(GE, GE)
        r_a, r_b, r_c = rview(2 * GE, GE), rview(3 * GE, GE), rview(4 * GE, GE)
        comb_tok = [rview(5 * GE, GE), rview(8 * GE + 2 * GG, GE)]
        r_exp = [rview(9 * GE + 2 * GG, GE), rview(10 * GE + 2 * GG, GE)]
        r_max, r_min = rview(6 * GE, 2 * GG), rview(6 * GE + 2 * GG, 2 * GG)
        r_gs, r_sel, r_t0, r_t1 = (rview(7 * GE + i * GG, GG) for i in range(4))
        r_top = rview(8 * GE, GG)
        r_sum = rview(8 * GE + GG, GROUPS)
        r_inv = rview(8 * GE + GG + GROUPS, GROUPS)

        stat = small[0:GT, 0:GROUPS * 6].rearrange("p (g n) -> p g n", g=GROUPS)
        mv = small[0:GT, 24:24 + GROUPS * 2].rearrange("p (g n) -> p g n", g=GROUPS)
        ve = small[0:GT, 32:32 + GROUPS]
        sd = small[0:GT, 36:36 + GROUPS]
        rstd = small[0:GT, 40:40 + GROUPS]
        r2 = small[0:GT, 44:44 + GROUPS]
        ve2 = small[0:GT, 48:48 + GROUPS]
        sd2 = small[0:GT, 52:52 + GROUPS]
        rstd_n = small[0:GT, 56:56 + GROUPS]
        bias_now = [small[:, 64:66], small[:, 66:68]]
        zsc = small[0:GT, 60:60 + GROUPS]

        s_patch_in = [[sem(f"patch_in_{par_name}_{i}") for i in range(KP // 2)] for par_name in ("even", "odd")]
        s_tokw_in = [sem(f"tokw_in_{i}") for i in range(KP // 2)]
        s_params_in = sem("params_in")
        s_consts_in = sem("consts_in")
        s_chunk_in = [sem("chunk_in_even"), sem("chunk_in_odd")]
        s_wo_in = sem("wo_in")
        s_patch_hi = sem("patch_hi")
        s_patch_lo = sem("patch_lo")
        s_patch_lo_odd = sem("patch_lo_odd")
        s_chunk_split = sem("chunk_split")
        s_wo_split = sem("wo_split")
        s_pair_in = [sem("pair_in_even"), sem("pair_in_odd")]
        s_comb_kept = sem("comb_kept")
        s_stored = [sem("stored_even"), sem("stored_odd")]
        s_comb_in = [sem("comb_in_even"), sem("comb_in_odd")]
        s_wsplit_hi = sem("wsplit_hi")
        s_wsplit_lo = sem("wsplit_lo")
        s_weighted_done = sem("weighted_done")
        s_added = sem("added")
        s_out_done = sem("out_done")
        s_h_copied = sem("h_copied")
        s_tokw_hi = sem("tokw_hi")
        s_tokw_lo = sem("tokw_lo")
        s_patch_used = sem("patch_used")
        s_res_done = sem("res_done")
        s_h_turned = sem("h_turned")
        s_z_done = sem("z_done")
        s_xn_done = sem("xn_done")
        s_z_turned = sem("z_turned")
        s_xn_split = sem("xn_split")
        s_k_proj = sem("k_proj")
        s_q_proj = sem("q_proj")
        s_v_proj = sem("v_proj")
        s_g_proj = sem("g_proj")
        s_k_scaled = sem("k_scaled")
        s_q_scaled = sem("q_scaled")
        s_v_copied = sem("v_copied")
        s_gated = sem("gated")
        s_v_ready = sem("v_ready")
        s_v_turned = sem("v_turned")
        s_masked = sem("masked")
        s_scores = sem("scores")
        s_og_done = sem("og_done")
        s_pv = sem("pv")
        s_zeroed = sem("zeroed")
        s_y_copied = sem("y_copied")
        s_og_first = sem("og_first")
        s_og_hi = sem("og_hi")
        s_og_lo = sem("og_lo")
        s_og_used = sem("og_used")
        s_h2_done = sem("h2_done")
        s_y_turned = sem("y_turned")
        s_acc_set = sem("acc_set")
        s_h2_turned = sem("h2_turned")
        s_x3_done = sem("x3_done")
        s_exp_done = sem("exp_done")
        s_x3_turned = sem("x3_turned")
        s_x3_copied = sem("x3_copied")
        s_logits = sem("logits")
        s_comb_done = sem("comb_done")
        s_comb_turned = sem("comb_turned")
        s_pair0_split = sem("pair0_split")
        s_x3_hi = sem("x3_hi")
        s_x3_lo = sem("x3_lo")
        s_g_ready = sem("g_ready")
        s_silu_done = sem("silu_done")
        s_u_ready = sem("u_ready")
        s_hidden_done = sem("hidden_done")
        s_hid_hi = sem("hid_hi")
        s_hid_lo = sem("hid_lo")
        s_y_ready = sem("y_ready")
        s_decay_e = sem("decay_e")
        s_pw_step = sem("pw_step")
        s_tables = sem("tables")
        s_stats = sem("stats")
        s_agg = sem("agg")
        s_veps = sem("veps")
        s_std = sem("std")
        s_rstd = sem("rstd")
        s_x2_done = sem("x2_done")
        s_v2 = sem("v2")
        s_std2 = sem("std2")
        s_zscale = sem("zscale")
        s_bias_ready = sem("bias_ready")
        s_r_step = sem("r_step")
        s_stats2 = sem("stats2")
        s_agg2 = sem("agg2")
        s_veps2 = sem("veps2")
        s_std3 = sem("std3")
        s_rstd2 = sem("rstd2")

        block = ctx.enter_context(nc.Block())

        def weight_parts(w, cols):
            return w[:, 0:cols], w[:, cols:2 * cols]

        tok_hi, tok_lo = weight_parts(w_edge, KP * D)
        wo_hi, wo_lo = weight_parts(w_edge, CH * D)

        @block.sync
        def _(sp):

            def load_patches(b):
                for i in range(KP // 2):
                    cols = slice(2 * i * BT, 2 * (i + 1) * BT)
                    sp.dma_start(patch_raw[b % 2][:, cols], patches[:, b, cols]).then_inc(s_patch_in[b % 2][i], 16)

            load_patches(0)
            sp.dma_start(par[:, :], params).then_inc(s_params_in, 16)
            load_patches(1)
            sp.dma_start(ident[:, :], ident_d).then_inc(s_consts_in, 16)
            sp.dma_start(causal[0:GT, :], causal_d).then_inc(s_consts_in, 16)
            sp.dma_start(before[0:GT, :], before_d).then_inc(s_consts_in, 16)
            sp.dma_start(route_w[:, :], w_route).then_inc(s_consts_in, 16)
            sp.dma_start(route_b[0:GT, :], b_route.broadcast_to([GT, EXPERTS])).then_inc(s_consts_in, 16)
            for c in range(2):
                sp.dma_start(raw[:, c * CHUNK_COLS:(c + 1) * CHUNK_COLS], w_qkvg[c]).then_inc(s_chunk_in[c], 16)
            sp.dma_start(raw[:, 2 * CHUNK_COLS:3 * CHUNK_COLS], w_o[0]).then_inc(s_wo_in, 16)
            for b in range(2, BLOCKS):
                sp.wait_ge(s_patch_hi, KP * (b - 1))
                sp.wait_ge(s_patch_lo, KP + (b - 2) * KP // 2)
                if b == 3:
                    sp.wait_ge(s_patch_lo_odd, KP // 2)
                load_patches(b)
            with sp.Fori(0, CH // 2 - 1) as q:
                for w in range(2):
                    sp.wait_ge(s_chunk_split, 4 * q + 2 * (w + 1))
                    sp.dma_start(raw[:, w * CHUNK_COLS:(w + 1) * CHUNK_COLS],
                                 w_qkvg[bass.ds(2 * q + 2 + w, 1)].rearrange("a p n -> p (a n)")
                                 ).then_inc(s_chunk_in[w], 16)
            sp.wait_ge(s_wo_split, 2)
            sp.dma_start(raw[:, 2 * CHUNK_COLS:3 * CHUNK_COLS], w_o[1]).then_inc(s_wo_in, 16)
            sp.wait_ge(s_wo_split, 4)
            sp.wait_ge(s_chunk_split, 2 * CH)
            for p in range(2):
                sp.dma_start(raw[:, p * PAIR_COLS:(p + 1) * PAIR_COLS], w_ffn[p]).then_inc(s_pair_in[p], 16)

            def store_comb(b):
                sp.wait_ge(s_comb_kept, b + 1)
                sp.dma_start(comb_rows[:, b * BT:(b + 1) * BT], comb_sb[b % 2]).then_inc(s_stored[b % 2], 16)

            def load_comb(pair, b):
                for e in range(2):
                    sp.dma_start(comb[b % 2][:, e * BT:(e + 1) * BT],
                                 comb_rows[bass.ds(2 * (pair - 1) + e, 1), b * BT:(b + 1) * BT
                                           ].broadcast_to([P, BT])).then_inc(s_comb_in[b % 2], 16)

            def load_weights(p, w):
                sp.dma_start(raw[:, w * PAIR_COLS:(w + 1) * PAIR_COLS],
                             w_ffn[bass.ds(p + 2, 1)].rearrange("a p n -> p (a n)")).then_inc(s_pair_in[w], 16)

            def load_weights_after_split(p, w):
                sp.wait_ge(s_wsplit_hi, 3 * p)
                sp.wait_ge(s_wsplit_lo, 3 * p)
                load_weights(p, w)

            sp.wait_ge(s_pair0_split, 2)
            load_weights(0, 0)
            for b in range(3):
                store_comb(b)
            sp.wait_ge(s_stored[0], 16 * 2)
            sp.wait_ge(s_stored[1], 16)
            load_comb(1, 0)
            load_comb(1, 1)
            store_comb(3)
            sp.wait_ge(s_stored[1], 16 * 2)

            def comb_ahead(p, blocks):
                for b in blocks:
                    sp.wait_ge(s_weighted_done, 2 * (BLOCKS * (p - 1) + b + 1))
                    load_comb(p + (b + 2) // BLOCKS, (b + 2) % BLOCKS)

            load_weights_after_split(1, 1)
            comb_ahead(1, range(BLOCKS))
            load_weights_after_split(2, 0)
            comb_ahead(2, range(BLOCKS))
            with sp.Fori(1, PAIRS // 2 - 1) as q:
                for w in (1, 0):
                    p = 2 * q + 2 - w
                    load_weights_after_split(p, w)
                    comb_ahead(p, range(BLOCKS))
            comb_ahead(PAIRS - 2, range(BLOCKS))
            comb_ahead(PAIRS - 1, range(2))
            for b in range(BLOCKS):
                sp.wait_ge(s_added, BLOCKS * (PAIRS - 1) + b + 1)
                sp.dma_start(out[:, b, :], token_store[:, b * GROUPS * D:b * GROUPS * D + KD * BT]
                             ).then_inc(s_out_done, 16)
            sp.wait_ge(s_out_done, 16 * BLOCKS)

        @block.tensor
        def _(pe):
            def three_pass(dst, terms):
                for k, (wh, wl, xh, xl, first, last) in enumerate(terms):
                    pe.matmul(dst, wl, xh, start=first, stop=False)
                    pe.matmul(dst, wh, xh, start=False, stop=False)
                    mm = pe.matmul(dst, wh, xl, start=False, stop=last)
                return mm

            def patch_project(b, chunks):
                if b >= 2 and 0 in chunks:
                    pe.wait_ge(s_h_copied, 2 * (b - 1))
                for k in chunks:
                    if b == 0:
                        pe.wait_ge(s_tokw_hi, k + 1)
                        pe.wait_ge(s_tokw_lo, k + 1)
                    pe.wait_ge(s_patch_hi, KP * b + k + 1)
                    if b == 0:
                        pe.wait_ge(s_patch_lo, k + 1)
                    elif k % 2 == 0:
                        pe.wait_ge(s_patch_lo, KP + (b - 1) * KP // 2 + k // 2 + 1)
                    else:
                        pe.wait_ge(s_patch_lo_odd, (b - 1) * KP // 2 + k // 2 + 1)
                    for m in range(KD):
                        cols = slice(k * D + m * P, k * D + (m + 1) * P)
                        mm = three_pass(bank[6 * (b % 2) + m][:, 0:BT], [
                            (tok_hi[:, cols], tok_lo[:, cols], mov_at(0, k), mov_at(1, k), k == 0, k == KP - 1)])
                    mm.then_inc(s_patch_used, 1)

            def turn_tokens(src, done):
                for g in range(GROUPS):
                    for m in range(KD):
                        mm = pe.transpose(bank[2 + g // 2][0:GT, (g % 2) * D + m * P:(g % 2) * D + (m + 1) * P],
                                          src[:, m * BT + g * GT:m * BT + (g + 1) * GT], ident[:, :])
                mm.then_inc(done, 1)

            def turn_channels(src, first_bank, done):
                for m in range(KD):
                    for g in range(GROUPS):
                        mm = pe.transpose(bank[first_bank + m][:, g * GT:(g + 1) * GT],
                                          src[0:GT, g * D + m * P:g * D + (m + 1) * P], ident[0:GT, 0:GT])
                mm.then_inc(done, 1)

            def turn_h(b):
                pe.wait_ge(s_h_copied, 2 * (b + 1))
                if b >= 1:
                    pe.wait_ge(s_res_done, b)
                turn_tokens(h_ch, s_h_turned)

            def turn_z(b):
                pe.wait_ge(s_z_done, b + 1)
                if b >= 1:
                    pe.wait_ge(s_xn_done, b)
                turn_channels(z_tok, 4, s_z_turned)

            patch_project(0, range(KP))
            pe.wait_ge(s_consts_in, 16 * 5)
            for b in range(BLOCKS - 1):
                patch_project(b + 1, range(2))
                turn_h(b)
                if b >= 1:
                    turn_z(b - 1)
                patch_project(b + 1, range(2, KP))

            def project(c, b, it, w, first=False, mats=range(MATS)):
                pe.wait_ge(s_chunk_split, 2 * (c + 1))
                pe.wait_ge(s_xn_split, b + 1)
                hi, lo = weight_parts(wbuf[w], CHUNK_COLS)
                ready = (s_k_proj, s_q_proj, s_v_proj, s_g_proj)
                for m in mats:
                    if not first:
                        pe.wait_ge((s_k_scaled, s_q_scaled, s_v_copied, s_gated)[m], it)
                    cols = [slice((m * KD + k) * P, (m * KD + k + 1) * P) for k in range(KD)]
                    three_pass(bank[m][:, 0:BT], [
                        (hi[:, cols[k]], lo[:, cols[k]], xn_at(0, k, b), xn_at(1, k, b), k == 0, k == KD - 1)
                        for k in range(KD)]).then_inc(ready[m], 1)

            def turn_values(it, first=False):
                pe.wait_ge(s_v_copied, it + 1)
                if not first:
                    pe.wait_ge(s_v_ready, it)
                for g in range(GROUPS):
                    mm = pe.transpose(bank[4][0:GT, g * P:(g + 1) * P], v_ch[:, g * GT:(g + 1) * GT], ident[:, :])
                mm.then_inc(s_v_turned, 1)

            def score(it):
                pe.wait_ge(s_k_scaled, it + 1)
                pe.wait_ge(s_q_scaled, it + 1)
                pe.wait_ge(s_masked, 2 * it + 2)
                for g in range(GROUPS):
                    dst = bank[6 + g // 2][:, (g % 2) * 2 * GT:(g % 2 + 1) * 2 * GT].rearrange(
                        "p (h t) -> p h t", h=2)
                    for j in range(len(ENDS)):
                        mm = pe.matmul(dst[0:ENDS[j], :, QOFF[j]:QOFF[j] + 2 * LENS[j]], k_dec[j][:, g, :],
                                       q_dec[:, :, g * GT + QOFF[j]:g * GT + QOFF[j] + 2 * LENS[j]],
                                       start=True, stop=True)
                    if g % 2:
                        mm.then_inc(s_scores, 1)

            def mix_values(it):
                pe.wait_ge(s_v_ready, it + 1)
                pe.wait_ge(s_og_done, it + 1)
                for g in range(GROUPS):
                    if g % 2 == 0:
                        pe.wait_ge(s_masked, 2 * it + g // 2 + 3)
                    for h in range(2):
                        mm = pe.matmul(bank[5][h * D_HEAD:(h + 1) * D_HEAD, g * GT:(g + 1) * GT],
                                       v_tok[0:GT, g, h * D_HEAD:(h + 1) * D_HEAD],
                                       probs[0:GT, (2 * g + h) * GT:(2 * g + h + 1) * GT], start=True, stop=True)
                mm.then_inc(s_pv, 1)

            def turn(q, last=False):
                for u in range(STEPS):
                    it = STEPS * q + u
                    score(it)
                    end = last and u == STEPS - 1
                    n = u + 1
                    if not end:
                        project(2 * q + n // BLOCKS, n % BLOCKS, it + 1, (n // BLOCKS) % 2)
                    mix_values(it)
                    if not end:
                        turn_values(it + 1)

            project(0, 0, 0, 0, first=True, mats=(0, 1))
            turn_h(BLOCKS - 1)
            turn_z(BLOCKS - 2)
            pe.wait_ge(s_res_done, BLOCKS)
            project(0, 0, 0, 0, first=True, mats=(2, 3))
            turn_z(BLOCKS - 1)
            pe.wait_ge(s_xn_done, BLOCKS)
            turn_values(0, first=True)
            pe.wait_ge(s_zeroed, 1)
            with pe.Fori(0, CH // 2 - 1) as q:
                turn(q)
            turn(CH // 2 - 1, last=True)

            def out_project(b, chunks=range(CH)):
                if 0 in chunks:
                    if b == 0:
                        pe.wait_ge(s_wo_split, 4)
                        pe.wait_ge(s_k_scaled, STEPS * CH // 2)
                        pe.wait_ge(s_q_scaled, STEPS * CH // 2)
                    else:
                        pe.wait_ge(s_y_copied, 2 * b)
                for k in chunks:
                    if b == 0:
                        pe.wait_ge(s_og_first, 2 * (k + 1))
                    else:
                        pe.wait_ge(s_og_hi, CH * (b - 1) + k + 1)
                        pe.wait_ge(s_og_lo, CH * (b - 1) + k + 1)
                    for m in range(KD):
                        cols = slice(k * D + m * P, k * D + (m + 1) * P)
                        mm = three_pass(bank[m][:, 0:BT], [
                            (wo_hi[:, cols], wo_lo[:, cols], mov_at(0, k), mov_at(1, k), k == 0, k == CH - 1)])
                    mm.then_inc(s_og_used, 1)

            def turn_y(b):
                pe.wait_ge(s_y_copied, 2 * (b + 1))
                if b == 0:
                    pe.wait_ge(s_v_copied, STEPS * CH // 2)
                    pe.wait_ge(s_gated, STEPS * CH // 2)
                else:
                    pe.wait_ge(s_h2_done, 2 * b)
                turn_tokens(y_ch, s_y_turned)

            def turn_h2(b):
                pe.wait_ge(s_h2_done, 2 * (b + 1))
                if b == 0:
                    pe.wait_ge(s_v_ready, STEPS * CH // 2)
                    pe.wait_ge(s_og_done, STEPS * CH // 2 + 1)
                    pe.wait_ge(s_masked, STEPS * CH + 2)
                else:
                    pe.wait_ge(s_acc_set, 2 * b)
                turn_channels(h2_tok, 4, s_h2_turned)
                pe.wait_ge(s_x3_done, b + 1)
                if b >= 1:
                    pe.wait_ge(s_exp_done, b)
                if b >= 2:
                    pe.wait_ge(s_comb_kept, b - 1)
                turn_channels(x3_tok, 6, s_x3_turned)

            def route(b):
                pe.wait_ge(s_x3_copied, 2 * (b + 1))
                for g in range(GROUPS):
                    for m in range(KD):
                        mm = pe.matmul(bank[6][0:GT, g * EXPERTS:(g + 1) * EXPERTS],
                                       x3_ch[:, m * BT + g * GT:m * BT + (g + 1) * GT],
                                       route_w[:, m * EXPERTS:(m + 1) * EXPERTS], start=m == 0, stop=m == KD - 1)
                mm.then_inc(s_logits, 1)

            def turn_comb(b):
                pe.wait_ge(s_comb_done, b + 1)
                for g in range(GROUPS):
                    mm = pe.transpose(bank[7][0:EXPERTS, g * GT:(g + 1) * GT],
                                      comb_tok[b % 2][:, g * EXPERTS:(g + 1) * EXPERTS], ident[0:GT, 0:GT])
                mm.then_inc(s_comb_turned, 1)

            out_project(0)
            turn_y(0)
            for b in range(BLOCKS - 1):
                out_project(b + 1, range(CH // 2))
                turn_h2(b)
                out_project(b + 1, range(CH // 2, CH))
                route(b)
                if b >= 1:
                    turn_comb(b - 1)
                turn_y(b + 1)

            def expert_up(p, b, n, w, first=False):
                if isinstance(p, int) and p == 0:
                    pe.wait_ge(s_pair0_split, 2)
                else:
                    pe.wait_ge(s_wsplit_hi, 3 * p)
                    pe.wait_ge(s_wsplit_lo, 3 * p)
                pe.wait_ge(s_x3_hi, 2 * (b + 1))
                pe.wait_ge(s_x3_lo, b + 1)
                hi, lo = weight_parts(wbuf[w], PAIR_COLS)
                for e in range(2):
                    for gu, (ready, free) in enumerate(((s_g_ready, s_silu_done), (s_u_ready, s_hidden_done))):
                        if not first:
                            pe.wait_ge(free, 2 * n - 1 + e)
                        cols = [slice(e * 3 * D + k * D + gu * P, e * 3 * D + k * D + gu * P + P) for k in range(KD)]
                        three_pass(bank[2 * e + gu][:, 0:BT], [
                            (hi[:, cols[k]], lo[:, cols[k]], xn_at(0, k, b), xn_at(1, k, b), k == 0, k == KD - 1)
                            for k in range(KD)]).then_inc(ready, 1)

            def expert_down(b, n, w, early=False):
                hi, lo = weight_parts(wbuf[w], PAIR_COLS)
                if not early:
                    pe.wait_ge(s_added, n - 1)
                for e in range(2):
                    pe.wait_ge(s_hid_hi, 2 * n + e + 1)
                    pe.wait_ge(s_hid_lo, 2 * n + e + 1)
                    x_hi, x_lo = mov_at(b % 2, 2 * e), mov_at(b % 2, 2 * e + 1)
                    for m in range(KD):
                        cols = slice(e * 3 * D + KD * D + m * P, e * 3 * D + KD * D + (m + 1) * P)
                        mm = three_pass(bank[4 + 2 * (b % 2) + m][:, 0:BT],
                                        [(hi[:, cols], lo[:, cols], x_hi, x_lo, e == 0, e == 1)])
                mm.then_inc(s_y_ready, 1)

            def pair_steps(p, w, last=False):
                for b in range(BLOCKS):
                    n = BLOCKS * p + b
                    if b < BLOCKS - 1:
                        expert_up(p, b + 1, n + 1, w)
                    elif not last:
                        expert_up(p + 1, 0, n + 1, 1 - w)
                    expert_down(b, n, w)

            pe.wait_ge(s_y_copied, 2 * BLOCKS)
            pe.wait_ge(s_h2_done, 2 * BLOCKS)
            expert_up(0, 0, 0, 0, first=True)
            turn_h2(BLOCKS - 1)
            expert_up(0, 1, 1, 0)
            route(BLOCKS - 1)
            pe.wait_ge(s_acc_set, 2 * BLOCKS)
            expert_down(0, 0, 0, early=True)
            expert_up(0, 2, 2, 0)
            turn_comb(BLOCKS - 2)
            pe.wait_ge(s_exp_done, BLOCKS)
            pe.wait_ge(s_comb_kept, BLOCKS - 1)
            expert_down(1, 1, 0, early=True)
            expert_up(0, 3, 3, 0)
            expert_down(2, 2, 0)
            expert_up(1, 0, BLOCKS, 1)
            pe.wait_ge(s_added, 2)
            turn_comb(BLOCKS - 1)
            pe.wait_ge(s_comb_kept, BLOCKS)
            expert_down(3, 3, 0)
            with pe.Fori(0, PAIRS // 2 - 1) as q:
                pair_steps(2 * q + 1, 1)
                pair_steps(2 * q + 2, 0)
            pair_steps(PAIRS - 2, 1)
            pair_steps(PAIRS - 1, 0, last=True)

        @block.vector
        def _(dve):
            def split_patches(b, chunks):
                for k in chunks:
                    dve.wait_ge(s_patch_hi, KP * b + k + 1)
                    dve.tensor_tensor(mov_at(1, k), patch_raw[b % 2][:, k * BT:(k + 1) * BT],
                                      mov_at(0, k).bitcast(F32), ALU.subtract).then_inc(s_patch_lo, 1)

            split_patches(0, range(KP))

            dve.memset(gate, 0.0).then_inc(s_og_done, 1)
            dve.memset(q_dec[:, :, :], 0.0).then_inc(s_zeroed, 1)

            dve.wait_ge(s_decay_e, 1)
            n = [0]

            def power(ins):
                n[0] += 1
                ins.then_inc(s_pw_step, 1)

            def powers_done():
                dve.wait_ge(s_pw_step, n[0])

            e_neg, alpha = decay[:, 0:CH], decay[:, CH:2 * CH]
            power(dve.tensor_scalar(e_neg, e_neg, 1.0, None, ALU.add))
            powers_done()
            power(dve.reciprocal(alpha, e_neg))
            powers_done()
            power(dve.tensor_scalar(pw[:, :, HALF + 1], alpha, MIN_DECAY, None, ALU.max))
            power(dve.tensor_scalar(rw[:, :, SEQ - 2], alpha, MIN_DECAY, None, ALU.max))
            power(dve.memset(pw[:, :, HALF:HALF + 1], 1.0))
            power(dve.memset(rw[:, :, SEQ - 1:SEQ], 1.0))
            k = 1
            while k < SEQ - 1:
                m = min(k, SEQ - 1 - k)
                powers_done()
                power(dve.tensor_tensor(pw[:, :, HALF + k + 1:HALF + k + 1 + m], pw[:, :, HALF + 1:HALF + 1 + m],
                                        pw[:, :, HALF + k:HALF + k + 1].broadcast_to([P, CH, m]), ALU.mult))
                e = SEQ - 1
                power(dve.tensor_tensor(rw[:, :, e - k - m:e - k], rw[:, :, e - m:e],
                                        rw[:, :, e - k:e - k + 1].broadcast_to([P, CH, m]), ALU.mult))
                k *= 2
            powers_done()
            power(dve.reciprocal(pw[:, :, 0:HALF], rw[:, :, SEQ - 1 - HALF:SEQ - 1]))
            power(dve.reciprocal(rw[:, :, SEQ:SEQ + HALF], pw[:, :, HALF + 1:2 * HALF + 1]))
            powers_done()
            tq = tab_q[:, :].rearrange("p (c t) -> p c t", c=CH)
            tk = tab_k[:, :].rearrange("p (c t) -> p c t", c=CH)

            def tables(j):
                s0, ln = STARTS[j], LENS[j]

                def images(t, at, n):
                    return t[:, :, at:at + 2 * n].rearrange("p c (i t) -> p c i t", i=2)

                def powers(t, at, n):
                    return t[:, :, at:at + n].rearrange("p c (o t) -> p c o t", o=1).broadcast_to([P, CH, 2, n])

                ins = dve.tensor_copy(images(tq, QOFF[j], ln), powers(pw, 0, ln))
                for s1, l1, o1 in list(zip(STARTS, LENS, QOFF))[:j + 1]:
                    ins = dve.tensor_copy(images(tk, KOFF[j] + o1, l1), powers(rw, SEQ - 1 - HALF - s0 + s1, l1))
                ins.then_inc(s_tables, 1)

            def two_banks(first, g):
                return bank[first + g // 2][0:GT, (g % 2) * D:(g % 2 + 1) * D]

            split_patches(1, range(0, KP, 2))
            for b in range(BLOCKS):
                dve.wait_ge(s_h_turned, b + 1)
                for g in range(GROUPS):
                    ins = dve.bn_stats(stat[:, g, :], two_banks(2, g))
                ins.then_inc(s_stats, 1)
                dve.wait_ge(s_stats, b + 1)
                for g in range(GROUPS):
                    ins = dve.bn_aggr(mv[:, g, :], stat[:, g, :])
                ins.then_inc(s_agg, 1)
                dve.wait_ge(s_agg, b + 1)
                dve.tensor_scalar(ve, mv[:, :, 1], EPS, None, ALU.add).then_inc(s_veps, 1)
                dve.wait_ge(s_std, b + 1)
                dve.reciprocal(rstd, sd).then_inc(s_rstd, 1)
                dve.wait_ge(s_rstd, 3 * b + 1)
                for g in range(GROUPS):
                    ins = dve.tensor_scalar(x2_tok[0:GT, g * D:(g + 1) * D], two_banks(2, g), mv[:, g, 0:1],
                                            rstd[:, g:g + 1], ALU.subtract, ALU.mult)
                ins.then_inc(s_x2_done, 1)
                dve.tensor_tensor(r2, rstd, rstd, ALU.mult).then_inc(s_rstd, 1)
                dve.wait_ge(s_rstd, 3 * b + 2)
                dve.tensor_tensor(r2, r2, mv[:, :, 1], ALU.mult).then_inc(s_rstd, 1)
                dve.wait_ge(s_rstd, 3 * b + 3)
                dve.tensor_scalar(ve2, r2, EPS, None, ALU.add).then_inc(s_v2, 1)
                dve.wait_ge(s_x2_done, b + 1)
                for g in range(GROUPS):
                    ins = dve.tensor_tensor(res(b)[:, g * D:(g + 1) * D], two_banks(2, g),
                                            x2_tok[0:GT, g * D:(g + 1) * D], ALU.add)
                ins.then_inc(s_res_done, 1)
                dve.wait_ge(s_std2, b + 1)
                dve.reciprocal(zsc, sd2).then_inc(s_zscale, 1)
                dve.wait_ge(s_zscale, b + 1)
                if b >= 1:
                    dve.wait_ge(s_z_turned, b)
                for g in range(GROUPS):
                    ins = dve.tensor_scalar(z_tok[0:GT, g * D:(g + 1) * D], x2_tok[0:GT, g * D:(g + 1) * D],
                                            zsc[:, g:g + 1], None, ALU.mult)
                ins.then_inc(s_z_done, 1)
                if b + 2 < BLOCKS:
                    split_patches(b + 2, range(0, KP, 2))
                for j in ((0, 1), (2,), (3, 4), (5,))[b]:
                    tables(j)

            dve.wait_ge(s_h_copied, 2 * BLOCKS)
            dve.memset(bank[6][:, :], 0.0).then_inc(s_masked, 1)
            dve.memset(bank[7][:, :], 0.0).then_inc(s_masked, 1)

            biases = par[:, PB + 2 * CH:PB + 4 * CH].rearrange("p (m c) -> p m c", m=2)

            def fetch_biases(c, w):
                dve.tensor_scalar(bias_now[w].rearrange("p (m o) -> p m o", o=1), biases[:, :, bass.ds(c, 1)],
                                  1.0, None, ALU.mult).then_inc(s_bias_ready, 1)

            def scale_keys(c, it):
                dve.wait_ge(s_k_proj, it + 1)
                src = bank[0][:, 0:BT].rearrange("p (g t) -> p g t", g=GROUPS)
                for j in range(len(ENDS)):
                    table = tab_k[:, bass.ds(c * KCOLS + KOFF[j], ENDS[j])]
                    ins = dve.scalar_tensor_tensor(
                        out=k_dec[j], in0=src[:, :, 0:ENDS[j]], scalar=par[:, bass.ds(PB + c, 1)],
                        in1=table.rearrange("p (o t) -> p o t", o=1).broadcast_to([P, GROUPS, ENDS[j]]),
                        op0=ALU.add, op1=ALU.mult)
                ins.then_inc(s_k_scaled, 1)

            def scale_queries(c, it):
                dve.wait_ge(s_q_proj, it + 1)
                for h in range(2):
                    rows = slice(h * D_HEAD, (h + 1) * D_HEAD)
                    ins = dve.scalar_tensor_tensor(
                        out=q_dec[rows, h, :].rearrange("p (g t) -> p g t", g=GROUPS),
                        in0=bank[1][rows, 0:BT].rearrange("p (g t) -> p g t", g=GROUPS),
                        scalar=par[rows, bass.ds(PB + CH + c, 1)],
                        in1=tab_q[rows, bass.ds(c * GT, GT)].rearrange("p (o t) -> p o t", o=1).broadcast_to(
                            [D_HEAD, GROUPS, GT]), op0=ALU.add, op1=ALU.mult)
                ins.then_inc(s_q_scaled, 1)

            def mask_scores(it):
                for k in range(2):
                    dve.wait_ge(s_scores, 2 * it + k + 1)
                    dve.tensor_tensor(
                        probs[0:GT, k * BT:(k + 1) * BT].rearrange("p (n t) -> p n t", n=4),
                        bank[6 + k][0:GT, 0:BT].rearrange("p (n t) -> p n t", n=4),
                        causal[0:GT, :].rearrange("p (o t) -> p o t", o=1).broadcast_to([GT, 4, GT]),
                        ALU.mult).then_inc(s_masked, 1)

            def gate_heads(c, b, it):
                dve.wait_ge(s_pv, it + 1)
                dve.wait_ge(s_gated, it + 1)
                dve.tensor_tensor(og_at(c, b), bank[5][:, 0:BT], gate, ALU.mult).then_inc(s_og_done, 1)

            def turn(q, last=False):
                for u in range(STEPS):
                    it = STEPS * q + u
                    mask_scores(it)
                    if not (last and u == STEPS - 1):
                        c = 2 * q + (u + 1) // BLOCKS
                        scale_keys(c, it + 1)
                        scale_queries(c, it + 1)
                    gate_heads(2 * q + u // BLOCKS, u % BLOCKS, it)
                    w = u // BLOCKS
                    if u % BLOCKS == 0 and not (last and w == 1):
                        fetch_biases(2 * q + w + 1, 1 - w)

            dve.wait_ge(s_tables, len(STARTS))
            fetch_biases(0, 0)
            scale_keys(0, 0)
            scale_queries(0, 0)
            with dve.Fori(0, CH // 2 - 1) as q:
                turn(q)
            turn(CH // 2 - 1, last=True)

            rs = [0]

            def r_op(ins):
                rs[0] += 1
                ins.then_inc(s_r_step, 1)
                dve.wait_ge(s_r_step, rs[0])

            def router(b):
                score3 = r_score.rearrange("p (g e) -> p g e", g=GROUPS)
                choice3 = r_choice.rearrange("p (g e) -> p g e", g=GROUPS)
                dve.wait_ge(s_exp_done, b + 1)
                r_op(dve.tensor_scalar(r_a, r_exp[b % 2], 1.0, None, ALU.add))
                r_op(dve.reciprocal(r_score, r_a))
                r_op(dve.tensor_tensor(choice3, score3, route_b[0:GT, :].rearrange("p (o e) -> p o e", o=1)
                                       .broadcast_to([GT, GROUPS, EXPERTS]), ALU.add))
                quad = r_choice.rearrange("p (n a) -> p n a", a=4)
                mx = r_max.rearrange("p (n a) -> p n a", a=2)
                mn = r_min.rearrange("p (n a) -> p n a", a=2)
                r_op(dve.tensor_tensor(mx, quad[:, :, 0:4:2], quad[:, :, 1:4:2], ALU.max))
                r_op(dve.tensor_tensor(mn, quad[:, :, 0:4:2], quad[:, :, 1:4:2], ALU.min))
                r_op(dve.tensor_tensor(r_gs, mx[:, :, 0], mx[:, :, 1], ALU.max))
                r_op(dve.tensor_tensor(r_t0, mx[:, :, 0], mx[:, :, 1], ALU.min))
                r_op(dve.tensor_tensor(r_t1, mn[:, :, 0], mn[:, :, 1], ALU.max))
                r_op(dve.tensor_tensor(r_t0, r_t0, r_t1, ALU.max))
                r_op(dve.tensor_tensor(r_gs, r_gs, r_t0, ALU.add))
                mine = r_gs.rearrange("p (n o) -> p n o", o=1).broadcast_to([GT, GG, ROUTE_GROUPS])
                c1, c2 = (c.rearrange("p (n j) -> p n j", j=ROUTE_GROUPS) for c in (cmp1, cmp2))
                for g in range(GROUPS):
                    n0 = g * ROUTE_GROUPS
                    theirs = r_gs[:, n0:n0 + ROUTE_GROUPS].rearrange("p (o j) -> p o j", o=1).broadcast_to(
                        [GT, ROUTE_GROUPS, ROUTE_GROUPS])
                    dve.tensor_tensor(c1[:, n0:n0 + ROUTE_GROUPS, :], theirs, mine[:, n0:n0 + ROUTE_GROUPS, :],
                                      ALU.is_gt)
                    ins = dve.tensor_tensor(c2[:, n0:n0 + ROUTE_GROUPS, :], theirs,
                                            mine[:, n0:n0 + ROUTE_GROUPS, :], ALU.is_equal)
                r_op(ins)
                r_op(dve.tensor_tensor(cmp2.rearrange("p (g n) -> p g n", g=GROUPS),
                                       cmp2.rearrange("p (g n) -> p g n", g=GROUPS),
                                       before[0:GT, :].rearrange("p (o n) -> p o n", o=1).broadcast_to(
                                           [GT, GROUPS, ROUTE_GROUPS * ROUTE_GROUPS]), ALU.mult))
                r_op(dve.tensor_tensor(cmp1, cmp1, cmp2, ALU.add))
                r_op(dve.tensor_reduce(r_sel, c1, AX.X, ALU.add))
                r_op(dve.tensor_scalar(r_sel, r_sel, TOP_GROUPS - 0.5, None, ALU.is_lt))
                r_op(dve.tensor_tensor(quad, quad, r_sel.rearrange("p (n o) -> p n o", o=1).broadcast_to(
                    [GT, GG, 4]), ALU.mult))
                r_op(dve.tensor_scalar(r_b, r_choice, 0.0, None, ALU.add))
                for g in range(GROUPS):
                    ins = dve.max(r_top[:, g * 8:(g + 1) * 8], r_b[:, g * EXPERTS:(g + 1) * EXPERTS])
                r_op(ins)
                for g in range(GROUPS):
                    ins = dve.match_replace(r_c[:, g * EXPERTS:(g + 1) * EXPERTS], r_top[:, g * 8:(g + 1) * 8],
                                            r_b[:, g * EXPERTS:(g + 1) * EXPERTS], -3e38)
                r_op(ins)
                r_op(dve.tensor_tensor(r_c, r_c, r_b, ALU.not_equal))
                r_op(dve.tensor_tensor(r_a, r_c, r_score, ALU.mult))
                r_op(dve.tensor_reduce(r_sum, r_a.rearrange("p (g e) -> p g e", g=GROUPS), AX.X, ALU.add))
                r_op(dve.tensor_scalar(r_sum, r_sum, 1e-20, None, ALU.add))
                r_op(dve.reciprocal(r_inv, r_sum))
                if b >= 2:
                    dve.wait_ge(s_comb_turned, b - 1)
                for g in range(GROUPS):
                    ins = dve.tensor_scalar(comb_tok[b % 2][:, g * EXPERTS:(g + 1) * EXPERTS],
                                            r_a[:, g * EXPERTS:(g + 1) * EXPERTS], r_inv[:, g:g + 1], ROUTE_SCALE,
                                            ALU.mult, ALU.mult)
                ins.then_inc(s_comb_done, 1)

            def norm(b):
                dve.wait_ge(s_y_turned, b + 1)
                for k in range(2):
                    ins = dve.tensor_tensor(h2_tok[0:GT, k * 2 * D:(k + 1) * 2 * D], bank[2 + k][0:GT, :],
                                            res(b)[:, k * 2 * D:(k + 1) * 2 * D], ALU.add)
                    ins.then_inc(s_h2_done, 1)
                dve.wait_ge(s_h2_done, 2 * (b + 1))
                for g in range(GROUPS):
                    ins = dve.bn_stats(stat[:, g, :], h2_tok[0:GT, g * D:(g + 1) * D])
                ins.then_inc(s_stats2, 1)
                dve.wait_ge(s_stats2, b + 1)
                for g in range(GROUPS):
                    ins = dve.bn_aggr(mv[:, g, :], stat[:, g, :])
                ins.then_inc(s_agg2, 1)
                dve.wait_ge(s_agg2, b + 1)
                dve.tensor_scalar(ve, mv[:, :, 1], EPS, None, ALU.add).then_inc(s_veps2, 1)
                dve.wait_ge(s_std3, b + 1)
                dve.reciprocal(rstd_n, sd).then_inc(s_rstd2, 1)
                dve.wait_ge(s_rstd2, b + 1)
                for g in range(GROUPS):
                    ins = dve.tensor_scalar(x3_tok[0:GT, g * D:(g + 1) * D], h2_tok[0:GT, g * D:(g + 1) * D],
                                            mv[:, g, 0:1], rstd_n[:, g:g + 1], ALU.subtract, ALU.mult)
                ins.then_inc(s_x3_done, 1)

            norm(0)
            norm(1)
            router(0)
            norm(2)
            router(1)
            norm(3)

            def hidden_units(b, n, shared=False, first=False):
                for e in range(2):
                    dve.wait_ge(s_u_ready, 2 * n + e + 1)
                    if shared:
                        dve.wait_ge(s_silu_done, 2 * n + e + 1)
                    else:
                        dve.wait_ge(s_weighted_done, 2 * (n - BLOCKS) + e + 1)
                    if not first:
                        dve.wait_ge(s_hid_lo, 2 * n - 1 + e)
                    dve.tensor_tensor(hidden[e], bank[2 * e + 1][:, 0:BT], silu_g[e] if shared else weighted[e],
                                      ALU.mult).then_inc(s_hidden_done, 1)
                for e in range(2):
                    dve.wait_ge(s_hid_hi, 2 * n + e + 1)
                    dve.tensor_tensor(mov_at(b % 2, 2 * e + 1), hidden[e], mov_at(b % 2, 2 * e).bitcast(F32),
                                      ALU.subtract).then_inc(s_hid_lo, 1)

            def split_third(p, b, w):
                cols = slice(b * 2 * D, (b + 1) * 2 * D)
                hi, lo = weight_parts(wbuf[1 - w], PAIR_COLS)
                dve.wait_ge(s_wsplit_hi, 3 * p + b + 1)
                dve.tensor_tensor(lo[:, cols], raw[:, (1 - w) * PAIR_COLS:(2 - w) * PAIR_COLS][:, cols],
                                  hi[:, cols].bitcast(F32), ALU.subtract).then_inc(s_wsplit_lo, 1)

            def add_down(b, n, again=True):
                dve.wait_ge(s_y_ready, n + 1)
                if again:
                    dve.wait_ge(s_added, n - BLOCKS + 1)
                for m in range(KD):
                    ins = dve.tensor_tensor(acc(b, m), bank[4 + 2 * (b % 2) + m][:, 0:BT], acc(b, m), ALU.add)
                ins.then_inc(s_added, 1)

            hidden_units(0, 0, shared=True, first=True)
            split_third(0, 0, 0)
            router(2)
            hidden_units(1, 1, shared=True)
            split_third(0, 1, 0)
            dve.wait_ge(s_acc_set, 2 * BLOCKS)
            add_down(0, 0, again=False)
            hidden_units(2, 2, shared=True)
            split_third(0, 2, 0)
            add_down(1, 1, again=False)
            router(3)
            hidden_units(3, 3, shared=True)
            add_down(2, 2, again=False)

            def pair(p, w, last=False, after_shared=False):
                for b in range(BLOCKS):
                    n = BLOCKS * p + b
                    hidden_units(b, n)
                    if b < 3 and not last:
                        split_third(p, b, w)
                    add_down((b - 1) % BLOCKS, n - 1, again=not (after_shared and b == 0))

            pair(1, 1, after_shared=True)
            pair(2, 0)
            with dve.Fori(1, PAIRS // 2 - 1) as q:
                pair(2 * q + 1, 1)
                pair(2 * q + 2, 0)
            pair(PAIRS - 2, 1)
            pair(PAIRS - 1, 0, last=True)
            add_down(BLOCKS - 1, BLOCKS * PAIRS - 1)

        @block.scalar
        def _(act):
            for i in range(KP // 2):
                cols = slice(2 * i * D, 2 * (i + 1) * D)
                act.dma_start(tok_raw[:, cols], w_tok[:, cols]).then_inc(s_tokw_in[i], 16)

            def split_patch(b, k):
                act.wait_ge(s_patch_in[b % 2][k // 2], 16 * (b // 2 + 1))
                if b >= 1:
                    act.wait_ge(s_patch_used, KP * (b - 1) + k + 1)
                act.activation(mov_at(0, k), patch_raw[b % 2][:, k * BT:(k + 1) * BT],
                               ACT.Copy).then_inc(s_patch_hi, 1)

            for k in range(KP):
                act.wait_ge(s_tokw_in[k // 2], 16)
                act.activation(tok_hi[:, k * D:(k + 1) * D], tok_raw[:, k * D:(k + 1) * D],
                               ACT.Copy).then_inc(s_tokw_hi, 1)
                split_patch(0, k)
            act.wait_ge(s_params_in, 16)
            act.activation(decay[:, 0:CH], par[:, PLOGIT:PLOGIT + CH], ACT.Exp, scale=-1.0).then_inc(s_decay_e, 1)

            def copy_h(b):
                for m in range(KD):
                    act.wait_ge(s_patch_used, KP * (b + 1))
                    if b >= 1 and m == 0:
                        act.wait_ge(s_h_turned, b)
                    act.activation(h_ch[:, m * BT:(m + 1) * BT], bank[6 * (b % 2) + m][:, 0:BT], ACT.Identity,
                                   bias=par[:, PTOKB + m:PTOKB + m + 1]).then_inc(s_h_copied, 1)

            def roots(b):
                act.wait_ge(s_veps, b + 1)
                act.activation(sd, ve, ACT.Sqrt).then_inc(s_std, 1)
                act.wait_ge(s_v2, b + 1)
                act.activation(sd2, ve2, ACT.Sqrt).then_inc(s_std2, 1)

            def affine(b):
                act.wait_ge(s_z_turned, b + 1)
                if b >= 1:
                    act.wait_ge(s_xn_split, b)
                for m in range(KD):
                    gamma, beta = par[:, PGAMMA + m:PGAMMA + m + 1], par[:, PBETA + m:PBETA + m + 1]
                    act.activation(xn_ch[:, m * BT:(m + 1) * BT], bank[4 + m][:, 0:BT], ACT.Identity,
                                   bias=beta, scale=gamma)
                    ins = act.activation(xn_at(0, m, b), bank[4 + m][:, 0:BT], ACT.Identity,
                                         bias=beta, scale=gamma)
                ins.then_inc(s_xn_done, 1)

            copy_h(0)
            for k in range(KP):
                split_patch(1, k)
            for b in range(BLOCKS):
                roots(b)
                if b + 1 < BLOCKS:
                    copy_h(b + 1)
                if b + 2 < BLOCKS:
                    for k in range(KP):
                        split_patch(b + 2, k)
                if b >= 1:
                    affine(b - 1)
            affine(BLOCKS - 1)

            def step(c, it, w):
                act.wait_ge(s_v_proj, it + 1)
                act.wait_ge(s_bias_ready, c + 1)
                act.activation(v_ch, bank[2][:, 0:BT], ACT.Identity,
                               bias=bias_now[w][:, 0:1]).then_inc(s_v_copied, 1)
                act.wait_ge(s_v_turned, it + 1)
                act.activation(v_tok[0:GT, :, :].rearrange("p g c -> p (g c)"), bank[4][0:GT, :],
                               ACT.Copy).then_inc(s_v_ready, 1)
                act.wait_ge(s_g_proj, it + 1)
                act.wait_ge(s_og_done, it + 1)
                act.activation(gate, bank[3][:, 0:BT], ACT.Silu,
                               bias=bias_now[w][:, 1:2]).then_inc(s_gated, 1)

            with act.Fori(0, CH // 2) as q:
                for u in range(STEPS):
                    step(2 * q + u // BLOCKS, STEPS * q + u, u // BLOCKS)

            def split_heads(b):
                for k in range(CH):
                    act.wait_ge(s_og_used, CH * (b - 1) + k + 1)
                    act.wait_ge(s_og_done, STEPS * CH // 2 + 1)
                    act.activation(mov_at(0, k), og[:, k * TOKENS + b * BT:k * TOKENS + (b + 1) * BT],
                                   ACT.Copy).then_inc(s_og_hi, 1)

            def keep_comb(b):
                act.wait_ge(s_comb_turned, b + 1)
                if b >= 2:
                    act.wait_ge(s_stored[b % 2], 16)
                act.activation(comb_sb[b % 2], bank[7][0:EXPERTS, 0:BT], ACT.Copy).then_inc(s_comb_kept, 1)

            def copy_y(b):
                act.wait_ge(s_og_used, CH * (b + 1))
                if b >= 1:
                    act.wait_ge(s_y_turned, b)
                for m in range(KD):
                    act.activation(y_ch[:, m * BT:(m + 1) * BT], bank[m][:, 0:BT], ACT.Identity,
                                   bias=par[:, PBO + m:PBO + m + 1]).then_inc(s_y_copied, 1)

            def root(b):
                act.wait_ge(s_veps2, b + 1)
                act.activation(sd, ve, ACT.Sqrt).then_inc(s_std3, 1)

            def copy_h2_x3(b):
                act.wait_ge(s_h2_turned, b + 1)
                for m in range(KD):
                    act.activation(acc(b, m), bank[4 + m][:, 0:BT], ACT.Copy).then_inc(s_acc_set, 1)
                act.wait_ge(s_x3_turned, b + 1)
                if b >= 1:
                    act.wait_ge(s_x3_lo, b)
                    act.wait_ge(s_logits, b)
                for m in range(KD):
                    act.activation(xn_at(0, m, b), bank[6 + m][:, 0:BT], ACT.Copy).then_inc(s_x3_hi, 1)
                    act.activation(x3_ch[:, m * BT:(m + 1) * BT], bank[6 + m][:, 0:BT], ACT.Copy).then_inc(
                        s_x3_copied, 1)

            def route_exp(b):
                act.wait_ge(s_logits, b + 1)
                if b >= 2:
                    act.wait_ge(s_comb_done, b - 1)
                act.activation(r_exp[b % 2], bank[6][0:GT, 0:GE], ACT.Exp, scale=-1.0).then_inc(s_exp_done, 1)

            copy_y(0)
            for b in range(BLOCKS - 1):
                root(b)
                split_heads(b + 1)
                copy_h2_x3(b)
                copy_y(b + 1)
                route_exp(b)
                if b >= 1:
                    keep_comb(b - 1)
            root(BLOCKS - 1)

            def silu_gates(n, first=False):
                for e in range(2):
                    act.wait_ge(s_g_ready, 2 * n + e + 1)
                    if not first:
                        act.wait_ge(s_hidden_done, 2 * n - 1 + e)
                    act.activation(silu_g[e], bank[2 * e][:, 0:BT], ACT.Silu).then_inc(s_silu_done, 1)

            def high_parts(b, n):
                for e in range(2):
                    act.wait_ge(s_hidden_done, 2 * n + e + 1)
                    act.activation(mov_at(b % 2, 2 * e), hidden[e], ACT.Copy).then_inc(s_hid_hi, 1)

            def split_third(p, b, w, first=False):
                if b == 0:
                    if w == 0:
                        act.wait_ge(s_pair_in[1], 8 * p + 16)
                    else:
                        act.wait_ge(s_pair_in[0], 8 * p + 24)
                    if not first:
                        act.wait_ge(s_y_ready, BLOCKS * p)
                cols = slice(b * 2 * D, (b + 1) * 2 * D)
                hi, lo = weight_parts(wbuf[1 - w], PAIR_COLS)
                act.activation(hi[:, cols], raw[:, (1 - w) * PAIR_COLS:(2 - w) * PAIR_COLS][:, cols],
                               ACT.Copy).then_inc(s_wsplit_hi, 1)

            silu_gates(0, first=True)
            high_parts(0, 0)
            split_third(0, 0, 0, first=True)
            copy_h2_x3(BLOCKS - 1)
            silu_gates(1)
            route_exp(BLOCKS - 1)
            high_parts(1, 1)
            split_third(0, 1, 0)
            silu_gates(2)
            keep_comb(BLOCKS - 2)
            high_parts(2, 2)
            split_third(0, 2, 0)
            silu_gates(3)
            high_parts(3, 3)

            def pair(p, w, last=False, comb_left=False):
                for b in range(BLOCKS):
                    n = BLOCKS * p + b
                    silu_gates(n)
                    if b == 0 and comb_left:
                        keep_comb(BLOCKS - 1)
                    high_parts(b, n)
                    if b < 3 and not last:
                        split_third(p, b, w)

            pair(1, 1, comb_left=True)
            pair(2, 0)
            with act.Fori(1, PAIRS // 2 - 1) as q:
                pair(2 * q + 1, 1)
                pair(2 * q + 2, 0)
            pair(PAIRS - 2, 1)
            pair(PAIRS - 1, 0, last=True)

        @block.gpsimd
        def _(pool):
            def split_chunk(w, cols):
                hi, lo = weight_parts(wbuf[w], cols)
                src = raw[:, w * cols:(w + 1) * cols]
                return hi, lo, src

            def split_weights(hi, lo, src, done, count):
                pool.tensor_copy(hi, src).then_inc(done, 1)
                pool.wait_ge(done, count + 1)
                pool.tensor_tensor(lo, src, hi.bitcast(F32), ALU.subtract).then_inc(done, 1)

            for k in range(KP):
                pool.wait_ge(s_tokw_hi, k + 1)
                pool.tensor_tensor(tok_lo[:, k * D:(k + 1) * D], tok_raw[:, k * D:(k + 1) * D],
                                   tok_hi[:, k * D:(k + 1) * D].bitcast(F32), ALU.subtract).then_inc(s_tokw_lo, 1)

            xparts = [t[:, :].rearrange("p (k t) -> p k t", k=KD) for t in xn]

            def split_patches(b):
                for k in range(1, KP, 2):
                    pool.wait_ge(s_patch_hi, KP * b + k + 1)
                    pool.tensor_tensor(mov_at(1, k), patch_raw[b % 2][:, k * BT:(k + 1) * BT],
                                       mov_at(0, k).bitcast(F32), ALU.subtract).then_inc(s_patch_lo_odd, 1)

            def low_part(b, src, done):
                pool.tensor_tensor(xparts[1][:, :, b * BT:(b + 1) * BT], src.rearrange("p (k t) -> p k t", k=KD),
                                   xparts[0][:, :, b * BT:(b + 1) * BT].bitcast(F32),
                                   ALU.subtract).then_inc(done, 1)

            split_patches(1)
            for b in range(BLOCKS):
                if b == 1:
                    pool.wait_ge(s_chunk_in[0], 16)
                    split_weights(*split_chunk(0, CHUNK_COLS), s_chunk_split, 0)
                if b + 2 < BLOCKS:
                    split_patches(b + 2)
                pool.wait_ge(s_xn_done, b + 1)
                low_part(b, xn_ch, s_xn_split)
            pool.wait_ge(s_chunk_in[1], 16)
            split_weights(*split_chunk(1, CHUNK_COLS), s_chunk_split, 2)

            def first_heads(k):
                pool.wait_ge(s_og_done, BLOCKS * k + 2)
                src = og[:, k * TOKENS:k * TOKENS + BT]
                pool.tensor_copy(mov_at(0, k), src).then_inc(s_og_first, 1)
                pool.wait_ge(s_og_first, 2 * k + 1)
                pool.tensor_tensor(mov_at(1, k), src, mov_at(0, k).bitcast(F32), ALU.subtract).then_inc(
                    s_og_first, 1)

            for c in range(2, CH):
                pool.wait_ge(s_chunk_in[c % 2], 16 * (c // 2 + 1))
                pool.wait_ge(s_g_proj, BLOCKS * (c - 1))
                split_weights(*split_chunk(c % 2, CHUNK_COLS), s_chunk_split, 2 * c)
                first_heads(c - 2)
            half = CH * D // 2
            for i in range(2):
                pool.wait_ge(s_wo_in, 16 * (i + 1))
                split_weights(wo_hi[:, i * half:(i + 1) * half], wo_lo[:, i * half:(i + 1) * half],
                              raw[:, 2 * CHUNK_COLS:3 * CHUNK_COLS], s_wo_split, 2 * i)
            first_heads(CH - 2)
            first_heads(CH - 1)
            pool.wait_ge(s_pair_in[0], 16)
            pool.wait_ge(s_g_proj, STEPS * CH // 2)
            split_weights(*split_chunk(0, PAIR_COLS), s_pair0_split, 0)

            def split_heads(b, chunks):
                for k in chunks:
                    pool.wait_ge(s_og_hi, CH * (b - 1) + k + 1)
                    pool.tensor_tensor(mov_at(1, k), og[:, k * TOKENS + b * BT:k * TOKENS + (b + 1) * BT],
                                       mov_at(0, k).bitcast(F32), ALU.subtract).then_inc(s_og_lo, 1)

            for b in range(BLOCKS):
                if b + 1 < BLOCKS:
                    split_heads(b + 1, range(CH))
                pool.wait_ge(s_x3_hi, 2 * (b + 1))
                pool.wait_ge(s_x3_copied, 2 * (b + 1))
                low_part(b, x3_ch, s_x3_lo)

            with pool.Fori(1, PAIRS) as p:
                for b in range(BLOCKS):
                    n = BLOCKS * p + b
                    pool.wait_ge(s_comb_in[b % 2], 64 * (p - 1) + 32 * (b // 2 + 1))
                    for e in range(2):
                        pool.wait_ge(s_silu_done, 2 * n + e + 1)
                        pool.wait_ge(s_hidden_done, 2 * n - 1 + e)
                        pool.tensor_tensor(weighted[e], silu_g[e], comb[b % 2][:, e * BT:(e + 1) * BT],
                                           ALU.mult).then_inc(s_weighted_done, 1)


def _token_order():
    import numpy as np
    order = []
    for g in range(IMAGES // 2):
        for s0, ln in zip(STARTS, LENS):
            for i in range(2):
                order += [(2 * g + i) * SEQ + s0 + t for t in range(ln)]
    return np.array(order)


def kernel(**inputs):
    import numpy as np
    import concourse.bacc as _bacc
    from concourse import mybir as _mybir
    from concourse.bass_utils import run_bass_kernel_spmd as _run

    a = {k: np.asarray(v) for k, v in inputs.items()}
    f = np.ascontiguousarray
    order = _token_order()

    def chunked(w):
        return w.reshape(-1, P, w.shape[-1]).transpose(1, 0, 2)

    x = a["x"].reshape(IMAGES, 3, 7, 16, 7, 16).transpose(0, 2, 4, 3, 5, 1).reshape(TOKENS, PATCH_D)
    patches = x[order].T.reshape(KP, P, BLOCKS, BT).transpose(1, 2, 0, 3).reshape(P, BLOCKS, KP * BT)
    w_tok = chunked(a["L0_tok_W"].T).reshape(P, KP * D)
    mats = np.stack([a[f"L0_attn_{n}"] for n in ("WK", "WQ", "WV", "Wg")])
    w_qkvg = mats.reshape(MATS, CH, P, KD, P).transpose(1, 4, 0, 3, 2).reshape(CH, P, CHUNK_COLS)
    w_o = chunked(a["L0_attn_WO"].T).reshape(P, 2, CH * D // 2).transpose(1, 0, 2)
    I = 128
    gates = np.concatenate([a["L0_ffn_sh_gate"].reshape(SHARED, I, D), a["L0_ffn_w_gate"]])
    ups = np.concatenate([a["L0_ffn_sh_up"].reshape(SHARED, I, D), a["L0_ffn_w_up"]])
    downs = np.concatenate([a["L0_ffn_sh_down"].reshape(D, SHARED, I).transpose(1, 0, 2), a["L0_ffn_w_down"]])
    E = EXPERTS + SHARED
    gu = np.stack([gates, ups], 1).reshape(E, 2, I, KD, P).transpose(0, 4, 3, 1, 2).reshape(E, P, KD * D)
    w_ffn = np.concatenate([gu, downs.transpose(0, 2, 1)], 2)
    w_ffn = w_ffn.reshape(PAIRS, 2, P, 3 * D).transpose(0, 2, 1, 3).reshape(PAIRS, P, PAIR_COLS)

    def column(v):
        return v.reshape(-1, P).T

    params = np.concatenate([column(a[f"L0_attn_{n}"]) for n in ("bK", "bQ", "bV", "bg")]
                            + [column(a["L0_attn_alpha_logit"].reshape(-1)), column(a["L0_tok_b"]),
                               column(a["L0_attn_bO"]), column(a["L0_attn_ln_gamma"]),
                               column(a["L0_attn_ln_beta"])], 1)
    image = np.concatenate([[i] * ln for ln in LENS for i in range(2)])
    time = np.concatenate([np.arange(s0, s0 + ln) for s0, ln in zip(STARTS, LENS) for i in range(2)])
    causal = ((image[:, None] == image[None]) & (time[:, None] <= time[None])).astype(np.float32)
    before = np.tile((np.arange(8)[None] < np.arange(8)[:, None]).astype(np.float32).reshape(1, 64), (GT, 1))
    arrays = {
        "patches": patches, "w_tok": w_tok, "w_qkvg": w_qkvg, "w_o": w_o, "w_ffn": w_ffn, "params": params,
        "w_route": chunked(a["L0_ffn_gate_w"].T).reshape(P, KD * EXPERTS),
        "b_route": a["L0_ffn_gate_bias"].reshape(1, EXPERTS),
        "identity": np.eye(P, dtype=np.float32), "causal_order": causal, "group_order": before,
    }
    nc = _bacc.Bacc("TRN2", target_bir_lowering=False, num_devices=1)
    args, arrays = [], {k: f(v) for k, v in arrays.items()}
    for name, v in arrays.items():
        args.append(nc.dram_tensor("in_" + name, v.shape, _mybir.dt.from_np(v.dtype), kind="ExternalInput").ap())
    args.append(nc.dram_tensor("comb_dram", (EXPERTS, TOKENS), F32, kind="Internal").ap())
    args.append(nc.dram_tensor("out_ch", (P, BLOCKS, KD * BT), F32, kind="ExternalOutput").ap())
    build(nc, *args)
    r = _run(nc, [{"in_" + k: v for k, v in arrays.items()}], core_ids=[0])
    got = r.results[0]["out_ch"].reshape(P, BLOCKS, KD, BT).transpose(1, 3, 2, 0).reshape(TOKENS, D)
    y = np.empty_like(got)
    y[order] = got
    return y.reshape(IMAGES, SEQ, D)
```

```python
from contextlib import ExitStack

import concourse.bass as bass
from concourse import mybir

ALU = mybir.AluOpType
ACT = mybir.ActivationFunctionType
AX = mybir.AxisListType
F32 = mybir.dt.float32
F32R = mybir.dt.float32r
I32 = mybir.dt.int32

P = 128
IMAGES, SEQ, D = 32, 49, 256
PATCH_D = 768
HEADS, D_HEAD = 16, 64
D_INNER = HEADS * D_HEAD
EXPERTS, SHARED, TOP_GROUPS, ROUTE_SCALE = 32, 2, 4, 2.5
ROUTE_GROUPS = 8
EPS = 1e-5

TOKENS = IMAGES * SEQ
GT = 2 * SEQ
GROUPS = 4
BT = GROUPS * GT
BLOCKS = TOKENS // BT
KD = D // P
KP = PATCH_D // P
PARTS = ((0, 1), (1, 3), (3, KP))
PART_OF = [i for i, (k0, k1) in enumerate(PARTS) for k in range(k0, k1)]
CH = D_INNER // P
STARTS = (0, 8, 16, 24, 32, 40)
LENS = (8, 8, 8, 8, 8, 9)
HALF = 4
MIN_DECAY = 1e-8
SPANS = len(STARTS) // 2
SPAN_T = 4 * STARTS[1]
FAR_KEYS = [SPAN_T * j + SPAN_T // 2 for j in range(SPANS)]
FAR_OFF = [sum(FAR_KEYS[:j]) for j in range(SPANS)]
FAR_COLS = sum(FAR_KEYS)
SPAN_TOKENS = [SPAN_T] * (SPANS - 1) + [GT - SPAN_T * (SPANS - 1)]
NEAR_Q = [n - SPAN_T // 2 for n in SPAN_TOKENS]
NEAR_OFF = [sum(NEAR_Q[:j]) for j in range(SPANS)]
KCOLS = FAR_COLS + GT
QCOLS = GT + sum(NEAR_Q)
POWERS = SEQ + HALF
STEPS = 2 * BLOCKS
PAIRS = (EXPERTS + SHARED) // 2
MATS = 4
PAIR_COLS = 2 * 3 * D
CHUNK_COLS = MATS * KD * P
GE = 2 * GROUPS * EXPERTS
GG = 2 * GROUPS * ROUTE_GROUPS

PB, PLOGIT, PTOKB, PBO, PGAMMA, PBETA, PCOLS = 0, 32, 40, 42, 44, 46, 48


def build(nc, patches, w_tok, w_qkvg, w_o, w_ffn, params, w_route, b_route, ident_d, causal_d,
          comb_rows, out):
    with ExitStack() as ctx:
        def sb(name, cols, dt=F32, rows=P):
            return ctx.enter_context(nc.sbuf_tensor(name, [rows, cols], dt))

        def sem(name):
            return ctx.enter_context(nc.semaphore(name))

        bank = [ctx.enter_context(nc.psum_tensor(f"bank{i}", [P, 512], F32)) for i in range(8)]

        xn = [sb("xn_hi", KD * TOKENS, F32R), sb("xn_lo", KD * TOKENS, F32R)]
        mov = sb("moving_parts", 2 * CH * BT, F32R)
        wbuf = [sb("weights_even", 2 * PAIR_COLS, F32R), sb("weights_odd", 2 * PAIR_COLS, F32R)]
        w_edge = sb("weights_tok_out", 2 * CH * D, F32R)
        og = sb("gated_heads", CH * TOKENS)
        token_store = sb("token_store", BLOCKS * GROUPS * D)
        raw = sb("weights_raw", 2 * PAIR_COLS)
        par = sb("channel_params", PCOLS)
        ident = sb("identity", P)
        causal = sb("causal", GT, I32)
        route_w = sb("route_w", KD * EXPERTS)
        route_b = sb("route_b", EXPERTS)
        decay = sb("decay", 2 * CH)
        tab_q = sb("powers_q", CH * QCOLS)
        tab_k = sb("powers_k", CH * KCOLS)
        work = sb("work", 2 * GROUPS * QCOLS + GROUPS * KCOLS + 2 * BT + BT + GROUPS * P + BT)
        small = sb("small", 96)
        rt = sb("router", 7 * GE + 9 * GG + 4 * GROUPS)

        def cut(t, at, n):
            return t[:, at:at + n], at + n

        at = 0
        q_dec, at = cut(work, at, 2 * GROUPS * QCOLS)
        k_dec, at = cut(work, at, GROUPS * KCOLS)
        probs, at = cut(work, at, 2 * BT)
        v_ch, at = cut(work, at, BT)
        v_tok, at = cut(work, at, GROUPS * P)
        gate, at = cut(work, at, BT)
        q_dec = q_dec.rearrange("p (h t) -> p h t", h=2)
        v_tok = v_tok.rearrange("p (g c) -> p g c", g=GROUPS)
        k_far = [k_dec[:, GROUPS * o:GROUPS * (o + n)].rearrange("p (g s) -> p g s", g=GROUPS)
                 for o, n in zip(FAR_OFF, FAR_KEYS)]
        k_near = k_dec[:, GROUPS * FAR_COLS:GROUPS * KCOLS].rearrange("p (g s) -> p g s", g=GROUPS)

        def near_queries(rows, heads, j):
            at = BT + GROUPS * NEAR_OFF[j]
            names = "p (g t) -> p g t" if isinstance(heads, int) else "p h (g t) -> p h g t"
            return q_dec[rows, heads, at:at + GROUPS * NEAR_Q[j]].rearrange(names, g=GROUPS)

        at = 0
        y_ch, at = cut(work, at, KD * BT)
        h2_tok, at = cut(work, at, GROUPS * D)
        x3_tok, at = cut(work, at, GROUPS * D)
        x3_ch, at = cut(work, at, KD * BT)
        comb_sb, at = cut(work, at, BT)
        comb_sb = comb_sb[0:2 * EXPERTS, :]
        at = CH * TOKENS // 2
        patch_raw = [None, None]
        patch_raw[0], at = cut(og, at, KP * BT)
        patch_raw[1] = og[:, 3584:3584 + KP * BT]
        h_ch, at = cut(og, at, KD * BT)
        z_tok, at = cut(og, at, GROUPS * D)
        xn_ch, at = cut(og, at, KD * BT)
        tok_raw = og[:, 0:KP * D]
        pw = og[:, 2048:2048 + CH * POWERS].rearrange("p (c e) -> p c e", c=CH)
        rw = og[:, 3072:3072 + CH * POWERS].rearrange("p (c e) -> p c e", c=CH)
        at = 0
        silu_g, weighted, hidden, comb = [], [], [], []
        for e in range(2):
            t, at = cut(og, at, BT)
            silu_g.append(t)
            t, at = cut(og, at, BT)
            weighted.append(t)
            t, at = cut(og, at, BT)
            hidden.append(t)
        for k in range(2):
            t, at = cut(og, at, 2 * BT)
            comb.append(t)

        def og_at(c, b):
            return og[:, bass.ds(c * TOKENS + b * BT, BT)]

        def xn_at(part, k, b):
            return xn[part][:, k * TOKENS + b * BT:k * TOKENS + (b + 1) * BT]

        xparts = [t[:, :].rearrange("p (k t) -> p k t", k=KD) for t in xn]

        def res(b):
            return token_store[0:GT, b * GROUPS * D:(b + 1) * GROUPS * D]

        def acc(b, m):
            return token_store[:, b * GROUPS * D + m * BT:b * GROUPS * D + (m + 1) * BT]

        def mov_at(part, c):
            return mov[:, (part * CH + c) * BT:(part * CH + c + 1) * BT]

        def patch_at(part, b, k):
            return mov_at(part, (KP * b + k) % CH)

        def rview(at, n):
            return rt[0:GT, at:at + n]

        r_exp, r_score, r_choice, r_a, r_b, r_c, comb_tok = (rview(i * GE, GE) for i in range(7))
        r_max, r_min = rview(7 * GE, 2 * GG), rview(7 * GE + 2 * GG, 2 * GG)
        r_gs, r_t0, r_t1, r_gtop, r_top = (rview(7 * GE + (4 + i) * GG, GG) for i in range(5))
        r_sel = r_t1
        r_sum = rview(7 * GE + 9 * GG, 2 * GROUPS)
        r_inv = rview(7 * GE + 9 * GG + 2 * GROUPS, 2 * GROUPS)

        stat = small[0:GT, 0:GROUPS * 6].rearrange("p (g n) -> p g n", g=GROUPS)
        mv = small[0:GT, 24:24 + GROUPS * 2].rearrange("p (g n) -> p g n", g=GROUPS)
        ve = small[0:GT, 32:32 + 2 * GROUPS]
        sd = small[0:GT, 40:40 + 2 * GROUPS]
        inv_std = small[0:GT, 48:48 + 2 * GROUPS]
        rstd, zscale = inv_std[:, 0:GROUPS], inv_std[:, GROUPS:2 * GROUPS]
        res_scale = small[0:GT, 56:56 + GROUPS]
        res_bias = small[0:GT, 60:60 + GROUPS]
        bias_now = [small[:, 64:66], small[:, 66:68]]
        warm_in, warm_out = small[:, 68:69], small[:, 69:70]

        s_patch_in = [[sem(f"patch_in_{parity}_{i}") for i in range(len(PARTS))] for parity in ("even", "odd")]
        s_tokw_in = [sem(f"tokw_in_{i}") for i in range(len(PARTS))]
        s_params_in = sem("params_in")
        s_consts_in = sem("consts_in")
        s_chunk_in = [sem("chunk_in_even"), sem("chunk_in_odd")]
        s_wo_in = sem("wo_in")
        s_warm = sem("warm")
        s_patch_hi = sem("patch_hi")
        s_patch_lo = sem("patch_lo")
        s_patch_lo_odd = sem("patch_lo_odd")
        s_chunk_split = sem("chunk_split")
        s_wo_split = sem("wo_split")
        s_pair_in = [sem("pair_in_even"), sem("pair_in_odd")]
        s_comb_kept = sem("comb_kept")
        s_stored = sem("stored")
        s_comb_in = [sem("comb_in_even"), sem("comb_in_odd")]
        s_wsplit_hi = sem("wsplit_hi")
        s_wsplit_lo = sem("wsplit_lo")
        s_weighted_done = sem("weighted_done")
        s_added = sem("added")
        s_out_done = sem("out_done")
        s_h_copied = sem("h_copied")
        s_tokw_hi = sem("tokw_hi")
        s_tokw_lo = sem("tokw_lo")
        s_patch_used = sem("patch_used")
        s_res_scale = sem("res_scale")
        s_res_done = sem("res_done")
        s_h_turned = sem("h_turned")
        s_z_done = sem("z_done")
        s_xn_read = sem("xn_read")
        s_xn_done = sem("xn_done")
        s_z_turned = sem("z_turned")
        s_xn_split = sem("xn_split")
        s_k_proj = sem("k_proj")
        s_q_proj = sem("q_proj")
        s_v_proj = sem("v_proj")
        s_g_proj = sem("g_proj")
        s_k_scaled = sem("k_scaled")
        s_q_scaled = sem("q_scaled")
        s_v_copied = sem("v_copied")
        s_gated = sem("gated")
        s_v_ready = sem("v_ready")
        s_v_turned = sem("v_turned")
        s_masked = sem("masked")
        s_scores = sem("scores")
        s_og_done = sem("og_done")
        s_pv = sem("pv")
        s_zeroed = sem("zeroed")
        s_y_first = sem("y_first")
        s_y_copied = sem("y_copied")
        s_og_first = sem("og_first")
        s_og_hi = sem("og_hi")
        s_og_lo = sem("og_lo")
        s_og_used = sem("og_used")
        s_h2_done = sem("h2_done")
        s_y_turned = sem("y_turned")
        s_acc_set = sem("acc_set")
        s_h2_turned = sem("h2_turned")
        s_x3_done = sem("x3_done")
        s_exp_done = sem("exp_done")
        s_x3_turned = sem("x3_turned")
        s_x3_copied = sem("x3_copied")
        s_logits = sem("logits")
        s_comb_done = sem("comb_done")
        s_comb_turned = sem("comb_turned")
        s_pair0_split = sem("pair0_split")
        s_x3_hi = sem("x3_hi")
        s_x3_lo = sem("x3_lo")
        s_g_ready = sem("g_ready")
        s_silu_done = sem("silu_done")
        s_u_ready = sem("u_ready")
        s_hidden_done = sem("hidden_done")
        s_hid_hi = sem("hid_hi")
        s_hid_lo = sem("hid_lo")
        s_y_ready = sem("y_ready")
        s_decay_e = sem("decay_e")
        s_pw_step = sem("pw_step")
        s_tables = sem("tables")
        s_stats = sem("stats")
        s_agg = sem("agg")
        s_veps = sem("veps")
        s_std = sem("std")
        s_rstd = sem("rstd")
        s_bias_ready = sem("bias_ready")
        s_r_step = sem("r_step")
        s_stats2 = sem("stats2")
        s_agg2 = sem("agg2")
        s_veps2 = sem("veps2")
        s_std3 = sem("std3")
        s_rstd2 = sem("rstd2")

        block = ctx.enter_context(nc.Block())

        def weight_parts(w, cols):
            return w[:, 0:cols], w[:, cols:2 * cols]

        def norm_bank(b):
            return 6 if b == BLOCKS - 1 else 2

        tok_hi, tok_lo = weight_parts(w_edge, KP * D)
        wo_hi, wo_lo = weight_parts(w_edge, CH * D)

        @block.sync
        def _(sp):

            def load_patches(b):
                for i, (k0, k1) in enumerate(PARTS):
                    cols = slice(k0 * BT, k1 * BT)
                    sp.dma_start(patch_raw[b % 2][:, cols], patches[:, b, cols]).then_inc(s_patch_in[b % 2][i], 16)
                    if b == 0:
                        cols = slice(k0 * D, k1 * D)
                        sp.dma_start(tok_raw[:, cols], w_tok[:, cols]).then_inc(s_tokw_in[i], 16)

            load_patches(0)
            sp.dma_start(par[:, :], params).then_inc(s_params_in, 16)
            load_patches(1)
            sp.dma_start(ident[:, :], ident_d).then_inc(s_consts_in, 16)
            sp.dma_start(causal[0:GT, :], causal_d).then_inc(s_consts_in, 16)
            sp.dma_start(route_w[:, :], w_route).then_inc(s_consts_in, 16)
            sp.dma_start(route_b[0:GT, :], b_route.broadcast_to([GT, EXPERTS])).then_inc(s_consts_in, 16)

            def load_chunk(c):
                sp.dma_start(raw[:, c * CHUNK_COLS:(c + 1) * CHUNK_COLS], w_qkvg[c]).then_inc(s_chunk_in[c], 16)

            for b in range(2, BLOCKS):
                sp.wait_ge(s_patch_hi, KP * (b - 1))
                sp.wait_ge(s_patch_lo, KP + (b - 2) * KP // 2)
                if b == 3:
                    sp.wait_ge(s_patch_lo_odd, KP // 2)
                load_patches(b)
                load_chunk(b - 2)
            sp.dma_start(raw[:, 2 * CHUNK_COLS:3 * CHUNK_COLS], w_o[0]).then_inc(s_wo_in, 16)
            with sp.Fori(0, CH // 2 - 1) as q:
                for w in range(2):
                    sp.wait_ge(s_chunk_split, 4 * q + 2 * (w + 1))
                    sp.dma_start(raw[:, w * CHUNK_COLS:(w + 1) * CHUNK_COLS],
                                 w_qkvg[bass.ds(2 * q + 2 + w, 1)].rearrange("a p n -> p (a n)")
                                 ).then_inc(s_chunk_in[w], 16)
            sp.wait_ge(s_wo_split, 2)
            sp.dma_start(raw[:, 2 * CHUNK_COLS:3 * CHUNK_COLS], w_o[1]).then_inc(s_wo_in, 16)
            sp.wait_ge(s_wo_split, 4)
            sp.wait_ge(s_chunk_split, 2 * CH)
            for p in range(2):
                sp.dma_start(raw[:, p * PAIR_COLS:(p + 1) * PAIR_COLS], w_ffn[p]).then_inc(s_pair_in[p], 16)

            def store_comb(i):
                sp.wait_ge(s_comb_kept, i + 1)
                sp.dma_start(comb_rows[2 * i * EXPERTS:2 * (i + 1) * EXPERTS, :], comb_sb).then_inc(s_stored, 16)

            def load_comb(pair, b):
                for e in range(2):
                    sp.dma_start(comb[b % 2][:, e * BT:(e + 1) * BT],
                                 comb_rows[bass.ds(b * EXPERTS + 2 * (pair - 1) + e, 1), :].broadcast_to([P, BT])
                                 ).then_inc(s_comb_in[b % 2], 16)

            def load_weights(p, w):
                sp.dma_start(raw[:, w * PAIR_COLS:(w + 1) * PAIR_COLS],
                             w_ffn[bass.ds(p + 2, 1)].rearrange("a p n -> p (a n)")).then_inc(s_pair_in[w], 16)

            def load_weights_after_split(p, w):
                sp.wait_ge(s_wsplit_hi, 3 * p)
                sp.wait_ge(s_wsplit_lo, 3 * p)
                load_weights(p, w)

            sp.wait_ge(s_pair0_split, 2)
            load_weights(0, 0)
            store_comb(0)
            sp.wait_ge(s_og_lo, CH * (BLOCKS - 1))
            sp.wait_ge(s_stored, 16)
            load_comb(1, 0)
            load_comb(1, 1)

            def comb_ahead(p, blocks):
                for b in blocks:
                    sp.wait_ge(s_weighted_done, 2 * (BLOCKS * (p - 1) + b + 1))
                    load_comb(p + (b + 2) // BLOCKS, (b + 2) % BLOCKS)

            load_weights_after_split(1, 1)
            store_comb(1)
            sp.wait_ge(s_stored, 16 * 2)
            comb_ahead(1, range(BLOCKS))
            load_weights_after_split(2, 0)
            comb_ahead(2, range(BLOCKS))
            with sp.Fori(1, PAIRS // 2 - 1) as q:
                for w in (1, 0):
                    p = 2 * q + 2 - w
                    load_weights_after_split(p, w)
                    comb_ahead(p, range(BLOCKS))
            comb_ahead(PAIRS - 2, range(BLOCKS))
            comb_ahead(PAIRS - 1, range(2))
            for b in range(BLOCKS):
                sp.wait_ge(s_added, BLOCKS * (PAIRS - 1) + b + 1)
                sp.dma_start(out[:, b, :], token_store[:, b * GROUPS * D:b * GROUPS * D + KD * BT]
                             ).then_inc(s_out_done, 16)
            sp.wait_ge(s_out_done, 16 * BLOCKS)

        @block.tensor
        def _(pe):
            def three_pass(dst, terms):
                for k, (wh, wl, xh, xl, first, last) in enumerate(terms):
                    pe.matmul(dst, wl, xh, start=first, stop=False)
                    pe.matmul(dst, wh, xh, start=False, stop=False)
                    mm = pe.matmul(dst, wh, xl, start=False, stop=last)
                return mm

            def patch_project(b, chunks):
                if b >= 2 and 0 in chunks:
                    pe.wait_ge(s_h_copied, 2 * (b - 1))
                for k in chunks:
                    if b == 0:
                        pe.wait_ge(s_tokw_hi, k + 1)
                        pe.wait_ge(s_tokw_lo, k + 1)
                    pe.wait_ge(s_patch_hi, KP * b + k + 1)
                    if b == 0:
                        pe.wait_ge(s_patch_lo, k + 1)
                    elif k % 2 == 0:
                        pe.wait_ge(s_patch_lo, KP + (b - 1) * KP // 2 + k // 2 + 1)
                    else:
                        pe.wait_ge(s_patch_lo_odd, (b - 1) * KP // 2 + k // 2 + 1)
                    for m in range(KD):
                        cols = slice(k * D + m * P, k * D + (m + 1) * P)
                        mm = three_pass(bank[6 * (b % 2) + m][:, 0:BT], [
                            (tok_hi[:, cols], tok_lo[:, cols], patch_at(0, b, k), patch_at(1, b, k),
                             k == 0, k == KP - 1)])
                    mm.then_inc(s_patch_used, 1)

            def turn_tokens(src, done, first_bank=2):
                for g in range(GROUPS):
                    for m in range(KD):
                        at = (g % 2) * D + m * P
                        mm = pe.transpose(bank[first_bank + g // 2][0:GT, at:at + P],
                                          src[:, m * BT + g * GT:m * BT + (g + 1) * GT], ident[:, :])
                mm.then_inc(done, 1)

            def turn_channels(src, first_bank, done):
                for m in range(KD):
                    for g in range(GROUPS):
                        mm = pe.transpose(bank[first_bank + m][:, g * GT:(g + 1) * GT],
                                          src[0:GT, g * D + m * P:g * D + (m + 1) * P], ident[0:GT, 0:GT])
                mm.then_inc(done, 1)

            def turn_h(b):
                pe.wait_ge(s_h_copied, 2 * (b + 1))
                if 1 <= b < BLOCKS - 1:
                    pe.wait_ge(s_res_done, b)
                turn_tokens(h_ch, s_h_turned, first_bank=norm_bank(b))

            def turn_z(b):
                pe.wait_ge(s_z_done, b + 1)
                if b >= 1:
                    pe.wait_ge(s_xn_read, 2 * b)
                turn_channels(z_tok, 4, s_z_turned)

            patch_project(0, range(KP))
            pe.wait_ge(s_consts_in, 16 * 4)
            for b in range(BLOCKS - 1):
                early = 4 if b >= 1 else 3
                patch_project(b + 1, range(early))
                turn_h(b)
                if b >= 1:
                    turn_z(b - 1)
                patch_project(b + 1, range(early, KP))

            def project(c, b, it, w, first=False, mats=range(MATS)):
                pe.wait_ge(s_chunk_split, 2 * (c + 1))
                pe.wait_ge(s_xn_split, b + 1)
                hi, lo = weight_parts(wbuf[w], CHUNK_COLS)
                ready = (s_k_proj, s_q_proj, s_v_proj, s_g_proj)
                for m in mats:
                    if not first:
                        pe.wait_ge((s_k_scaled, s_q_scaled, s_v_copied, s_gated)[m], it)
                    cols = [slice((m * KD + k) * P, (m * KD + k + 1) * P) for k in range(KD)]
                    three_pass(bank[m][:, 0:BT], [
                        (hi[:, cols[k]], lo[:, cols[k]], xn_at(0, k, b), xn_at(1, k, b), k == 0, k == KD - 1)
                        for k in range(KD)]).then_inc(ready[m], 1)

            def turn_values(it, first=False):
                pe.wait_ge(s_v_copied, it + 1)
                if not first:
                    pe.wait_ge(s_v_ready, it)
                for g in range(GROUPS):
                    mm = pe.transpose(bank[4][0:GT, g * P:(g + 1) * P], v_ch[:, g * GT:(g + 1) * GT], ident[:, :])
                mm.then_inc(s_v_turned, 1)

            def score(it):
                pe.wait_ge(s_k_scaled, it + 1)
                pe.wait_ge(s_q_scaled, it + 1)
                pe.wait_ge(s_masked, 2 * it + 2)
                for g in range(GROUPS):
                    dst = bank[6 + g // 2][:, (g % 2) * 2 * GT:(g % 2 + 1) * 2 * GT].rearrange(
                        "p (h t) -> p h t", h=2)
                    for j in reversed(range(SPANS)):
                        k0, n = SPAN_T * j, SPAN_TOKENS[j]
                        n_far = n if j else SPAN_T // 2
                        pe.matmul(dst[0:FAR_KEYS[j], :, k0:k0 + n_far], k_far[j][:, g, :],
                                  q_dec[:, :, g * GT + k0:g * GT + k0 + n_far], start=True, stop=True)
                        mm = pe.matmul(dst[k0:k0 + n, :, k0 + SPAN_T // 2:k0 + n], k_near[:, g, k0:k0 + n],
                                       near_queries(slice(0, P), slice(0, 2), j)[:, :, g, :], start=True, stop=True)
                    if g % 2:
                        mm.then_inc(s_scores, 1)

            def mix_values(it):
                pe.wait_ge(s_v_ready, it + 1)
                pe.wait_ge(s_og_done, it + 1)
                for g in range(GROUPS):
                    if g % 2 == 0:
                        pe.wait_ge(s_masked, 2 * it + g // 2 + 3)
                    for h in range(2):
                        mm = pe.matmul(bank[5][h * D_HEAD:(h + 1) * D_HEAD, g * GT:(g + 1) * GT],
                                       v_tok[0:GT, g, h * D_HEAD:(h + 1) * D_HEAD],
                                       probs[0:GT, (2 * g + h) * GT:(2 * g + h + 1) * GT], start=True, stop=True)
                mm.then_inc(s_pv, 1)

            def turn(q, last=False):
                for u in range(STEPS):
                    it = STEPS * q + u
                    score(it)
                    end = last and u == STEPS - 1
                    n = u + 1
                    if not end:
                        project(2 * q + n // BLOCKS, n % BLOCKS, it + 1, (n // BLOCKS) % 2)
                    mix_values(it)
                    if not end:
                        turn_values(it + 1)

            project(0, 0, 0, 0, first=True, mats=(0,))
            turn_h(BLOCKS - 1)
            project(0, 0, 0, 0, first=True, mats=(1,))
            turn_z(BLOCKS - 2)
            pe.wait_ge(s_res_done, BLOCKS - 1)
            project(0, 0, 0, 0, first=True, mats=(2, 3))
            pe.wait_ge(s_xn_read, 2 * (BLOCKS - 1))
            turn_values(0, first=True)
            pe.wait_ge(s_v_ready, 1)
            turn_z(BLOCKS - 1)
            pe.wait_ge(s_xn_read, 2 * BLOCKS)
            pe.wait_ge(s_zeroed, 1)
            with pe.Fori(0, CH // 2 - 1) as q:
                turn(q)
            turn(CH // 2 - 1, last=True)

            def out_project(b, chunks=range(CH)):
                if 0 in chunks:
                    if b == 0:
                        pe.wait_ge(s_wo_split, 4)
                        pe.wait_ge(s_k_scaled, STEPS * CH // 2)
                        pe.wait_ge(s_q_scaled, STEPS * CH // 2)
                    else:
                        pe.wait_ge(s_y_copied, 2 * b)
                def product(k, m):
                    cols = slice(k * D + m * P, k * D + (m + 1) * P)
                    return three_pass(bank[m][:, 0:BT], [
                        (wo_hi[:, cols], wo_lo[:, cols], mov_at(0, k), mov_at(1, k), k == 0, k == CH - 1)])

                def heads_split(k):
                    if b == 0:
                        pe.wait_ge(s_og_first, 2 * (k + 1))
                    else:
                        pe.wait_ge(s_og_hi, CH * (b - 1) + k + 1)
                        pe.wait_ge(s_og_lo, CH * (b - 1) + k + 1)

                for k in chunks:
                    if k < CH - 2:
                        heads_split(k)
                        product(k, 0)
                        product(k, 1).then_inc(s_og_used, 1)
                if CH - 1 in chunks:
                    heads_split(CH - 2)
                    product(CH - 2, 0)
                    heads_split(CH - 1)
                    product(CH - 1, 0).then_inc(s_y_first, 1)
                    product(CH - 2, 1).then_inc(s_og_used, 1)
                    product(CH - 1, 1).then_inc(s_og_used, 1)

            def turn_y(b):
                pe.wait_ge(s_y_copied, 2 * (b + 1))
                if b == 0:
                    pe.wait_ge(s_v_copied, STEPS * CH // 2)
                    pe.wait_ge(s_gated, STEPS * CH // 2)
                else:
                    pe.wait_ge(s_h2_done, 2 * b)
                turn_tokens(y_ch, s_y_turned)

            def turn_h2(b):
                pe.wait_ge(s_h2_done, 2 * (b + 1))
                if b == 0:
                    pe.wait_ge(s_v_ready, STEPS * CH // 2)
                    pe.wait_ge(s_og_done, STEPS * CH // 2 + 1)
                else:
                    pe.wait_ge(s_acc_set, 2 * b)
                turn_channels(h2_tok, 4, s_h2_turned)

            def turn_x3(b):
                pe.wait_ge(s_x3_done, b + 1)
                if b == 0:
                    pe.wait_ge(s_masked, STEPS * CH + 2)
                else:
                    pe.wait_ge(s_exp_done, b)
                turn_channels(x3_tok, 6, s_x3_turned)

            def route(b):
                pe.wait_ge(s_x3_copied, 2 * (b + 1))
                pe.wait_ge(s_x3_hi, 2 * (b + 1))
                for g in range(GROUPS):
                    for m in range(KD):
                        mm = pe.matmul(bank[6][0:GT, g * EXPERTS:(g + 1) * EXPERTS],
                                       x3_ch[:, m * BT + g * GT:m * BT + (g + 1) * GT],
                                       route_w[:, m * EXPERTS:(m + 1) * EXPERTS], start=m == 0, stop=m == KD - 1)
                mm.then_inc(s_logits, 1)

            def turn_comb(i):
                pe.wait_ge(s_comb_done, i + 1)
                for g in range(GROUPS):
                    mm = pe.transpose(bank[7][0:2 * EXPERTS, g * GT:(g + 1) * GT],
                                      comb_tok[:, 2 * g * EXPERTS:2 * (g + 1) * EXPERTS], ident[0:GT, 0:GT])
                mm.then_inc(s_comb_turned, 1)

            out_project(0)
            for b in range(BLOCKS - 1):
                turn_y(b)
                out_project(b + 1, range(2))
                if b >= 1:
                    route(b - 1)
                out_project(b + 1, range(2, 4))
                turn_h2(b)
                out_project(b + 1, range(4, CH))
                turn_x3(b)
            turn_y(BLOCKS - 1)
            route(BLOCKS - 2)

            def expert_up(p, b, n, w, first=False, between=None):
                if isinstance(p, int) and p == 0:
                    pe.wait_ge(s_pair0_split, 2)
                else:
                    pe.wait_ge(s_wsplit_hi, 3 * p)
                    pe.wait_ge(s_wsplit_lo, 3 * p)
                pe.wait_ge(s_x3_hi, 2 * (b + 1))
                pe.wait_ge(s_x3_lo, b + 1)
                hi, lo = weight_parts(wbuf[w], PAIR_COLS)
                for e in range(2):
                    if between is not None and e == 1:
                        between()
                    if first and e == 1:
                        pe.wait_ge(s_h2_done, 2 * BLOCKS)
                    for gu, (ready, free) in enumerate(((s_g_ready, s_silu_done), (s_u_ready, s_hidden_done))):
                        if not first:
                            pe.wait_ge(free, 2 * n - 1 + e)
                        cols = [slice(e * 3 * D + k * D + gu * P, e * 3 * D + k * D + gu * P + P) for k in range(KD)]
                        three_pass(bank[2 * e + gu][:, 0:BT], [
                            (hi[:, cols[k]], lo[:, cols[k]], xn_at(0, k, b), xn_at(1, k, b), k == 0, k == KD - 1)
                            for k in range(KD)]).then_inc(ready, 1)

            def expert_down(b, n, w, early=False):
                hi, lo = weight_parts(wbuf[w], PAIR_COLS)
                if not early:
                    pe.wait_ge(s_added, n - 1)
                for e in range(2):
                    pe.wait_ge(s_hid_hi, 2 * n + e + 1)
                    pe.wait_ge(s_hid_lo, 2 * n + e + 1)
                    x_hi, x_lo = mov_at(b % 2, 2 * e), mov_at(b % 2, 2 * e + 1)
                    for m in range(KD):
                        cols = slice(e * 3 * D + KD * D + m * P, e * 3 * D + KD * D + (m + 1) * P)
                        mm = three_pass(bank[4 + 2 * (b % 2) + m][:, 0:BT],
                                        [(hi[:, cols], lo[:, cols], x_hi, x_lo, e == 0, e == 1)])
                mm.then_inc(s_y_ready, 1)

            def pair_steps(p, w, last=False):
                for b in range(BLOCKS):
                    n = BLOCKS * p + b
                    if b < BLOCKS - 1:
                        expert_up(p, b + 1, n + 1, w)
                    elif not last:
                        expert_up(p + 1, 0, n + 1, 1 - w)
                    expert_down(b, n, w)

            pe.wait_ge(s_y_copied, 2 * BLOCKS)
            expert_up(0, 0, 0, 0, first=True)
            turn_h2(BLOCKS - 1)
            turn_x3(BLOCKS - 1)
            expert_up(0, 1, 1, 0)
            route(BLOCKS - 1)
            pe.wait_ge(s_acc_set, 2 * BLOCKS)
            expert_down(0, 0, 0, early=True)
            turn_comb(0)
            expert_up(0, 2, 2, 0)
            pe.wait_ge(s_exp_done, BLOCKS)
            pe.wait_ge(s_comb_kept, 1)
            expert_down(1, 1, 0, early=True)
            expert_up(0, 3, 3, 0)
            expert_down(2, 2, 0)
            pe.wait_ge(s_added, 2)
            expert_up(1, 0, BLOCKS, 1, between=lambda: turn_comb(1))
            pe.wait_ge(s_comb_kept, 2)
            expert_down(3, 3, 0)
            with pe.Fori(0, PAIRS // 2 - 1) as q:
                pair_steps(2 * q + 1, 1)
                pair_steps(2 * q + 2, 0)
            pair_steps(PAIRS - 2, 1)
            pair_steps(PAIRS - 1, 0, last=True)

        @block.vector
        def _(dve):
            def split_patches(b, chunks):
                for k in chunks:
                    dve.wait_ge(s_patch_hi, KP * b + k + 1)
                    dve.tensor_tensor(patch_at(1, b, k), patch_raw[b % 2][:, k * BT:(k + 1) * BT],
                                      patch_at(0, b, k).bitcast(F32), ALU.subtract).then_inc(s_patch_lo, 1)

            dve.memset(warm_in, 0.0).then_inc(s_warm, 1)
            split_patches(0, range(KP))

            dve.memset(gate, 0.0).then_inc(s_og_done, 1)
            dve.memset(q_dec[:, :, :], 0.0).then_inc(s_zeroed, 1)
            split_patches(1, range(0, KP, 2))

            dve.wait_ge(s_decay_e, 1)
            n = [0]

            def power(ins):
                n[0] += 1
                ins.then_inc(s_pw_step, 1)

            def powers_done():
                dve.wait_ge(s_pw_step, n[0])

            e_neg, alpha = decay[:, 0:CH], decay[:, CH:2 * CH]
            power(dve.tensor_scalar(e_neg, e_neg, 1.0, None, ALU.add))
            powers_done()
            power(dve.reciprocal(alpha, e_neg))
            powers_done()
            power(dve.tensor_scalar(pw[:, :, HALF + 1], alpha, MIN_DECAY, None, ALU.max))
            power(dve.tensor_scalar(rw[:, :, SEQ - 2], alpha, MIN_DECAY, None, ALU.max))
            power(dve.memset(pw[:, :, HALF:HALF + 1], 1.0))
            power(dve.memset(rw[:, :, SEQ - 1:SEQ], 1.0))
            k = 1
            while k < SEQ - 1:
                m = min(k, SEQ - 1 - k)
                powers_done()
                power(dve.tensor_tensor(pw[:, :, HALF + k + 1:HALF + k + 1 + m], pw[:, :, HALF + 1:HALF + 1 + m],
                                        pw[:, :, HALF + k:HALF + k + 1].broadcast_to([P, CH, m]), ALU.mult))
                e = SEQ - 1
                power(dve.tensor_tensor(rw[:, :, e - k - m:e - k], rw[:, :, e - m:e],
                                        rw[:, :, e - k:e - k + 1].broadcast_to([P, CH, m]), ALU.mult))
                k *= 2
            powers_done()
            power(dve.reciprocal(pw[:, :, 0:HALF], rw[:, :, SEQ - 1 - HALF:SEQ - 1]))
            power(dve.reciprocal(rw[:, :, SEQ:SEQ + HALF], pw[:, :, HALF + 1:2 * HALF + 1]))
            powers_done()
            tq = tab_q[:, :].rearrange("p (c t) -> p c t", c=CH)
            tk = tab_k[:, :].rearrange("p (c t) -> p c t", c=CH)

            def tables(j):
                far, near = STARTS[2 * j] + HALF, STARTS[2 * j + 1] + HALF
                near_at = GT + NEAR_OFF[j]

                def images(t, at, n):
                    return t[:, :, at:at + 2 * n].rearrange("p c (i t) -> p c i t", i=2)

                def powers(t, at, n):
                    return t[:, :, at:at + n].rearrange("p c (o t) -> p c o t", o=1).broadcast_to([P, CH, 2, n])

                for i in (2 * j, 2 * j + 1):
                    dve.tensor_copy(images(tq, 2 * STARTS[i], LENS[i]),
                                    powers(pw, STARTS[i] - far + HALF, LENS[i]))
                    ins = dve.tensor_copy(images(tk, FAR_COLS + 2 * STARTS[i], LENS[i]),
                                          powers(rw, SEQ - 1 - near + STARTS[i], LENS[i]))
                dve.tensor_copy(images(tq, near_at, LENS[2 * j + 1]), powers(pw, 0, LENS[2 * j + 1]))
                for i in range(2 * j + 1):
                    ins = dve.tensor_copy(images(tk, FAR_OFF[j] + 2 * STARTS[i], LENS[i]),
                                          powers(rw, SEQ - 1 - far + STARTS[i], LENS[i]))
                ins.then_inc(s_tables, 1)

            def two_banks(first, g):
                return bank[first + g // 2][0:GT, (g % 2) * D:(g % 2 + 1) * D]

            biases = par[:, PB + 2 * CH:PB + 4 * CH].rearrange("p (m c) -> p m c", m=2)

            def fetch_biases(c, w):
                dve.tensor_scalar(bias_now[w].rearrange("p (m o) -> p m o", o=1), biases[:, :, bass.ds(c, 1)],
                                  1.0, None, ALU.mult).then_inc(s_bias_ready, 1)

            fetch_biases(0, 0)
            for b in range(BLOCKS):
                if b + 2 < BLOCKS:
                    split_patches(b + 2, range(0, 4, 2))
                dve.wait_ge(s_h_turned, b + 1)
                for g in range(GROUPS):
                    ins = dve.bn_stats(stat[:, g, :], two_banks(norm_bank(b), g))
                ins.then_inc(s_stats, 1)
                dve.wait_ge(s_stats, b + 1)
                if b >= 1:
                    dve.wait_ge(s_z_done, b)
                    dve.wait_ge(s_res_scale, b)
                for g in range(GROUPS):
                    ins = dve.bn_aggr(mv[:, g, :], stat[:, g, :])
                ins.then_inc(s_agg, 1)
                dve.wait_ge(s_agg, b + 1)
                dve.tensor_scalar(ve[:, 0:GROUPS], mv[:, :, 1], EPS, None, ALU.add)
                dve.tensor_scalar(ve[:, GROUPS:2 * GROUPS], mv[:, :, 1], 1.0 + EPS, EPS * EPS,
                                  ALU.mult, ALU.add).then_inc(s_veps, 1)
                dve.wait_ge(s_std, b + 1)
                dve.reciprocal(inv_std, sd).then_inc(s_rstd, 1)
                dve.wait_ge(s_rstd, b + 1)
                if b >= 1:
                    dve.wait_ge(s_z_turned, b)
                for g in range(GROUPS):
                    ins = dve.tensor_scalar(z_tok[0:GT, g * D:(g + 1) * D], two_banks(norm_bank(b), g),
                                            mv[:, g, 0:1], zscale[:, g:g + 1], ALU.subtract, ALU.mult)
                ins.then_inc(s_z_done, 1)
                if b >= 1:
                    dve.wait_ge(s_res_done, b)
                dve.tensor_scalar(res_scale, rstd, 1.0, None, ALU.add)
                dve.scalar_tensor_tensor(out=res_bias, in0=mv[:, :, 0], scalar=-1.0, in1=rstd,
                                         op0=ALU.mult, op1=ALU.mult).then_inc(s_res_scale, 1)
                if b + 2 < BLOCKS:
                    split_patches(b + 2, range(4, KP, 2))
                for j in ((0,), (1, 2), (), ())[b]:
                    tables(j)

            def scale_keys(c, it):
                dve.wait_ge(s_k_proj, it + 1)
                src = bank[0][:, 0:BT].rearrange("p (g t) -> p g t", g=GROUPS)
                for dst, off, n in [(k_far[j], FAR_OFF[j], FAR_KEYS[j]) for j in range(SPANS)] + [
                        (k_near, FAR_COLS, GT)]:
                    table = tab_k[:, bass.ds(c * KCOLS + off, n)]
                    ins = dve.scalar_tensor_tensor(
                        out=dst, in0=src[:, :, 0:n], scalar=par[:, bass.ds(PB + c, 1)],
                        in1=table.rearrange("p (o t) -> p o t", o=1).broadcast_to([P, GROUPS, n]),
                        op0=ALU.add, op1=ALU.mult)
                ins.then_inc(s_k_scaled, 1)

            def scale_queries(c, it):
                dve.wait_ge(s_q_proj, it + 1)
                for h in range(2):
                    rows = slice(h * D_HEAD, (h + 1) * D_HEAD)
                    q_bias = par[rows, bass.ds(PB + CH + c, 1)]
                    src = bank[1][rows, 0:BT].rearrange("p (g t) -> p g t", g=GROUPS)
                    dve.scalar_tensor_tensor(
                        out=q_dec[rows, h, 0:BT].rearrange("p (g t) -> p g t", g=GROUPS),
                        in0=src, scalar=q_bias,
                        in1=tab_q[rows, bass.ds(c * QCOLS, GT)].rearrange("p (o t) -> p o t", o=1).broadcast_to(
                            [D_HEAD, GROUPS, GT]), op0=ALU.add, op1=ALU.mult)
                    for j in range(SPANS):
                        table = tab_q[rows, bass.ds(c * QCOLS + GT + NEAR_OFF[j], NEAR_Q[j])]
                        q0 = SPAN_T * j + SPAN_T // 2
                        ins = dve.scalar_tensor_tensor(
                            out=near_queries(rows, h, j), in0=src[:, :, q0:q0 + NEAR_Q[j]], scalar=q_bias,
                            in1=table.rearrange("p (o t) -> p o t", o=1).broadcast_to(
                                [D_HEAD, GROUPS, NEAR_Q[j]]), op0=ALU.add, op1=ALU.mult)
                ins.then_inc(s_q_scaled, 1)

            def mask_scores(it):
                for k in range(2):
                    dve.wait_ge(s_scores, 2 * it + k + 1)
                    dve.tensor_tensor(
                        probs[0:GT, k * BT:(k + 1) * BT].bitcast(I32).rearrange("p (n t) -> p n t", n=4),
                        bank[6 + k][0:GT, 0:BT].bitcast(I32).rearrange("p (n t) -> p n t", n=4),
                        causal[0:GT, :].rearrange("p (o t) -> p o t", o=1).broadcast_to([GT, 4, GT]),
                        ALU.bitwise_and).then_inc(s_masked, 1)

            def gate_heads(c, b, it):
                dve.wait_ge(s_pv, it + 1)
                dve.wait_ge(s_gated, it + 1)
                dve.tensor_tensor(og_at(c, b), bank[5][:, 0:BT], gate, ALU.mult).then_inc(s_og_done, 1)

            def turn(q, last=False):
                for u in range(STEPS):
                    it = STEPS * q + u
                    mask_scores(it)
                    if not (last and u == STEPS - 1):
                        c = 2 * q + (u + 1) // BLOCKS
                        scale_keys(c, it + 1)
                        scale_queries(c, it + 1)
                    gate_heads(2 * q + u // BLOCKS, u % BLOCKS, it)
                    w = u // BLOCKS
                    if u % BLOCKS == 0 and not (last and w == 1):
                        fetch_biases(2 * q + w + 1, 1 - w)

            dve.wait_ge(s_tables, SPANS)
            scale_keys(0, 0)
            scale_queries(0, 0)
            dve.wait_ge(s_res_done, BLOCKS)
            dve.memset(bank[6][:, 0:BT], 0.0).then_inc(s_masked, 1)
            dve.memset(bank[7][:, 0:BT], 0.0).then_inc(s_masked, 1)
            with dve.Fori(0, CH // 2 - 1) as q:
                turn(q)
            turn(CH // 2 - 1, last=True)

            rs = [0]

            def r_op(ins):
                rs[0] += 1
                ins.then_inc(s_r_step, 1)
                dve.wait_ge(s_r_step, rs[0])

            LOW, HIGH = -3e38, 3e38
            quad = r_choice.rearrange("p (n a) -> p n a", a=4)

            def best_marked(out, top, src, n):
                for g in range(2 * GROUPS):
                    ins = dve.match_replace(out[:, g * n:(g + 1) * n], top[:, g * 8:(g + 1) * 8],
                                            src[:, g * n:(g + 1) * n], LOW)
                return ins

            def route_groups(i):
                score3 = r_score.rearrange("p (g e) -> p g e", e=EXPERTS)
                choice3 = r_choice.rearrange("p (g e) -> p g e", e=EXPERTS)
                dve.wait_ge(s_exp_done, 2 * (i + 1))
                if i >= 1:
                    dve.wait_ge(s_comb_done, i)
                r_op(dve.tensor_scalar(r_a, r_exp, 1.0, None, ALU.add))
                r_op(dve.reciprocal(r_score, r_a))
                r_op(dve.tensor_tensor(choice3, score3, route_b[0:GT, :].rearrange("p (o e) -> p o e", o=1)
                                       .broadcast_to([GT, 2 * GROUPS, EXPERTS]), ALU.add))
                mx = r_max.rearrange("p (n a) -> p n a", a=2)
                mn = r_min.rearrange("p (n a) -> p n a", a=2)
                dve.tensor_tensor(mx, quad[:, :, 0:4:2], quad[:, :, 1:4:2], ALU.max)
                r_op(dve.tensor_tensor(mn, quad[:, :, 0:4:2], quad[:, :, 1:4:2], ALU.min))
                dve.tensor_tensor(r_gs, mx[:, :, 0], mx[:, :, 1], ALU.max)
                dve.tensor_tensor(r_t0, mx[:, :, 0], mx[:, :, 1], ALU.min)
                r_op(dve.tensor_tensor(r_t1, mn[:, :, 0], mn[:, :, 1], ALU.max))
                r_op(dve.tensor_tensor(r_t0, r_t0, r_t1, ALU.max))
                r_op(dve.tensor_tensor(r_gs, r_gs, r_t0, ALU.add))
                for g in range(2 * GROUPS):
                    ins = dve.max(r_gtop[:, g * 8:(g + 1) * 8], r_gs[:, g * 8:(g + 1) * 8])
                r_op(ins)
                r_op(dve.memset(r_gtop.rearrange("p (n j) -> p n j", j=8)[:, :, TOP_GROUPS:8], HIGH))
                r_op(best_marked(r_sel, r_gtop, r_gs, ROUTE_GROUPS))
                r_op(dve.tensor_tensor(r_sel, r_sel, r_gs, ALU.not_equal))
                r_op(dve.tensor_tensor(quad, quad, r_sel.rearrange("p (n o) -> p n o", o=1).broadcast_to(
                    [GT, GG, 4]), ALU.mult))
                r_op(dve.tensor_scalar(r_b, r_choice, 0.0, None, ALU.add))

            def route_experts(i):
                for g in range(2 * GROUPS):
                    ins = dve.max(r_top[:, g * 8:(g + 1) * 8], r_b[:, g * EXPERTS:(g + 1) * EXPERTS])
                r_op(ins)
                r_op(best_marked(r_c, r_top, r_b, EXPERTS))
                r_op(dve.tensor_tensor(r_c, r_c, r_b, ALU.not_equal))
                r_op(dve.tensor_tensor(r_a, r_c, r_score, ALU.mult))
                r_op(dve.tensor_reduce(r_sum, r_a.rearrange("p (g e) -> p g e", e=EXPERTS), AX.X, ALU.add))
                r_op(dve.tensor_scalar(r_sum, r_sum, 1e-20, None, ALU.add))
                r_op(dve.reciprocal(r_inv, r_sum))
                if i >= 1:
                    dve.wait_ge(s_comb_turned, i)
                for g in range(2 * GROUPS):
                    ins = dve.tensor_scalar(comb_tok[:, g * EXPERTS:(g + 1) * EXPERTS],
                                            r_a[:, g * EXPERTS:(g + 1) * EXPERTS], r_inv[:, g:g + 1], ROUTE_SCALE,
                                            ALU.mult, ALU.mult)
                ins.then_inc(s_comb_done, 1)

            def norm(b):
                dve.wait_ge(s_y_turned, b + 1)
                for k in range(2):
                    ins = dve.tensor_tensor(h2_tok[0:GT, k * 2 * D:(k + 1) * 2 * D], bank[2 + k][0:GT, :],
                                            res(b)[:, k * 2 * D:(k + 1) * 2 * D], ALU.add)
                    ins.then_inc(s_h2_done, 1)
                dve.wait_ge(s_h2_done, 2 * (b + 1))
                for g in range(GROUPS):
                    ins = dve.bn_stats(stat[:, g, :], h2_tok[0:GT, g * D:(g + 1) * D])
                ins.then_inc(s_stats2, 1)
                dve.wait_ge(s_stats2, b + 1)
                for g in range(GROUPS):
                    ins = dve.bn_aggr(mv[:, g, :], stat[:, g, :])
                ins.then_inc(s_agg2, 1)
                dve.wait_ge(s_agg2, b + 1)
                dve.tensor_scalar(ve[:, 0:GROUPS], mv[:, :, 1], EPS, None, ALU.add).then_inc(s_veps2, 1)
                dve.wait_ge(s_std3, b + 1)
                dve.reciprocal(rstd, sd[:, 0:GROUPS]).then_inc(s_rstd2, 1)
                dve.wait_ge(s_rstd2, b + 1)
                for g in range(GROUPS):
                    ins = dve.tensor_scalar(x3_tok[0:GT, g * D:(g + 1) * D], h2_tok[0:GT, g * D:(g + 1) * D],
                                            mv[:, g, 0:1], rstd[:, g:g + 1], ALU.subtract, ALU.mult)
                ins.then_inc(s_x3_done, 1)

            norm(0)
            for b in range(1, BLOCKS):
                norm(b)
                if b == BLOCKS - 2:
                    route_groups(0)

            def hidden_units(b, n, shared=False, first=False):
                for e in range(2):
                    dve.wait_ge(s_u_ready, 2 * n + e + 1)
                    if shared:
                        dve.wait_ge(s_silu_done, 2 * n + e + 1)
                    else:
                        dve.wait_ge(s_weighted_done, 2 * (n - BLOCKS) + e + 1)
                    if not first:
                        dve.wait_ge(s_hid_lo, 2 * n - 1 + e)
                    dve.tensor_tensor(hidden[e], bank[2 * e + 1][:, 0:BT], silu_g[e] if shared else weighted[e],
                                      ALU.mult).then_inc(s_hidden_done, 1)
                for e in range(0 if shared else 2):
                    dve.wait_ge(s_hid_hi, 2 * n + e + 1)
                    dve.tensor_tensor(mov_at(b % 2, 2 * e + 1), hidden[e], mov_at(b % 2, 2 * e).bitcast(F32),
                                      ALU.subtract).then_inc(s_hid_lo, 1)

            def split_third(p, b, w):
                cols = slice(b * 2 * D, (b + 1) * 2 * D)
                hi, lo = weight_parts(wbuf[1 - w], PAIR_COLS)
                dve.wait_ge(s_wsplit_hi, 3 * p + b + 1)
                dve.tensor_tensor(lo[:, cols], raw[:, (1 - w) * PAIR_COLS:(2 - w) * PAIR_COLS][:, cols],
                                  hi[:, cols].bitcast(F32), ALU.subtract).then_inc(s_wsplit_lo, 1)

            def add_down(b, n, again=True):
                dve.wait_ge(s_y_ready, n + 1)
                if again:
                    dve.wait_ge(s_added, n - BLOCKS + 1)
                for m in range(KD):
                    ins = dve.tensor_tensor(acc(b, m), bank[4 + 2 * (b % 2) + m][:, 0:BT], acc(b, m), ALU.add)
                ins.then_inc(s_added, 1)

            hidden_units(0, 0, shared=True, first=True)
            route_experts(0)
            hidden_units(1, 1, shared=True)
            route_groups(1)
            dve.wait_ge(s_acc_set, 2 * BLOCKS)
            add_down(0, 0, again=False)
            hidden_units(2, 2, shared=True)
            add_down(1, 1, again=False)
            route_experts(1)
            hidden_units(3, 3, shared=True)
            add_down(2, 2, again=False)

            def pair(p, w, last=False, after_shared=False):
                for b in range(BLOCKS):
                    n = BLOCKS * p + b
                    hidden_units(b, n)
                    if b < 3 and not last:
                        split_third(p, b, w)
                    add_down((b - 1) % BLOCKS, n - 1, again=not (after_shared and b == 0))

            pair(1, 1, after_shared=True)
            pair(2, 0)
            with dve.Fori(1, PAIRS // 2 - 1) as q:
                pair(2 * q + 1, 1)
                pair(2 * q + 2, 0)
            pair(PAIRS - 2, 1)
            pair(PAIRS - 1, 0, last=True)
            add_down(BLOCKS - 1, BLOCKS * PAIRS - 1)

        @block.scalar
        def _(act):
            act.wait_ge(s_warm, 1)
            act.activation(warm_out, warm_in, ACT.Copy)

            def split_patch(b, k):
                act.wait_ge(s_patch_in[b % 2][PART_OF[k]], 16 * (b // 2 + 1))
                if KP * b + k >= CH:
                    act.wait_ge(s_patch_used, KP * b + k - CH + 1)
                act.activation(patch_at(0, b, k), patch_raw[b % 2][:, k * BT:(k + 1) * BT],
                               ACT.Copy).then_inc(s_patch_hi, 1)

            for k in range(KP):
                act.wait_ge(s_tokw_in[PART_OF[k]], 16)
                act.activation(tok_hi[:, k * D:(k + 1) * D], tok_raw[:, k * D:(k + 1) * D],
                               ACT.Copy).then_inc(s_tokw_hi, 1)
                split_patch(0, k)
            act.wait_ge(s_params_in, 16)
            act.activation(decay[:, 0:CH], par[:, PLOGIT:PLOGIT + CH], ACT.Exp, scale=-1.0).then_inc(s_decay_e, 1)

            def copy_h(b):
                for m in range(KD):
                    act.wait_ge(s_patch_used, KP * (b + 1))
                    if b >= 1 and m == 0:
                        act.wait_ge(s_h_turned, b)
                    act.activation(h_ch[:, m * BT:(m + 1) * BT], bank[6 * (b % 2) + m][:, 0:BT], ACT.Identity,
                                   bias=par[:, PTOKB + m:PTOKB + m + 1]).then_inc(s_h_copied, 1)

            def root(b):
                act.wait_ge(s_veps, b + 1)
                act.activation(sd, ve, ACT.Sqrt).then_inc(s_std, 1)

            def residual(b):
                act.wait_ge(s_z_done, b + 1)
                act.wait_ge(s_res_scale, b + 1)
                for g in range(GROUPS):
                    ins = act.activation(res(b)[:, g * D:(g + 1) * D],
                                         bank[norm_bank(b) + g // 2][0:GT, (g % 2) * D:(g % 2 + 1) * D],
                                         ACT.Identity, bias=res_bias[:, g:g + 1], scale=res_scale[:, g:g + 1])
                ins.then_inc(s_res_done, 1)

            def affine(b):
                act.wait_ge(s_z_turned, b + 1)
                if b >= 1:
                    act.wait_ge(s_xn_split, b)
                for m in range(KD):
                    gamma, beta = par[:, PGAMMA + m:PGAMMA + m + 1], par[:, PBETA + m:PBETA + m + 1]
                    act.activation(xn_ch[:, m * BT:(m + 1) * BT], bank[4 + m][:, 0:BT], ACT.Identity,
                                   bias=beta, scale=gamma).then_inc(s_xn_read, 1)
                act.wait_ge(s_xn_read, 2 * (b + 1))
                act.activation(xparts[0][:, :, b * BT:(b + 1) * BT], xn_ch.rearrange("p (k t) -> p k t", k=KD),
                               ACT.Copy).then_inc(s_xn_done, 1)

            for k in range(KP):
                split_patch(1, k)
            copy_h(0)
            def values(c, it, w):
                act.wait_ge(s_v_proj, it + 1)
                act.wait_ge(s_bias_ready, c + 1)
                act.activation(v_ch, bank[2][:, 0:BT], ACT.Identity,
                               bias=bias_now[w][:, 0:1]).then_inc(s_v_copied, 1)
                act.wait_ge(s_v_turned, it + 1)
                act.activation(v_tok[0:GT, :, :].rearrange("p g c -> p (g c)"), bank[4][0:GT, :],
                               ACT.Copy).then_inc(s_v_ready, 1)

            def gates(it, w):
                act.wait_ge(s_g_proj, it + 1)
                act.wait_ge(s_og_done, it + 1)
                act.activation(gate, bank[3][:, 0:BT], ACT.Silu,
                               bias=bias_now[w][:, 1:2]).then_inc(s_gated, 1)

            for b in range(BLOCKS - 1):
                if b + 2 < BLOCKS:
                    for k in range(3):
                        split_patch(b + 2, k)
                if b >= 1:
                    affine(b - 1)
                root(b)
                if b + 2 < BLOCKS:
                    for k in range(3, KP):
                        split_patch(b + 2, k)
                copy_h(b + 1)
                residual(b)
            root(BLOCKS - 1)
            affine(BLOCKS - 2)
            values(0, 0, 0)
            residual(BLOCKS - 1)
            affine(BLOCKS - 1)
            gates(0, 0)

            def turn(q, first=0):
                for u in range(first, STEPS):
                    values(2 * q + u // BLOCKS, STEPS * q + u, u // BLOCKS)
                    gates(STEPS * q + u, u // BLOCKS)

            turn(0, first=1)
            with act.Fori(1, CH // 2) as q:
                turn(q)

            def split_heads(b, chunks):
                for k in chunks if b < BLOCKS else ():
                    act.wait_ge(s_og_used, CH * (b - 1) + k + 1)
                    act.wait_ge(s_og_done, STEPS * CH // 2 + 1)
                    act.activation(mov_at(0, k), og[:, k * TOKENS + b * BT:k * TOKENS + (b + 1) * BT],
                                   ACT.Copy).then_inc(s_og_hi, 1)

            def keep_comb(i):
                act.wait_ge(s_comb_turned, i + 1)
                if i >= 1:
                    act.wait_ge(s_stored, 16 * i)
                act.activation(comb_sb, bank[7][0:2 * EXPERTS, 0:BT], ACT.Copy).then_inc(s_comb_kept, 1)

            def copy_y(b):
                if b >= 1:
                    act.wait_ge(s_y_turned, b)
                for m in range(KD):
                    if m == 0:
                        act.wait_ge(s_y_first, b + 1)
                    else:
                        act.wait_ge(s_og_used, CH * (b + 1))
                    act.activation(y_ch[:, m * BT:(m + 1) * BT], bank[m][:, 0:BT], ACT.Identity,
                                   bias=par[:, PBO + m:PBO + m + 1]).then_inc(s_y_copied, 1)

            def root_2(b):
                act.wait_ge(s_veps2, b + 1)
                act.activation(sd[:, 0:GROUPS], ve[:, 0:GROUPS], ACT.Sqrt).then_inc(s_std3, 1)

            def copy_h2(b):
                act.wait_ge(s_h2_turned, b + 1)
                for m in range(KD):
                    act.activation(acc(b, m), bank[4 + m][:, 0:BT], ACT.Copy).then_inc(s_acc_set, 1)

            def copy_x3(b):
                act.wait_ge(s_x3_turned, b + 1)
                if b >= 1:
                    act.wait_ge(s_x3_lo, b)
                    act.wait_ge(s_logits, b)
                for m in range(KD):
                    act.activation(x3_ch[:, m * BT:(m + 1) * BT], bank[6 + m][:, 0:BT], ACT.Copy).then_inc(
                        s_x3_copied, 1)
                for m in range(KD):
                    act.activation(xn_at(0, m, b), bank[6 + m][:, 0:BT], ACT.Copy).then_inc(s_x3_hi, 1)

            def route_exp(b):
                act.wait_ge(s_logits, b + 1)
                if b >= 2:
                    act.wait_ge(s_r_step, 1)
                act.activation(r_exp.rearrange("p (g b e) -> p g b e", g=GROUPS, b=2)[:, :, b % 2, :],
                               bank[6][0:GT, 0:GROUPS * EXPERTS].rearrange("p (g e) -> p g e", g=GROUPS),
                               ACT.Exp, scale=-1.0).then_inc(s_exp_done, 1)

            split_heads(1, range(CH - 2))
            copy_y(0)
            split_heads(1, range(CH - 2, CH))
            for b in range(BLOCKS - 1):
                split_heads(b + 2, range(2))
                if b >= 1:
                    route_exp(b - 1)
                split_heads(b + 2, range(2, 3))
                root_2(b)
                copy_h2(b)
                split_heads(b + 2, range(3, CH - 2))
                copy_y(b + 1)
                split_heads(b + 2, range(CH - 2, CH))
                copy_x3(b)
            route_exp(BLOCKS - 2)
            root_2(BLOCKS - 1)

            def silu_gates(n, first=False):
                for e in range(2):
                    act.wait_ge(s_g_ready, 2 * n + e + 1)
                    if not first:
                        act.wait_ge(s_hidden_done, 2 * n - 1 + e)
                    act.activation(silu_g[e], bank[2 * e][:, 0:BT], ACT.Silu).then_inc(s_silu_done, 1)

            def high_parts(b, n):
                for e in range(2):
                    act.wait_ge(s_hidden_done, 2 * n + e + 1)
                    act.activation(mov_at(b % 2, 2 * e), hidden[e], ACT.Copy).then_inc(s_hid_hi, 1)

            def split_third(p, b, w, first=False):
                if b == 0:
                    if w == 0:
                        act.wait_ge(s_pair_in[1], 8 * p + 16)
                    else:
                        act.wait_ge(s_pair_in[0], 8 * p + 24)
                    if not first:
                        act.wait_ge(s_y_ready, BLOCKS * p)
                cols = slice(b * 2 * D, (b + 1) * 2 * D)
                hi, lo = weight_parts(wbuf[1 - w], PAIR_COLS)
                act.activation(hi[:, cols], raw[:, (1 - w) * PAIR_COLS:(2 - w) * PAIR_COLS][:, cols],
                               ACT.Copy).then_inc(s_wsplit_hi, 1)

            silu_gates(0, first=True)
            copy_h2(BLOCKS - 1)
            high_parts(0, 0)
            copy_x3(BLOCKS - 1)
            split_third(0, 0, 0, first=True)
            silu_gates(1)
            route_exp(BLOCKS - 1)
            high_parts(1, 1)
            split_third(0, 1, 0)
            keep_comb(0)
            silu_gates(2)
            high_parts(2, 2)
            split_third(0, 2, 0)
            silu_gates(3)
            high_parts(3, 3)
            keep_comb(1)

            def pair(p, w, last=False):
                for b in range(BLOCKS):
                    n = BLOCKS * p + b
                    silu_gates(n)
                    high_parts(b, n)
                    if b < 3 and not last:
                        split_third(p, b, w)

            pair(1, 1)
            pair(2, 0)
            with act.Fori(1, PAIRS // 2 - 1) as q:
                pair(2 * q + 1, 1)
                pair(2 * q + 2, 0)
            pair(PAIRS - 2, 1)
            pair(PAIRS - 1, 0, last=True)

        @block.gpsimd
        def _(pool):
            def split_chunk(w, cols):
                hi, lo = weight_parts(wbuf[w], cols)
                src = raw[:, w * cols:(w + 1) * cols]
                return hi, lo, src

            def split_high(hi, lo, src, done):
                pool.tensor_copy(hi, src).then_inc(done, 1)

            def split_rest(hi, lo, src, done, count):
                pool.wait_ge(done, count + 1)
                pool.tensor_tensor(lo, src, hi.bitcast(F32), ALU.subtract).then_inc(done, 1)

            def split_weights(hi, lo, src, done, count):
                split_high(hi, lo, src, done)
                split_rest(hi, lo, src, done, count)

            for k in range(KP):
                pool.wait_ge(s_tokw_hi, k + 1)
                pool.tensor_tensor(tok_lo[:, k * D:(k + 1) * D], tok_raw[:, k * D:(k + 1) * D],
                                   tok_hi[:, k * D:(k + 1) * D].bitcast(F32), ALU.subtract).then_inc(s_tokw_lo, 1)

            def split_patches(b, chunks=range(1, KP, 2)):
                for k in chunks:
                    pool.wait_ge(s_patch_hi, KP * b + k + 1)
                    pool.tensor_tensor(patch_at(1, b, k), patch_raw[b % 2][:, k * BT:(k + 1) * BT],
                                       patch_at(0, b, k).bitcast(F32), ALU.subtract).then_inc(s_patch_lo_odd, 1)

            def low_part(b, src, done):
                pool.tensor_tensor(xparts[1][:, :, b * BT:(b + 1) * BT], src.rearrange("p (k t) -> p k t", k=KD),
                                   xparts[0][:, :, b * BT:(b + 1) * BT].bitcast(F32),
                                   ALU.subtract).then_inc(done, 1)

            def attention_input(b):
                pool.wait_ge(s_xn_done, b + 1)
                low_part(b, xn_ch, s_xn_split)

            split_patches(1)
            pool.wait_ge(s_chunk_in[0], 16)
            split_high(*split_chunk(0, CHUNK_COLS), s_chunk_split)
            split_patches(2, (1, 3))
            split_rest(*split_chunk(0, CHUNK_COLS), s_chunk_split, 0)
            split_patches(2, (5,))
            split_patches(3)
            attention_input(0)
            pool.wait_ge(s_chunk_in[1], 16)
            split_weights(*split_chunk(1, CHUNK_COLS), s_chunk_split, 2)
            for b in range(1, BLOCKS):
                attention_input(b)

            def first_heads(k):
                pool.wait_ge(s_og_done, BLOCKS * k + 2)
                src = og[:, k * TOKENS:k * TOKENS + BT]
                pool.tensor_copy(mov_at(0, k), src).then_inc(s_og_first, 1)
                pool.wait_ge(s_og_first, 2 * k + 1)
                pool.tensor_tensor(mov_at(1, k), src, mov_at(0, k).bitcast(F32), ALU.subtract).then_inc(
                    s_og_first, 1)

            for c in range(2, CH):
                pool.wait_ge(s_chunk_in[c % 2], 16 * (c // 2 + 1))
                pool.wait_ge(s_g_proj, BLOCKS * (c - 1))
                split_weights(*split_chunk(c % 2, CHUNK_COLS), s_chunk_split, 2 * c)
                first_heads(c - 2)
            half = CH * D // 2
            for i in range(2):
                pool.wait_ge(s_wo_in, 16 * (i + 1))
                split_weights(wo_hi[:, i * half:(i + 1) * half], wo_lo[:, i * half:(i + 1) * half],
                              raw[:, 2 * CHUNK_COLS:3 * CHUNK_COLS], s_wo_split, 2 * i)
            first_heads(CH - 2)
            first_heads(CH - 1)
            pool.wait_ge(s_pair_in[0], 16)
            pool.wait_ge(s_g_proj, STEPS * CH // 2)
            split_weights(*split_chunk(0, PAIR_COLS), s_pair0_split, 0)

            def split_heads(b, chunks):
                for k in chunks:
                    pool.wait_ge(s_og_hi, CH * (b - 1) + k + 1)
                    pool.tensor_tensor(mov_at(1, k), og[:, k * TOKENS + b * BT:k * TOKENS + (b + 1) * BT],
                                       mov_at(0, k).bitcast(F32), ALU.subtract).then_inc(s_og_lo, 1)

            def experts_input(b):
                pool.wait_ge(s_x3_hi, 2 * (b + 1))
                pool.wait_ge(s_x3_copied, 2 * (b + 1))
                low_part(b, x3_ch, s_x3_lo)

            split_heads(1, range(CH))
            for b in range(BLOCKS - 1):
                if b + 2 < BLOCKS:
                    split_heads(b + 2, range(CH))
                experts_input(b)

            next_hi, next_lo = weight_parts(wbuf[1], PAIR_COLS)
            for b in range(BLOCKS):
                for e in range(2):
                    pool.wait_ge(s_hid_hi, 2 * b + e + 1)
                    pool.tensor_tensor(mov_at(b % 2, 2 * e + 1), hidden[e], mov_at(b % 2, 2 * e).bitcast(F32),
                                       ALU.subtract).then_inc(s_hid_lo, 1)
                if b == 0:
                    experts_input(BLOCKS - 1)
                if b < 3:
                    cols = slice(b * 2 * D, (b + 1) * 2 * D)
                    pool.wait_ge(s_wsplit_hi, b + 1)
                    pool.tensor_tensor(next_lo[:, cols], raw[:, PAIR_COLS:2 * PAIR_COLS][:, cols],
                                       next_hi[:, cols].bitcast(F32), ALU.subtract).then_inc(s_wsplit_lo, 1)

            with pool.Fori(1, PAIRS) as p:
                for b in range(BLOCKS):
                    n = BLOCKS * p + b
                    pool.wait_ge(s_comb_in[b % 2], 64 * (p - 1) + 32 * (b // 2 + 1))
                    for e in range(2):
                        pool.wait_ge(s_silu_done, 2 * n + e + 1)
                        pool.wait_ge(s_hidden_done, 2 * n - 1 + e)
                        pool.tensor_tensor(weighted[e], silu_g[e], comb[b % 2][:, e * BT:(e + 1) * BT],
                                           ALU.mult).then_inc(s_weighted_done, 1)


def _token_order():
    import numpy as np
    order = []
    for g in range(IMAGES // 2):
        for s0, ln in zip(STARTS, LENS):
            for i in range(2):
                order += [(2 * g + i) * SEQ + s0 + t for t in range(ln)]
    return np.array(order)


def kernel(**inputs):
    import numpy as np
    import concourse.bacc as _bacc
    from concourse import mybir as _mybir
    from concourse.bass_utils import run_bass_kernel_spmd as _run

    a = {k: np.asarray(v) for k, v in inputs.items()}
    f = np.ascontiguousarray
    order = _token_order()

    def chunked(w):
        return w.reshape(-1, P, w.shape[-1]).transpose(1, 0, 2)

    x = a["x"].reshape(IMAGES, 3, 7, 16, 7, 16).transpose(0, 2, 4, 3, 5, 1).reshape(TOKENS, PATCH_D)
    patches = x[order].T.reshape(KP, P, BLOCKS, BT).transpose(1, 2, 0, 3).reshape(P, BLOCKS, KP * BT)
    w_tok = chunked(a["L0_tok_W"].T).reshape(P, KP * D)
    mats = np.stack([a[f"L0_attn_{n}"] for n in ("WK", "WQ", "WV", "Wg")])
    w_qkvg = mats.reshape(MATS, CH, P, KD, P).transpose(1, 4, 0, 3, 2).reshape(CH, P, CHUNK_COLS)
    w_o = chunked(a["L0_attn_WO"].T).reshape(P, 2, CH * D // 2).transpose(1, 0, 2)
    I = 128
    gates = np.concatenate([a["L0_ffn_sh_gate"].reshape(SHARED, I, D), a["L0_ffn_w_gate"]])
    ups = np.concatenate([a["L0_ffn_sh_up"].reshape(SHARED, I, D), a["L0_ffn_w_up"]])
    downs = np.concatenate([a["L0_ffn_sh_down"].reshape(D, SHARED, I).transpose(1, 0, 2), a["L0_ffn_w_down"]])
    E = EXPERTS + SHARED
    gu = np.stack([gates, ups], 1).reshape(E, 2, I, KD, P).transpose(0, 4, 3, 1, 2).reshape(E, P, KD * D)
    w_ffn = np.concatenate([gu, downs.transpose(0, 2, 1)], 2)
    w_ffn = w_ffn.reshape(PAIRS, 2, P, 3 * D).transpose(0, 2, 1, 3).reshape(PAIRS, P, PAIR_COLS)

    def column(v):
        return v.reshape(-1, P).T

    params = np.concatenate([column(a[f"L0_attn_{n}"]) for n in ("bK", "bQ", "bV", "bg")]
                            + [column(a["L0_attn_alpha_logit"].reshape(-1)), column(a["L0_tok_b"]),
                               column(a["L0_attn_bO"]), column(a["L0_attn_ln_gamma"]),
                               column(a["L0_attn_ln_beta"])], 1)
    image = np.concatenate([[i] * ln for ln in LENS for i in range(2)])
    time = np.concatenate([np.arange(s0, s0 + ln) for s0, ln in zip(STARTS, LENS) for i in range(2)])
    causal = np.where((image[:, None] == image[None]) & (time[:, None] <= time[None]), -1, 0).astype(np.int32)
    arrays = {
        "patches": patches, "w_tok": w_tok, "w_qkvg": w_qkvg, "w_o": w_o, "w_ffn": w_ffn, "params": params,
        "w_route": chunked(a["L0_ffn_gate_w"].T).reshape(P, KD * EXPERTS),
        "b_route": a["L0_ffn_gate_bias"].reshape(1, EXPERTS),
        "identity": np.eye(P, dtype=np.float32), "causal_order": causal,
    }
    nc = _bacc.Bacc("TRN2", target_bir_lowering=False, num_devices=1)
    args, arrays = [], {k: f(v) for k, v in arrays.items()}
    for name, v in arrays.items():
        args.append(nc.dram_tensor("in_" + name, v.shape, _mybir.dt.from_np(v.dtype), kind="ExternalInput").ap())
    args.append(nc.dram_tensor("comb_dram", (BLOCKS * EXPERTS, BT), F32, kind="Internal").ap())
    args.append(nc.dram_tensor("out_ch", (P, BLOCKS, KD * BT), F32, kind="ExternalOutput").ap())
    build(nc, *args)
    r = _run(nc, [{"in_" + k: v for k, v in arrays.items()}], core_ids=[0])
    got = r.results[0]["out_ch"].reshape(P, BLOCKS, KD, BT).transpose(1, 3, 2, 0).reshape(TOKENS, D)
    y = np.empty_like(got)
    y[order] = got
    return y.reshape(IMAGES, SEQ, D)
```
